# Optimizing a Trainium2 kernel written in Bass

```python
import numpy as np
import jax
import jax.numpy as jnp

def _softmax(x, axis=-1):
    return jax.nn.softmax(x, axis=axis)

def _gelu(x):
    return jax.nn.gelu(x, approximate=True)

def _silu(x):
    return jax.nn.silu(x)

def _sigmoid(x):
    return jax.nn.sigmoid(x)

def _layernorm(x, axis=-1, eps=1e-05):
    m = jnp.mean(x, axis=axis, keepdims=True)
    v = jnp.var(x, axis=axis, keepdims=True)
    return (x - m) / jnp.sqrt(v + eps)

def _scatter_add(tgt, idx, src, axis=0):
    return tgt.at[idx].add(src)

def _segment_sum(src, seg, n):
    return jax.ops.segment_sum(src, seg, n)
kernel_name = 'mk_gnn_resnorm_d4_gnn_r8_16e9f8'

def setup_inputs(seed: int=0):
    np.random.seed(seed)
    _w = jnp.asarray

    def _rec_inputs():
        import jax
        import jax.numpy as jnp
        _gk = jax.random.key(seed)
        x = -0.0003713 + 1 * jax.random.normal(jax.random.fold_in(_gk, 1), (6250, 256), jnp.float32)
        src = jax.random.randint(jax.random.fold_in(_gk, 2), (100000,), 0, 6250, jnp.int32)
        dst = jnp.minimum((6250 * jax.random.uniform(jax.random.fold_in(_gk, 3), (100000,)) ** 2.0).astype(jnp.int32), 49999)
        _o = jnp.argsort(dst, stable=True)
        src = src[_o]
        dst = dst[_o]
        edge_attr3_1x1 = jax.random.uniform(jax.random.fold_in(_gk, 13), (100000, 1, 1), jnp.float32, 0.0, 0.999998)
        edge_weight = jax.random.uniform(jax.random.fold_in(_gk, 15), (100000,), jnp.float32, 0.0, 1)
        return (x, src, dst, edge_attr3_1x1, edge_weight)
    x, src, dst, edge_attr3_1x1, edge_weight = _rec_inputs()

    def _L0_gnn_setup():
        import jax, jax.numpy as jnp
        import numpy as np
        N, E = (6250, 100000)
        NFEAT, NHID, NCLASS, HEADS = (256, 256, 64, 4)
        NEG_SLOPE = 0.2

        def gat_conv(x, src, dst, W, a_src, a_dst, b):
            H, C = a_src.shape
            h = (x @ W).reshape(-1, H, C)
            alpha_s = jnp.einsum('nhc,hc->nh', h, a_src)
            alpha_d = jnp.einsum('nhc,hc->nh', h, a_dst)
            e = jax.nn.leaky_relu(alpha_s[src] + alpha_d[dst], NEG_SLOPE)
            m = jax.ops.segment_max(e, dst, num_segments=N)
            ex = jnp.exp(e - m[dst])
            s = jax.ops.segment_sum(ex, dst, num_segments=N)
            alpha = ex / (s[dst] + 1e-16)
            out = jax.ops.segment_sum(h[src] * alpha[:, :, None], dst, num_segments=N)
            return out.reshape(-1, H * C) + b
        key = jax.random.key(seed)
        ks = jax.random.split(key, 12)
        glorot = lambda k, shape: jax.random.normal(k, shape, jnp.float32) * jnp.sqrt(2.0 / (shape[0] + shape[-1]))
        x = jax.random.normal(ks[0], (N, NFEAT), jnp.float32)
        edge_index = jax.random.randint(ks[1], (2, E), 0, N, jnp.int64)
        W1 = glorot(ks[2], (NFEAT, HEADS * NCLASS))
        att_src1 = glorot(ks[3], (HEADS, NCLASS))
        att_dst1 = glorot(ks[4], (HEADS, NCLASS))
        b1 = jnp.zeros((HEADS * NCLASS,), jnp.float32)
        W2 = glorot(ks[5], (NHID, HEADS * NCLASS))
        att_src2 = glorot(ks[6], (HEADS, NCLASS))
        att_dst2 = glorot(ks[7], (HEADS, NCLASS))
        b2 = jnp.zeros((HEADS * NCLASS,), jnp.float32)
        return {'x': x, 'edge_index': edge_index, 'W1': W1, 'att_src1': att_src1, 'att_dst1': att_dst1, 'b1': b1, 'W2': W2, 'att_src2': att_src2, 'att_dst2': att_dst2, 'b2': b2}
    _L0_gnn_all = _L0_gnn_setup()
    _L0_gnn_in = {k: v for k, v in _L0_gnn_all.items() if k in ('W1', 'att_src1', 'att_dst1', 'b1', 'W2', 'att_src2', 'att_dst2', 'b2')}
    del _L0_gnn_all

    def _L1_gnn_setup():
        import jax, jax.numpy as jnp
        import numpy as np
        N = 6250
        E = 100000
        D = 256
        H = 256

        def _graph_conv(x, src, dst, W_rel, b, W_root):
            agg = jax.ops.segment_sum(x[src], dst, num_segments=N)
            return agg @ W_rel + b + x @ W_root
        key = jax.random.key(seed)
        ks = jax.random.split(key, 11)

        def lin(k, fan_in, shape):
            s = 1.0 / np.sqrt(fan_in)
            return jax.random.uniform(k, shape, jnp.float32, -s, s)
        return {'x': jax.random.normal(ks[0], (N, D), jnp.float32), 'edge_index': jax.random.randint(ks[1], (2, E), 0, N, dtype=jnp.int64), 'W1_rel': lin(ks[2], D, (D, H)), 'b1': lin(ks[3], D, (H,)), 'W1_root': lin(ks[4], D, (D, H)), 'W2_rel': lin(ks[5], H, (H, H)), 'b2': lin(ks[6], H, (H,)), 'W2_root': lin(ks[7], H, (H, H)), 'W3_rel': lin(ks[8], H, (H, H)), 'b3': lin(ks[9], H, (H,)), 'W3_root': lin(ks[10], H, (H, H))}
    _L1_gnn_all = _L1_gnn_setup()
    _L1_gnn_in = {k: v for k, v in _L1_gnn_all.items() if k in ('W1_rel', 'b1', 'W1_root', 'W2_rel', 'b2', 'W2_root', 'W3_rel', 'b3', 'W3_root')}
    del _L1_gnn_all

    def _L2_gnn_setup():
        import jax, jax.numpy as jnp
        import numpy as np
        BN_EPS = 1e-05

        def _batchnorm(h, gamma, beta):
            mean = jnp.mean(h, axis=0, keepdims=True)
            var = jnp.var(h, axis=0, keepdims=True)
            return (h - mean) * jax.lax.rsqrt(var + BN_EPS) * gamma + beta
        key = jax.random.key(seed)
        ks = jax.random.split(key, 10)
        N, E, D = (12500, 400000, 256)
        x = jax.random.normal(ks[0], (N, D), dtype=jnp.float32)
        edge_src = jax.random.randint(ks[1], (E,), 0, N, dtype=jnp.int32)
        edge_dst = jax.random.randint(ks[2], (E,), 0, N, dtype=jnp.int32)
        edge_vals = jnp.ones((E,), dtype=jnp.float32)
        n_norm = jax.random.uniform(ks[3], (N, 1), dtype=jnp.float32)
        s = 1.0 / np.sqrt(D)
        w1 = jax.random.uniform(ks[4], (D, D), jnp.float32, -s, s)
        gamma1 = jnp.ones((D,), jnp.float32)
        beta1 = jnp.zeros((D,), jnp.float32)
        w2 = jax.random.uniform(ks[5], (D, D), jnp.float32, -s, s)
        eps_weight = jnp.zeros((1,), jnp.float32)
        gamma_h = jnp.ones((D,), jnp.float32)
        beta_h = jnp.zeros((D,), jnp.float32)
        return {'x': x, 'edge_src': edge_src, 'edge_dst': edge_dst, 'edge_vals': edge_vals, 'n_norm': n_norm, 'w1': w1, 'gamma1': gamma1, 'beta1': beta1, 'w2': w2, 'eps_weight': eps_weight, 'gamma_h': gamma_h, 'beta_h': beta_h}
    _L2_gnn_all = _L2_gnn_setup()
    _L2_gnn_in = {k: v for k, v in _L2_gnn_all.items() if k in ('w1', 'gamma1', 'beta1', 'w2', 'eps_weight', 'gamma_h', 'beta_h')}
    del _L2_gnn_all

    def _L3_gnn_setup():
        import jax, jax.numpy as jnp
        import numpy as np
        N, F_IN, H, OUT, E = (4000, 256, 4, 64, 64000)
        NEG_SLOPE = 0.2
        key = jax.random.key(seed)
        ks = jax.random.split(key, 7)
        return {'feat': jax.random.normal(ks[0], (N, F_IN), dtype=jnp.float32), 'dist': jax.random.uniform(ks[1], (E, 1, 1), dtype=jnp.float32), 'W': jax.random.normal(ks[2], (F_IN, H * OUT), dtype=jnp.float32) * (1.0 / np.sqrt(F_IN)), 'w_att_src': jax.random.normal(ks[3], (1, H, OUT), dtype=jnp.float32) * 0.1, 'w_att_dst': jax.random.normal(ks[4], (1, H, OUT), dtype=jnp.float32) * 0.1, 'src': jax.random.randint(ks[5], (E,), 0, N, dtype=jnp.int32), 'dst': jax.random.randint(ks[6], (E,), 0, N, dtype=jnp.int32)}
    _L3_gnn_all = _L3_gnn_setup()
    _L3_gnn_in = {k: v for k, v in _L3_gnn_all.items() if k in ('W', 'w_att_src', 'w_att_dst')}
    del _L3_gnn_all
    return {'x': x, 'src': src, 'dst': dst, 'edge_attr3_1x1': edge_attr3_1x1, 'edge_weight': edge_weight, 'L0_gnn_W1': _L0_gnn_in['W1'], 'L0_gnn_att_src1': _L0_gnn_in['att_src1'], 'L0_gnn_att_dst1': _L0_gnn_in['att_dst1'], 'L0_gnn_b1': _L0_gnn_in['b1'], 'L0_gnn_W2': _L0_gnn_in['W2'], 'L0_gnn_att_src2': _L0_gnn_in['att_src2'], 'L0_gnn_att_dst2': _L0_gnn_in['att_dst2'], 'L0_gnn_b2': _L0_gnn_in['b2'], 'L1_gnn_W1_rel': _L1_gnn_in['W1_rel'], 'L1_gnn_b1': _L1_gnn_in['b1'], 'L1_gnn_W1_root': _L1_gnn_in['W1_root'], 'L1_gnn_W2_rel': _L1_gnn_in['W2_rel'], 'L1_gnn_b2': _L1_gnn_in['b2'], 'L1_gnn_W2_root': _L1_gnn_in['W2_root'], 'L1_gnn_W3_rel': _L1_gnn_in['W3_rel'], 'L1_gnn_b3': _L1_gnn_in['b3'], 'L1_gnn_W3_root': _L1_gnn_in['W3_root'], 'L2_gnn_w1': _L2_gnn_in['w1'], 'L2_gnn_gamma1': _L2_gnn_in['gamma1'], 'L2_gnn_beta1': _L2_gnn_in['beta1'], 'L2_gnn_w2': _L2_gnn_in['w2'], 'L2_gnn_eps_weight': _L2_gnn_in['eps_weight'], 'L2_gnn_gamma_h': _L2_gnn_in['gamma_h'], 'L2_gnn_beta_h': _L2_gnn_in['beta_h'], 'L3_gnn_W': _L3_gnn_in['W'], 'L3_gnn_w_att_src': _L3_gnn_in['w_att_src'], 'L3_gnn_w_att_dst': _L3_gnn_in['w_att_dst']}

def reference(x, src, dst, edge_attr3_1x1, edge_weight, L0_gnn_W1, L0_gnn_att_src1, L0_gnn_att_dst1, L0_gnn_b1, L0_gnn_W2, L0_gnn_att_src2, L0_gnn_att_dst2, L0_gnn_b2, L1_gnn_W1_rel, L1_gnn_b1, L1_gnn_W1_root, L1_gnn_W2_rel, L1_gnn_b2, L1_gnn_W2_root, L1_gnn_W3_rel, L1_gnn_b3, L1_gnn_W3_root, L2_gnn_w1, L2_gnn_gamma1, L2_gnn_beta1, L2_gnn_w2, L2_gnn_eps_weight, L2_gnn_gamma_h, L2_gnn_beta_h, L3_gnn_W, L3_gnn_w_att_src, L3_gnn_w_att_dst):
    import jax
    import jax.numpy as jnp

    def _L0_gnn_ref(x, edge_index, W1, att_src1, att_dst1, b1, W2, att_src2, att_dst2, b2):
        import jax, jax.numpy as jnp
        import numpy as np
        N, E = (6250, 100000)
        NFEAT, NHID, NCLASS, HEADS = (256, 256, 64, 4)
        NEG_SLOPE = 0.2

        def gat_conv(x, src, dst, W, a_src, a_dst, b):
            H, C = a_src.shape
            h = (x @ W).reshape(-1, H, C)
            alpha_s = jnp.einsum('nhc,hc->nh', h, a_src)
            alpha_d = jnp.einsum('nhc,hc->nh', h, a_dst)
            e = jax.nn.leaky_relu(alpha_s[src] + alpha_d[dst], NEG_SLOPE)
            m = jax.ops.segment_max(e, dst, num_segments=N)
            ex = jnp.exp(e - m[dst])
            s = jax.ops.segment_sum(ex, dst, num_segments=N)
            alpha = ex / (s[dst] + 1e-16)
            out = jax.ops.segment_sum(h[src] * alpha[:, :, None], dst, num_segments=N)
            return out.reshape(-1, H * C) + b
        loops = jnp.arange(N, dtype=edge_index.dtype)
        src = jnp.concatenate([edge_index[0], loops])
        dst = jnp.concatenate([edge_index[1], loops])
        x0 = jax.nn.relu(gat_conv(x, src, dst, W1, att_src1, att_dst1, b1))
        x2 = gat_conv(x0, src, dst, W2, att_src2, att_dst2, b2)
        return x2

    def _L1_gnn_ref(x, edge_index, W1_rel, b1, W1_root, W2_rel, b2, W2_root, W3_rel, b3, W3_root):
        import jax, jax.numpy as jnp
        import numpy as np
        N = 6250
        E = 100000
        D = 256
        H = 256

        def _graph_conv(x, src, dst, W_rel, b, W_root):
            agg = jax.ops.segment_sum(x[src], dst, num_segments=N)
            return agg @ W_rel + b + x @ W_root
        src, dst = (edge_index[0], edge_index[1])
        h = jax.nn.elu(_graph_conv(x, src, dst, W1_rel, b1, W1_root))
        h = jax.nn.elu(_graph_conv(h, src, dst, W2_rel, b2, W2_root))
        h = jax.nn.elu(_graph_conv(h, src, dst, W3_rel, b3, W3_root))
        return h

    def _L2_gnn_ref(x, edge_src, edge_dst, edge_vals, n_norm, w1, gamma1, beta1, w2, eps_weight, gamma_h, beta_h):
        import jax, jax.numpy as jnp
        import numpy as np
        BN_EPS = 1e-05

        def _batchnorm(h, gamma, beta):
            mean = jnp.mean(h, axis=0, keepdims=True)
            var = jnp.var(h, axis=0, keepdims=True)
            return (h - mean) * jax.lax.rsqrt(var + BN_EPS) * gamma + beta
        N = x.shape[0]
        msgs = edge_vals[:, None] * x[edge_src]
        agg = jax.ops.segment_sum(msgs, edge_dst, num_segments=N)
        y = agg + eps_weight * x
        h = jax.nn.relu(_batchnorm(y @ w1.T, gamma1, beta1))
        y = h @ w2.T
        y = y * n_norm
        y = _batchnorm(y, gamma_h, beta_h)
        y = jax.nn.relu(y)
        y = y + x
        return y

    def _L3_gnn_ref(feat, dist, W, w_att_src, w_att_dst, src, dst):
        import jax, jax.numpy as jnp
        import numpy as np
        N, F_IN, H, OUT, E = (4000, 256, 4, 64, 64000)
        NEG_SLOPE = 0.2
        n = feat.shape[0]
        ft = (feat @ W).reshape(n, H, OUT)
        e_src = jnp.sum(ft * w_att_src, axis=-1, keepdims=True)
        e_dst = jnp.sum(ft * w_att_dst, axis=-1, keepdims=True)
        e = e_src[src] + e_dst[dst]
        e = jnp.where(e >= 0, e, NEG_SLOPE * e)
        emax = jax.ops.segment_max(e, dst, num_segments=n)
        ex = jnp.exp(e - emax[dst])
        denom = jax.ops.segment_sum(ex, dst, num_segments=n)
        a = ex / denom[dst] * dist
        m = ft[src] * a
        out = jax.ops.segment_sum(m, dst, num_segments=n)
        return out.reshape(n, H * OUT)
    edge_index = jnp.stack([src, dst])
    deg = jnp.maximum(jax.ops.segment_sum(jnp.ones(dst.shape, jnp.float32), dst, num_segments=6250), 1.0)
    deg_isqrt = deg ** (-0.5)
    x = _layernorm(x + _L0_gnn_ref(x, edge_index, L0_gnn_W1, L0_gnn_att_src1, L0_gnn_att_dst1, L0_gnn_b1, L0_gnn_W2, L0_gnn_att_src2, L0_gnn_att_dst2, L0_gnn_b2), axis=-1)
    x = _layernorm(x + _L1_gnn_ref(x, edge_index, L1_gnn_W1_rel, L1_gnn_b1, L1_gnn_W1_root, L1_gnn_W2_rel, L1_gnn_b2, L1_gnn_W2_root, L1_gnn_W3_rel, L1_gnn_b3, L1_gnn_W3_root), axis=-1)
    x = _layernorm(x + _L2_gnn_ref(x, src, dst, edge_weight, deg_isqrt[:, None], L2_gnn_w1, L2_gnn_gamma1, L2_gnn_beta1, L2_gnn_w2, L2_gnn_eps_weight, L2_gnn_gamma_h, L2_gnn_beta_h), axis=-1)
    x = _layernorm(x + _L3_gnn_ref(x, edge_attr3_1x1, L3_gnn_W, L3_gnn_w_att_src, L3_gnn_w_att_dst, src, dst), axis=-1)
    return x

_drawn_inputs = setup_inputs


def setup_inputs(seed=0):
    import zlib

    import numpy as np

    out = dict(_drawn_inputs(seed))
    spreads = {'L0_gnn_b1': (0.0, 0.1),
     'L0_gnn_b2': (0.0, 0.1),
     'L2_gnn_gamma1': (1.0, 0.2),
     'L2_gnn_beta1': (0.0, 0.1),
     'L2_gnn_gamma_h': (1.0, 0.2),
     'L2_gnn_beta_h': (0.0, 0.1)}
    factors = {'L0_gnn_att_dst1': 9.987,
     'L0_gnn_att_dst2': 8.84,
     'L1_gnn_b2': 4.344,
     'L1_gnn_b3': 24.823,
     'L3_gnn_w_att_dst': 25.446,
     'L3_gnn_w_att_src': 3.848}
    for name, (base, spread) in spreads.items():
        noise = np.random.default_rng([zlib.crc32(name.encode()), seed]).standard_normal(out[name].shape)
        drawn = base * np.exp(spread * noise) if base else spread * noise
        out[name] = jnp.asarray(drawn.astype(out[name].dtype))
    for name, factor in factors.items():
        out[name] = (out[name] * factor).astype(out[name].dtype)
    return out
```

```python
from contextlib import ExitStack

import concourse.bass as bass
from concourse import mybir

P = 128
N = 6250
E = 100000
D = 256
H = 4
C = D // H
NT = -(-N // P)
NTP = NT + NT % 2
NP = NTP * P
SP_, SC = 125, 800
U = 8
SLOTS = 4
NCH = -(-(E // P + 1 + NT) // (U * SLOTS)) * U * SLOTS
NCH = max(NCH, 832)
EP = NCH * P
RUN = NCH // 32
RL = RUN * P
LOW, HIGH = 128, NT
RW = 4
MSG_ONE = D
MSG_P = D + 1
MSG_M = D + 1 + H
MSGW = D + 1 + 2 * H
NEG = -1.0e30
NO_NODE = -1.0
SLOPE = 0.2
EPS = 1e-5

ALU = mybir.AluOpType
ACT = mybir.ActivationFunctionType
AX = mybir.AxisListType
F32 = mybir.dt.float32
BF16 = mybir.dt.bfloat16
U16 = mybir.dt.uint16
I32 = mybir.dt.int32
assert E == SP_ * SC and NCH % (U * SLOTS) == 0 and NCH * P >= E + NT * (P - 1)


class Steps:

    def __init__(self, eng, sem):
        self.eng, self.sem, self.n = eng, sem, 0

    def __call__(self, ins):
        ins.then_inc(self.sem, 1)
        self.n += 1
        self.eng.wait_ge(self.sem, self.n)


def repeat_inner(ap, n):
    return ap.unsqueeze(2).to_broadcast([ap.shape[0], ap.shape[1], n])


def by_chunk(heads):
    return heads[:].rearrange("p h c -> p c h")


def by_pairs(eng, body):
    for s in range(2):
        body(s, s, True)
    with eng.Fori(1, NTP // 2) as i:
        for s in range(2):
            body(i * 2 + s, s, False)


def repeat_outer(ap, n):
    return ap.unsqueeze(1).to_broadcast([ap.shape[0], n, ap.shape[1]])


class Mem:

    def __init__(self, nc, ctx, phase):
        self.nc, self.ctx, self.phase, self.sems = nc, ctx, phase, []

    def sb(self, name, shape, dt=F32):
        return self.ctx.enter_context(self.nc.sbuf_tensor(f"{self.phase}_{name}", shape, dt))

    def ps(self, name, shape, dt=F32):
        return self.ctx.enter_context(self.nc.psum_tensor(f"{self.phase}_{name}", shape, dt))

    def sem(self, name):
        if not self.sems:
            self.ctx.callback(self.clear)
        self.sems.append(self.nc.alloc_semaphore(f"{self.phase}_{name}"))
        return self.sems[-1]

    def clear(self):
        self.nc.clear_and_free_semaphores(self.sems)
        self.nc.all_engine_barrier()


def setup_phase(nc, k, src, dst, ew, dist, x, table_x, rec_hi):
    with ExitStack() as ctx:
        m = Mem(nc, ctx, "setup")
        ints = m.sb("edge_ints", [P, 2, SC], I32)
        fls = m.sb("edge_floats", [P, 2, SC], F32)
        pads = m.sb("pad_records", [P, NCH, RW])
        zero = m.sb("zero_rows", [P, D])
        edges_in = m.sem("edges_in")
        const = m.sem("const_made")
        pad_made = m.sem("pad_made")
        out_done = m.sem("setup_stored")
        dv = m.sem("setup_dve")
        block = ctx.enter_context(nc.Block())

        @block.sync
        def _(sp):
            for n, a in enumerate((src, dst)):
                sp.dma_start(ints[0:SP_, n, :], a.rearrange("(p s) -> p s", p=SP_)).then_inc(edges_in, 16)
            sp.dma_start(fls[0:SP_, 0, :], ew.rearrange("(p s) -> p s", p=SP_)).then_inc(edges_in, 16)
            sp.dma_start(fls[0:SP_, 1, :], dist.rearrange("(p s) a b -> p (s a b)", p=SP_)).then_inc(edges_in, 16)
            sp.dma_start(table_x[0:N, :], x).then_inc(out_done, 16)
            sp.wait_ge(pad_made, 3)
            sp.dma_start(rec_hi.rearrange("(p q) w -> p (q w)", p=P),
                         pads[:].rearrange("p a b -> p (a b)")).then_inc(out_done, 16)
            sp.dma_start(table_x[N:N + 128, :], zero[:]).then_inc(out_done, 16)
            sp.dma_start(table_x[N + 128:NP, :], zero[0:NP - N - 128, :]).then_inc(out_done, 16)
            sp.wait_ge(out_done, 64)

        @block.gpsimd
        def _(pool):
            st = Steps(pool, const)
            pool.iota(k.chunk_no[:], [[P * P, NCH // P + 1]], base=0, channel_multiplier=P,
                      allow_small_or_imprecise_dtypes=True)
            pool.iota(k.iota[:], [[1, P]], base=0, channel_multiplier=0,
                      allow_small_or_imprecise_dtypes=True)
            st(pool.memset(k.ident[:], 0.0))
            st(pool.affine_select(out=k.ident[:], in_=k.ident[:], compare_op=ALU.not_equal, fill=1.0,
                                  base=0, pattern=[[-1, P]], channel_multiplier=1))
            st(pool.memset(k.before[:], 1.0))
            st(pool.affine_select(out=k.before[:], in_=k.before[:], compare_op=ALU.is_ge, fill=0.0,
                                  base=-1, pattern=[[1, P]], channel_multiplier=-1))
            pool.memset(k.ones[:], 1.0)

        @block.vector
        def _(dve):
            st = Steps(dve, dv)
            st(dve.memset(pads[:], 0.0))
            dve.memset(pads[:, :, 1], NO_NODE).then_inc(pad_made, 2)
            dve.memset(zero[:], 0.0).then_inc(pad_made, 1)
            dve.wait_ge(edges_in, 64)
            dve.tensor_copy(k.rec[0:SP_, :, 0], ints[0:SP_, 0, :])
            dve.tensor_copy(k.rec[0:SP_, :, 1], ints[0:SP_, 1, :])
            dve.tensor_copy(k.rec[0:SP_, :, 2], fls[0:SP_, 0, :])
            dve.tensor_copy(k.rec[0:SP_, :, 3], fls[0:SP_, 1, :])


def sort_phase(nc, k, name, buckets, high, rec_from, rec_to, tile_dram):
    CB = 8
    with ExitStack() as ctx:
        m = Mem(nc, ctx, name)
        key = m.sb("key", [P, SC])
        key_i = m.sb("key_i", [P, SC], I32)
        rank = m.sb("rank", [P, SC])
        pos = m.sb("pos", [P, SC], I32)
        mask = m.sb("mask", [P, SC], BF16)
        count = m.sb("count", [P, SC])
        one_row = m.sb("one_row", [P, SC])
        totals = m.sb("totals", [P, P])
        start = m.sb("start", [P, P])
        size = m.sb("size", [P, P])
        size_i = m.sb("size_i", [P, P], I32)
        base = m.sb("base", [P, P])
        pos_ring = m.sb("pos_ring", [P, 2, CB], I32)
        rec_ring = m.sb("rec_ring", [P, 2, CB, RW])
        chunk_at = m.sb("chunk_at", [P, NCH // P + 1, NT]) if high else None
        before_ps = m.ps("before_ps", [P, 512])
        total_ps = m.ps("total_ps", [P, 512])
        loaded = m.sem(f"loaded")
        dv = m.sem(f"dve")
        in_loop = m.sem(f"bucket_steps")
        in_loop2 = m.sem(f"base_steps")
        totals_made = m.sem(f"totals")
        base_ps_made = m.sem(f"base_ps")
        pos_made = m.sem(f"pos")
        ring_full = m.sem(f"ring_full")
        scattered = [m.sem(f"scattered{s}") for s in range(2)]
        turn = m.sem("scatter_turn")
        block = ctx.enter_context(nc.Block())
        S = slice(0, SP_)

        @block.sync
        def _(sp):
            if rec_from is not None:
                sp.dma_start(k.rec[S].rearrange("p a b -> p (a b)"),
                             rec_from.rearrange("(p s) w -> p (s w)", p=SP_)).then_inc(loaded, 16)

        @block.vector
        def _(dve):
            st = Steps(dve, dv)
            if rec_from is not None:
                dve.wait_ge(loaded, 16)
            st(dve.tensor_copy(key_i[S], k.rec[S, :, 1]))
            if high:
                st(dve.tensor_scalar(pos[S], key_i[S], 7, None, op0=ALU.arith_shift_right))
            else:
                st(dve.tensor_scalar(pos[S], key_i[S], LOW - 1, None, op0=ALU.bitwise_and))
            st(dve.tensor_copy(key[S], pos[S]))
            st(dve.memset(rank[:], 0.0))
            st(dve.memset(one_row[:], 1.0))
            st(dve.memset(totals[:], 0.0))
            with dve.Fori(0, buckets) as b:
                dve.tensor_scalar(mask[S], key[S], k.iota[S, bass.ds(b, 1)], None,
                                  op0=ALU.is_equal).then_inc(in_loop, 1)
                dve.wait_ge(in_loop, b * 4 + 1)
                dve.tensor_tensor_scan(count[S], one_row[S], mask[S], 0.0,
                                       op0=ALU.mult, op1=ALU.add).then_inc(in_loop, 1)
                dve.wait_ge(in_loop, b * 4 + 2)
                dve.tensor_copy(totals[S, bass.ds(b, 1)], count[S, SC - 1:SC]).then_inc(in_loop, 1)
                dve.copy_predicated(rank[S], mask[S].bitcast(U16), count[S]).then_inc(in_loop, 1)
                dve.wait_ge(in_loop, b * 4 + 4)
            dve.sem_inc(totals_made, 1)
            dve.wait_ge(base_ps_made, 1)
            st(dve.tensor_copy(size[:, 0:buckets], total_ps[:, 0:buckets]))
            if high:
                st(dve.tensor_scalar(size[:, 0:buckets], size[:, 0:buckets], float(P - 1), None, op0=ALU.add))
                st(dve.tensor_copy(size_i[:, 0:buckets], size[:, 0:buckets]))
                st(dve.tensor_scalar(size_i[:, 0:buckets], size_i[:, 0:buckets], -P, None, op0=ALU.bitwise_and))
                st(dve.tensor_copy(size[:, 0:buckets], size_i[:, 0:buckets]))
            st(dve.tensor_tensor_scan(start[:, 0:buckets], one_row[:, 0:buckets], size[:, 0:buckets], 0.0,
                                      op0=ALU.mult, op1=ALU.add))
            if high:
                nq = NCH // P + 1
                cols = k.chunk_no[:, 0:nq]
                st(dve.tensor_tensor(chunk_at[:, 0:nq, :], repeat_inner(cols, NT),
                                     repeat_outer(start[:, 0:NT], nq), ALU.is_ge))
                st(dve.tensor_reduce(k.tile_of[:, 0:nq], chunk_at[:, 0:nq, :], AX.X, ALU.add))
                st(dve.tensor_scalar(k.tile_of[:, 0:nq], k.tile_of[:, 0:nq], float(NT - 1), float(MSGW),
                                     op0=ALU.min, op1=ALU.mult))
                st(dve.tensor_copy(k.tile_off_i[:, 0:nq], k.tile_of[:, 0:nq]))
            st(dve.tensor_tensor(start[:, 0:buckets], start[:, 0:buckets], size[:, 0:buckets], ALU.subtract))
            st(dve.tensor_tensor(base[:, 0:buckets], before_ps[:, 0:buckets], start[:, 0:buckets], ALU.add))
            with dve.Fori(0, buckets) as b:
                dve.tensor_scalar(count[S], key[S], k.iota[S, bass.ds(b, 1)], base[S, bass.ds(b, 1)],
                                  op0=ALU.is_equal, op1=ALU.mult).then_inc(in_loop2, 1)
                dve.wait_ge(in_loop2, b * 2 + 1)
                dve.tensor_tensor(rank[S], rank[S], count[S], ALU.add).then_inc(in_loop2, 1)
                dve.wait_ge(in_loop2, b * 2 + 2)
            st(dve.tensor_scalar(rank[S], rank[S], -1.0, None, op0=ALU.add))
            dve.tensor_copy(pos[S], rank[S]).then_inc(pos_made, 1)

        @block.tensor
        def _(pe):
            pe.wait_ge(totals_made, 1)
            pe.matmul(before_ps[:, 0:buckets], k.before[S, :], totals[S, 0:buckets], start=True, stop=True)
            pe.matmul(total_ps[:, 0:buckets], k.ones[S, :], totals[S, 0:buckets], start=True,
                      stop=True).then_inc(base_ps_made, 1)

        @block.scalar
        def _(act):
            def fill(s, at):
                act.copy(pos_ring[S, s, :], pos[S, bass.ds(at, CB)])
                act.copy(rec_ring[S, s].rearrange("p a b -> p (a b)"),
                         k.rec[S].rearrange("p a b -> p (a b)")[:, bass.ds(at * RW, CB * RW)]).then_inc(ring_full, 1)

            act.wait_ge(pos_made, 1)
            for s in range(2):
                fill(s, s * CB)
            with act.Fori(1, SC // CB // 2) as i:
                for s in range(2):
                    act.wait_ge(scattered[s], i * (16 * CB))
                    fill(s, (i * 2 + s) * CB)

        @block.gpsimd
        def _(pool):
            with pool.Fori(0, SC // CB // 2) as i:
                for s in range(2):
                    pool.wait_ge(ring_full, i * 2 + s + 1)
                    pool.sem_inc(turn, 1)
                    for c in range(CB):
                        pool.indirect_dma_start(
                            out=rec_to, out_offset=bass.IndirectOffsetOnAxis(ap=pos_ring[S, s, c:c + 1], axis=0),
                            in_=rec_ring[S, s, c, :], in_offset=None).then_inc(scattered[s], 16)
            for s in range(2):
                pool.wait_ge(scattered[s], SC // 2 * 16)
    if high:
        with ExitStack() as ctx:
            m = Mem(nc, ctx, "chunks")
            stored = m.sem("tile_offsets_stored")
            block = ctx.enter_context(nc.Block())
            nf = NCH // P

            @block.sync
            def _(sp):
                sp.dma_start(tile_dram[0:nf * P].rearrange("(q p) -> p q", p=P), k.tile_off_i[:, 0:nf],
                             allow_slow_non_contiguous=True).then_inc(stored, 16)
                sp.dma_start(tile_dram[nf * P:NCH].rearrange("(p q) -> p q", q=1),
                             k.tile_off_i[0:NCH - nf * P, nf:nf + 1]).then_inc(stored, 16)
                sp.wait_ge(stored, 32)
                sp.dma_start(k.tile_off[0:1, :], tile_dram.rearrange("(a c) -> a c", a=1)).then_inc(stored, 16)
                sp.wait_ge(stored, 48)


def edges_phase(nc, k, rec_hi, flags_dram):
    with ExitStack() as ctx:
        m = Mem(nc, ctx, "edges")
        rec = m.sb("rec", [P, NCH, RW])
        dst_i = m.sb("dst_i", [P, NCH], I32)
        low_i = m.sb("low_i", [P, NCH], I32)
        none = m.sb("none", [P, NCH])
        dst4 = m.sb("dst4", [P, H, NCH])
        dst_scan = m.sb("dst_scan", [P, RL])
        breaks = m.sb("breaks", [P, RL + 1])
        ends = m.sb("ends", [P, 4])
        row = m.sb("row", [1, 3, P])
        tp = [m.ps(f"tp{n}", [P, P]) for n in range(2)]
        rows_ps = m.ps("rows_ps", [P, 512])
        loaded, dv, stored = m.sem("loaded"), m.sem("dve"), m.sem("stored")
        dst4_made, turned, taken = m.sem("dst4_made"), m.sem("turned"), m.sem("taken")
        ends_made, rows_made = m.sem("ends_made"), m.sem("rows_made")
        first_made, first_turned = m.sem("first_made"), m.sem("first_turned")
        breaks_made = m.sem("breaks_made")
        block = ctx.enter_context(nc.Block())

        @block.sync
        def _(sp):
            half = NCH // 2
            by_edge = rec_hi.rearrange("(c e) w -> e c w", e=P)
            sp.dma_start(rec[:, 0:half, :], by_edge[:, 0:half, :]).then_inc(loaded, 16)
            sp.dma_start(rec[:, half:, :], by_edge[:, half:, :]).then_inc(loaded, 16)
            sp.wait_ge(breaks_made, 1)
            sp.dma_start(flags_dram, breaks[:]).then_inc(stored, 16)
            sp.wait_ge(stored, 16)

        @block.vector
        def _(dve):
            st = Steps(dve, dv)
            dve.wait_ge(loaded, 32)
            dve.tensor_copy(dst4[:], repeat_outer(rec[:, :, 1], H)).then_inc(dst4_made, 1)
            st(dve.tensor_copy(k.src[:], rec[:, :, 0]))
            st(dve.tensor_copy(k.weight[:], rec[:, :, 2]))
            st(dve.tensor_copy(k.dist[:], rec[:, :, 3]))
            st(dve.tensor_scalar(none[:], rec[:, :, 1], 0.0, float(8 * P), op0=ALU.is_lt, op1=ALU.mult))
            st(dve.tensor_scalar(k.local[:], rec[:, :, 1], 0.0, None, op0=ALU.max))
            st(dve.tensor_copy(k.dst[:], k.local[:]))
            st(dve.tensor_scalar(low_i[:], k.dst[:], P - 1, None, op0=ALU.bitwise_and))
            st(dve.tensor_copy(k.local[:], low_i[:]))
            st(dve.tensor_tensor(k.local[:], k.local[:], none[:], ALU.add))
            for c in range(RUN):
                dve.wait_ge(turned, c + 1)
                dve.tensor_copy(dst_scan[:, c * P:(c + 1) * P], tp[c % 2][:]).then_inc(taken, 1)
            dve.wait_ge(taken, RUN)
            st(dve.memset(breaks[:], 0.0))
            st(dve.tensor_tensor(breaks[:, 1:RL], dst_scan[:, 1:RL], dst_scan[:, 0:RL - 1], ALU.not_equal))
            st(dve.tensor_reduce(ends[:, 2:3], breaks[:], AX.X, ALU.max))
            st(dve.tensor_scalar(breaks[:], breaks[:], NEG, None, op0=ALU.mult))
            dve.sem_inc(breaks_made, 1)
            st(dve.tensor_copy(ends[:, 0:1], dst_scan[:, 0:1]))
            st(dve.tensor_copy(ends[:, 1:2], dst_scan[:, RL - 1:RL]))
            dve.sem_inc(ends_made, 1)
            dve.wait_ge(rows_made, 1)
            st(dve.tensor_copy(row[0:1].rearrange("a b c -> a (b c)"), rows_ps[0:1, 0:3 * P]))
            st(dve.memset(k.breaks_in[:], 1.0))
            for h in range(H):
                st(dve.tensor_tensor(k.breaks_in[0:1, 32 * h + 1:32 * h + 32], row[0:1, 0, 32 * h + 1:32 * h + 32],
                                     row[0:1, 1, 32 * h:32 * h + 31], ALU.not_equal))
            st(dve.tensor_tensor(k.through_fwd[:], k.breaks_in[0:1, 0:P], row[0:1, 2, :], ALU.max))
            st(dve.tensor_tensor(k.through_back[:], k.breaks_in[0:1, 1:P + 1], row[0:1, 2, :], ALU.max))
            st(dve.tensor_copy(row[0:1, 0, :], k.breaks_in[0:1, 0:P]))
            dve.sem_inc(first_made, 1)
            st(dve.tensor_scalar(k.through_fwd[:], k.through_fwd[:], NEG, None, op0=ALU.mult))
            st(dve.tensor_scalar(k.through_back[:], k.through_back[:], NEG, None, op0=ALU.mult))
            st(dve.tensor_scalar(k.breaks_in[:], k.breaks_in[:], NEG, None, op0=ALU.mult))
            dve.wait_ge(first_turned, 1)
            st(dve.tensor_copy(k.first_in_run[:], rows_ps[:, 384:385]))

        @block.tensor
        def _(pe):
            pe.wait_ge(dst4_made, 1)
            by_run = dst4[:].rearrange("p h (r c) -> p c (h r)", c=RUN)
            for c in range(RUN):
                if c >= 2:
                    pe.wait_ge(taken, c - 1)
                pe.transpose(tp[c % 2][:], by_run[:, c], k.ident[:]).then_inc(turned, 1)
            pe.wait_ge(ends_made, 1)
            for n in range(3):
                ins = pe.transpose(rows_ps[0:1, n * P:(n + 1) * P], ends[:, n:n + 1], k.ident[:])
            ins.then_inc(rows_made, 1)
            pe.wait_ge(first_made, 1)
            pe.transpose(rows_ps[:, 384:385], row[0:1, 0, :], k.ident[0:1, 0:1]).then_inc(first_turned, 1)


def aggregate_phase(nc, k, name, table, acc, scale, head_scale, softmax, width):
    with ExitStack() as ctx:
        m = Mem(nc, ctx, name)
        ring = m.sb("messages", [P, SLOTS, U, MSGW])
        index = m.sb("index", [P, SLOTS, U], I32)
        member = m.sb("member", [P, 2, U, P])
        sums = [m.ps(f"sums{j}", [P, 512]) for j in range(U)]
        gathered = [m.sem(f"gathered{s}") for s in range(SLOTS)]
        turn = m.sem("gather_turn")
        index_ready = m.sem("index_ready")
        set_up = m.sem("set_up")
        prepared = m.sem("prepared")
        member_made = m.sem("member_made")
        chunk_summed = m.sem("chunk_summed")
        chunk_added = m.sem("chunk_added")
        block = ctx.enter_context(nc.Block())
        units = NCH // U

        @block.gpsimd
        def _(pool):
            with pool.Fori(0, units // SLOTS) as i:
                for s in range(SLOTS):
                    pool.wait_ge(index_ready, i * SLOTS + s + 1)
                    pool.sem_inc(turn, 1)
                    for j in range(U):
                        pool.indirect_dma_start(
                            out=ring[:, s, j, 0:D], out_offset=None, in_=table,
                            in_offset=bass.IndirectOffsetOnAxis(ap=index[:, s, j:j + 1], axis=0),
                        ).then_inc(gathered[s], 16)

        @block.scalar
        def _(act):
            def fill(s, u):
                if softmax:
                    act.copy(ring[:, s, :, MSG_P:MSG_P + H],
                             by_chunk(k.numer)[:, bass.ds(u * U, U), :])
                if width > MSG_M:
                    act.copy(ring[:, s, :, MSG_M:MSG_M + H],
                             by_chunk(k.first_max)[:, bass.ds(u * U, U), :])
                act.copy(index[:, s, :], k.src[:, bass.ds(u * U, U)]).then_inc(index_ready, 1)

            act.wait_ge(set_up, 1)
            for s in range(SLOTS):
                fill(s, s)
            with act.Fori(1, units // SLOTS) as i:
                for s in range(SLOTS):
                    act.wait_ge(chunk_summed, i * (SLOTS * U) + (s + 1 - SLOTS) * U)
                    fill(s, i * SLOTS + s)

        @block.vector
        def _(dve):
            def prepare(i, s):
                u = i * SLOTS + s
                dve.wait_ge(index_ready, u + 1)
                dve.tensor_tensor(member[:, s % 2], repeat_outer(k.iota[:], U),
                                  repeat_inner(k.local[:, bass.ds(u * U, U)], P), ALU.is_equal).then_inc(member_made, 1)
                dve.wait_ge(gathered[s], i * (16 * U) + 16 * U)
                msgs = ring[:, s, :, 0:D]
                if scale is None:
                    dve.sem_inc(prepared, 1)
                elif head_scale:
                    for j in range(U):
                        mj = ring[:, s, j, 0:D].rearrange("p (h f) -> p h f", h=H)
                        ins = dve.tensor_tensor(mj, mj, repeat_inner(by_chunk(scale)[:, u * U + j, :], C), ALU.mult)
                    ins.then_inc(prepared, 1)
                else:
                    dve.tensor_tensor(msgs, msgs, repeat_inner(scale[:, bass.ds(u * U, U)], D),
                                      ALU.mult).then_inc(prepared, 1)

            def add(i, s):
                u = i * SLOTS + s
                offs = nc.values_load_multi_w_load_instructions(
                    k.tile_off[0:1, bass.ds(u * U, U)], engines=(mybir.EngineType.DVE,),
                    min_val=0, max_val=(NT - 1) * MSGW, skip_runtime_bounds_check_because="made so")[1]
                for j in range(U):
                    dve.wait_ge(chunk_summed, u * U + (j + 1))
                    dve.wait_ge(chunk_added, u * U + (j + 1))
                    at = acc[:, bass.ds(offs[j], width)]
                    dve.tensor_tensor(at, at, sums[j][:, 0:width], ALU.add).then_inc(chunk_added, 1)

            dve.memset(acc, 0.0).then_inc(chunk_added, 1)
            dve.memset(ring[:, :, :, MSG_ONE], 1.0).then_inc(set_up, 1)
            prepare(0, 0)
            with dve.Fori(0, units // SLOTS - 1) as i:
                for s in range(SLOTS):
                    prepare(i + (s + 1) // SLOTS, (s + 1) % SLOTS)
                    add(i, s)
            last = units // SLOTS - 1
            for s in range(SLOTS):
                if s + 1 < SLOTS:
                    prepare(last, s + 1)
                add(last, s)

        @block.tensor
        def _(pe):
            def sum_unit(i, s, first):
                u = i * SLOTS + s
                pe.wait_ge(member_made, u + 1)
                pe.wait_ge(prepared, u + 1)
                for j in range(U):
                    if not first:
                        pe.wait_ge(chunk_added, u * U + (j + 2 - U))
                    pe.matmul(sums[j][:, 0:width], member[:, s % 2, j, :], ring[:, s, j, 0:width],
                              start=True, stop=True).then_inc(chunk_summed, 1)

            for s in range(SLOTS):
                sum_unit(0, s, s == 0)
            with pe.Fori(1, units // SLOTS) as i:
                for s in range(SLOTS):
                    sum_unit(i, s, False)


def project_phase(nc, k, name, table_in, w, att_src, att_dst, table_h, table_a):
    WE = D + 2 * H
    with ExitStack() as ctx:
        m = Mem(nc, ctx, name)
        w_sb = m.sb("w", [P, 2, WE])
        att = m.sb("att", [P, 2, D])
        prod = m.sb("prod", [P, 2, D])
        xin = m.sb("xin", [P, 2, D])
        xt = m.sb("xt", [P, 2, D])
        h_out = m.sb("h_out", [P, 2, WE])
        xt_ps = [m.ps(f"xt_ps{s}", [P, 512]) for s in range(2)]
        h_ps = [m.ps(f"h_ps{s}", [P, 512]) for s in range(2)]
        w_in, dv = m.sem("w_in"), m.sem("dve")
        w_ready = m.sem("w_ready")
        loaded = [m.sem(f"loaded{s}") for s in range(2)]
        stored = [m.sem(f"stored{s}") for s in range(2)]
        turned, xt_made, summed, h_made = m.sem("turned"), m.sem("xt_made"), m.sem("summed"), m.sem("h_made")
        block = ctx.enter_context(nc.Block())

        @block.sync
        def _(sp):
            for c in range(2):
                sp.dma_start(w_sb[:, c, 0:D], w[c * P:(c + 1) * P, :]).then_inc(w_in, 16)
            for n, a in enumerate((att_src, att_dst)):
                flat = a.rearrange("h c -> (h c)") if len(a.shape) == 2 else a.rearrange("a h c -> (a h c)")
                sp.dma_start(att[:, n, :], flat.partition_broadcast(P)).then_inc(w_in, 16)

            def load(t, s, first):
                if not first:
                    sp.wait_ge(turned, t - 1)
                sp.dma_start(xin[:, s, :], table_in[bass.ds(t * P, P), :]).then_inc(loaded[s], 16)

            by_pairs(sp, load)

        @block.tensor
        def _(pe):
            pe.wait_ge(w_ready, 1)

            def tile(t, s, first):
                pe.wait_ge(loaded[s], (t // 2) * 16 + 16 if first else (t - s) * 8 + 16)
                for c in range(2):
                    ins = pe.transpose(xt_ps[s][:, c * P:(c + 1) * P], xin[:, s, c * P:(c + 1) * P], k.ident[:])
                ins.then_inc(turned, 1)
                pe.wait_ge(xt_made, t + 1)
                if not first:
                    pe.wait_ge(h_made, t - 1)
                for c in range(2):
                    ins = pe.matmul(h_ps[s][:, 0:WE], xt[:, s, c * P:(c + 1) * P], w_sb[:, c, :],
                                    start=(c == 0), stop=(c == 1))
                ins.then_inc(summed, 1)

            by_pairs(pe, tile)

        @block.scalar
        def _(act):
            def tile(t, s, first):
                act.wait_ge(turned, t + 1)
                if not first:
                    act.wait_ge(summed, t - 1)
                act.copy(xt[:, s, :], xt_ps[s][:, 0:D]).then_inc(xt_made, 1)

            by_pairs(act, tile)

        @block.vector
        def _(dve):
            st = Steps(dve, dv)
            dve.wait_ge(w_in, 64)
            for n in range(2):
                for c in range(2):
                    st(dve.tensor_tensor(prod[:, c, :], w_sb[:, c, 0:D], att[:, n, :], ALU.mult))
                    st(dve.tensor_reduce(w_sb[:, c, D + n * H:D + (n + 1) * H],
                                         prod[:, c, :].rearrange("p (h f) -> p h f", h=H), AX.X, ALU.add))
            dve.sem_inc(w_ready, 1)

            def tile(t, s, first):
                dve.wait_ge(summed, t + 1)
                if not first:
                    dve.wait_ge(stored[s], (t - s) * 16)
                dve.tensor_copy(h_out[:, s, :], h_ps[s][:, 0:WE]).then_inc(h_made, 1)

            by_pairs(dve, tile)

        @block.gpsimd
        def _(pool):
            def tile(t, s, first):
                pool.wait_ge(h_made, t + 1)
                pool.dma_start(table_h[bass.ds(t * P, P), :], h_out[:, s, 0:D]).then_inc(stored[s], 16)
                pool.dma_start(table_a[bass.ds(t * P, P), :], h_out[:, s, D:WE]).then_inc(stored[s], 16)

            by_pairs(pool, tile)
            for s in range(2):
                pool.wait_ge(stored[s], NTP * 16)


def lookup_phase(nc, k, name, table_a, z, z_self):
    UL = 16
    with ExitStack() as ctx:
        m = Mem(nc, ctx, name)
        index = m.sb("index", [P, 2, 2, UL], I32)
        found = m.sb("found", [P, 2, 2, UL, 2 * H])
        gathered = [m.sem(f"gathered{s}") for s in range(2)]
        turn = m.sem("gather_turn")
        index_ready, taken, dv = m.sem("index_ready"), m.sem("taken"), m.sem("dve")
        block = ctx.enter_context(nc.Block())
        pairs = NCH // UL // 2

        @block.scalar
        def _(act):
            def fill(s, u):
                act.copy(index[:, s, 0, :], k.src[:, bass.ds(u * UL, UL)])
                act.copy(index[:, s, 1, :], k.dst[:, bass.ds(u * UL, UL)]).then_inc(index_ready, 1)

            for s in range(2):
                fill(s, s)
            with act.Fori(1, pairs) as i:
                for s in range(2):
                    act.wait_ge(taken, i * 2 + (s - 1))
                    fill(s, i * 2 + s)

        @block.gpsimd
        def _(pool):
            with pool.Fori(0, pairs) as i:
                for s in range(2):
                    pool.wait_ge(index_ready, i * 2 + s + 1)
                    pool.sem_inc(turn, 1)
                    for n in range(2):
                        for j in range(UL):
                            pool.indirect_dma_start(
                                out=found[:, s, n, j, :], out_offset=None, in_=table_a,
                                in_offset=bass.IndirectOffsetOnAxis(ap=index[:, s, n, j:j + 1], axis=0),
                            ).then_inc(gathered[s], 16)

        @block.vector
        def _(dve):
            with dve.Fori(0, pairs) as i:
                for s in range(2):
                    u = i * 2 + s
                    dve.wait_ge(gathered[s], i * (32 * UL) + 32 * UL)
                    if z_self is not None:
                        dve.tensor_tensor(by_chunk(z_self)[:, bass.ds(u * UL, UL), :], found[:, s, 1, :, 0:H],
                                          found[:, s, 1, :, H:], ALU.add)
                    dve.tensor_tensor(by_chunk(z)[:, bass.ds(u * UL, UL), :], found[:, s, 0, :, 0:H],
                                      found[:, s, 1, :, H:], ALU.add).then_inc(taken, 1)


def softmax_phase(nc, k, name, flags_dram, z, z_self, scaled):
    with ExitStack() as ctx:
        m = Mem(nc, ctx, name)
        breaks = m.sb("breaks", [P, RL + 1])
        z_scan = m.sb("z_scan", [P, RL])
        self_scan = m.sb("self_scan", [P, RL]) if z_self is not None else None
        fwd = m.sb("fwd", [P, RL])
        back = m.sb("back", [P, RL])
        row = m.sb("row", [1, 2, P + 2])
        carry = m.sb("carry", [P, 2])
        tp = [m.ps(f"tp{n}", [P, P]) for n in range(4)]
        row_ps = m.ps("row_ps", [P, 512])
        flags_in, dv = m.sem("flags_in"), m.sem("dve")
        leaky_made, turned, taken_v, taken_a = m.sem("leaky_made"), m.sem("turned"), m.sem("taken_dve"), m.sem("taken_act")
        last_made, row_made, row_carried, carry_made = m.sem("last_made"), m.sem("row_made"), m.sem("row_carried"), m.sem("carry_made")
        max_made, numer_made = m.sem("max_made"), m.sem("numer_made")
        block = ctx.enter_context(nc.Block())
        both = z_self is not None
        by_run = lambda t: t[:].rearrange("p h (r c) -> p c (h r)", c=RUN)

        @block.sync
        def _(sp):
            sp.dma_start(breaks[:], flags_dram).then_inc(flags_in, 16)

        @block.tensor
        def _(pe):
            pe.wait_ge(leaky_made, 1)
            for c in range(RUN):
                if c >= 2:
                    pe.wait_ge(taken_a, c - 1)
                pe.transpose(tp[c % 2][:], by_run(z)[:, c], k.ident[:]).then_inc(turned, 1)
                if both:
                    if c >= 2:
                        pe.wait_ge(taken_v, c - 1)
                    pe.transpose(tp[2 + c % 2][:], by_run(z_self)[:, c], k.ident[:]).then_inc(turned, 1)
            for n, (source, at) in enumerate(((fwd, RL - 1), (back, 0))):
                pe.wait_ge(last_made, n + 1)
                pe.transpose(row_ps[0:1, 0:P], source[:, at:at + 1], k.ident[:]).then_inc(row_made, 1)
                pe.wait_ge(row_carried, n + 1)
                pe.transpose(row_ps[:, 256 + n:257 + n], row[0:1, 1, 0:P], k.ident[0:1, 0:1]).then_inc(carry_made, 1)
            pe.wait_ge(max_made, 1)
            pe.wait_ge(taken_a, RUN)
            if both:
                pe.wait_ge(taken_v, RUN)
            for c in range(RUN):
                if c >= 2:
                    pe.wait_ge(taken_a, RUN + c - 1)
                pe.transpose(tp[c % 2][:], back[:, c * P:(c + 1) * P], k.ident[:]).then_inc(turned, 1)
                if both:
                    if c >= 2:
                        pe.wait_ge(taken_v, RUN + c - 1)
                    pe.transpose(tp[2 + c % 2][:], fwd[:, c * P:(c + 1) * P], k.ident[:]).then_inc(turned, 1)

        per = 2 if both else 1

        @block.scalar
        def _(act):
            for c in range(RUN):
                act.wait_ge(turned, per * c + 1)
                act.copy(z_scan[:, c * P:(c + 1) * P], tp[c % 2][:]).then_inc(taken_a, 1)
            for c in range(RUN):
                act.wait_ge(turned, per * (RUN + c) + 1)
                act.copy(by_run(k.numer)[:, c], tp[c % 2][:]).then_inc(taken_a, 1)
            act.wait_ge(numer_made, 1)
            act.activation(k.numer[:], k.numer[:], ACT.Exp).then_inc(numer_made, 1)

        @block.vector
        def _(dve):
            st = Steps(dve, dv)
            for t in (z, z_self) if both else (z,):
                st(dve.scalar_tensor_tensor(t[:], t[:], SLOPE, t[:], op0=ALU.mult, op1=ALU.max))
            dve.sem_inc(leaky_made, 1)
            if both:
                for c in range(RUN):
                    dve.wait_ge(turned, 2 * c + 2)
                    dve.tensor_copy(self_scan[:, c * P:(c + 1) * P], tp[2 + c % 2][:]).then_inc(taken_v, 1)
                dve.wait_ge(taken_v, RUN)
            dve.wait_ge(flags_in, 16)
            dve.wait_ge(taken_a, RUN)
            st(dve.memset(row[:], 0.0))

            def scan_fwd(initial):
                return dve.tensor_tensor_scan(fwd[:], breaks[:, 0:RL], z_scan[:], initial, op0=ALU.add, op1=ALU.max)

            def scan_back(initial):
                return dve.tensor_tensor_scan(back[:, ::-1], breaks[:, 1:RL + 1][:, ::-1], fwd[:, ::-1], initial,
                                              op0=ALU.add, op1=ALU.max)

            st(scan_fwd(NEG))
            dve.sem_inc(last_made, 1)
            dve.wait_ge(row_made, 1)
            st(dve.tensor_tensor_scan(row[0:1, 0, 1:P + 1], k.through_fwd[:], row_ps[0:1, 0:P], NEG,
                                      op0=ALU.add, op1=ALU.max))
            st(dve.tensor_tensor(row[0:1, 1, 0:P], row[0:1, 0, 0:P], k.breaks_in[0:1, 0:P], ALU.add))
            dve.sem_inc(row_carried, 1)
            dve.wait_ge(carry_made, 1)
            st(dve.tensor_copy(carry[:, 0:1], row_ps[:, 256:257]))
            st(scan_fwd(carry[:, 0:1]))
            st(scan_back(NEG))
            dve.sem_inc(last_made, 1)
            dve.wait_ge(row_made, 2)
            st(dve.memset(row[0:1, 0, P:P + 2], 0.0))
            st(dve.tensor_tensor_scan(row[0:1, 0, 0:P][:, ::-1], k.through_back[0:1, ::-1], row_ps[0:1, 0:P][:, ::-1],
                                      NEG, op0=ALU.add, op1=ALU.max))
            st(dve.tensor_tensor(row[0:1, 1, 0:P], row[0:1, 0, 1:P + 1], k.breaks_in[0:1, 1:P + 1], ALU.add))
            dve.sem_inc(row_carried, 1)
            dve.wait_ge(carry_made, 2)
            st(dve.tensor_copy(carry[:, 1:2], row_ps[:, 257:258]))
            st(scan_back(carry[:, 1:2]))
            if both:
                st(dve.tensor_tensor(back[:], back[:], self_scan[:], ALU.max))
                st(dve.tensor_scalar(fwd[:], breaks[:, 0:RL], 0.0, None, op0=ALU.not_equal))
                st(dve.tensor_copy(fwd[:, 0:1], k.first_in_run[:]))
                st(dve.tensor_tensor(fwd[:], fwd[:], back[:], ALU.mult))
            dve.sem_inc(max_made, 1)
            if both:
                for c in range(RUN):
                    dve.wait_ge(turned, 2 * (RUN + c) + 2)
                    dve.tensor_copy(by_run(k.first_max)[:, c], tp[2 + c % 2][:]).then_inc(taken_v, 1)
            dve.wait_ge(taken_a, 2 * RUN)
            dve.tensor_tensor(k.numer[:], z[:], k.numer[:], ALU.subtract).then_inc(numer_made, 1)
            if scaled is not None:
                dve.wait_ge(numer_made, 2)
                dve.tensor_tensor(scaled[:], k.numer[:], repeat_outer(k.dist[:], H), ALU.mult)


def attention_end_phase(nc, k, name, acc, table_h, table_a, bias, residual, table_out):
    own = table_a is not None
    with ExitStack() as ctx:
        m = Mem(nc, ctx, name)
        a_sb = m.sb("a", [P, NTP, 2 * H])
        zn = m.sb("zn", [P, NTP, H])
        mx = m.sb("mx", [P, NTP, H])
        inv = m.sb("inv", [P, NTP, H])
        no_edge = m.sb("no_edge", [P, NTP])
        bias_sb = m.sb("bias", [P, D])
        h_in = m.sb("h_in", [P, 2, D])
        x_in = m.sb("x_in", [P, 2, D])
        y = m.sb("y", [P, 2, D])
        dv, small_in, numer_ready, numer_made = m.sem("dve"), m.sem("small_in"), m.sem("numer_ready"), m.sem("numer_made")
        loaded = [m.sem(f"loaded{s}") for s in range(2)]
        stored = [m.sem(f"stored{s}") for s in range(2)]
        steps, used, made = m.sem("tile_steps"), m.sem("used"), m.sem("made")
        block = ctx.enter_context(nc.Block())
        acc3 = acc.rearrange("p (t w) -> p t w", w=MSGW)
        ready = {}
        loads = int(own) + int(residual is not None)

        @block.sync
        def _(sp):
            if own:
                sp.dma_start(a_sb[:], table_a.rearrange("(t p) a -> p t a", p=P)).then_inc(small_in, 16)
                sp.dma_start(bias_sb[:], bias.partition_broadcast(P)).then_inc(small_in, 16)

            def load(t, s, first):
                if not first:
                    sp.wait_ge(used, t - 1)
                if own:
                    sp.dma_start(h_in[:, s, :], table_h[bass.ds(t * P, P), :]).then_inc(loaded[s], 16)
                if residual is not None:
                    sp.dma_start(x_in[:, s, :], residual[bass.ds(t * P, P), :]).then_inc(loaded[s], 16)

            by_pairs(sp, load)

        @block.scalar
        def _(act):
            if own:
                act.wait_ge(numer_ready, 1)
                act.activation(zn[:], zn[:], ACT.Exp).then_inc(numer_made, 1)

        @block.vector
        def _(dve):
            st = Steps(dve, dv)
            sums_p = acc3[:, :, MSG_P:MSG_P + H]
            if own:
                dve.wait_ge(small_in, 32)
                st(dve.tensor_tensor(zn[:], a_sb[:, :, 0:H], a_sb[:, :, H:], ALU.add))
                st(dve.scalar_tensor_tensor(zn[:], zn[:], SLOPE, zn[:], op0=ALU.mult, op1=ALU.max))
                st(dve.tensor_scalar(no_edge[:], acc3[:, :, MSG_ONE], 0.5, None, op0=ALU.is_lt))
                st(dve.tensor_tensor(mx[:], zn[:], repeat_inner(no_edge[:], H), ALU.mult))
                st(dve.tensor_tensor(mx[:], mx[:], acc3[:, :, MSG_M:MSG_M + H], ALU.add))
                st(dve.tensor_tensor(zn[:], zn[:], mx[:], ALU.subtract))
                dve.sem_inc(numer_ready, 1)
                dve.wait_ge(numer_made, 1)
                st(dve.tensor_tensor(inv[:], zn[:], sums_p, ALU.add))
                st(dve.tensor_scalar(inv[:], inv[:], 1e-16, None, op0=ALU.add))
            else:
                st(dve.tensor_scalar(inv[:], sums_p, 1e-30, None, op0=ALU.max))
            st(dve.reciprocal(inv[:], inv[:]))
            if own:
                st(dve.tensor_tensor(zn[:], zn[:], inv[:], ALU.mult))
            flat_inv, flat_own = (t[:].rearrange("p t h -> p (t h)") for t in (inv, zn))
            by_head = lambda ap: ap.rearrange("p (h f) -> p h f", h=H)
            seq = []
            total = 1 + 3 * own + 1

            def tile(t, s, first):
                n = [0]

                def step(ins):
                    n[0] += 1
                    ins.then_inc(steps, 1)
                    dve.wait_ge(steps, t * total + n[0])

                if loads:
                    dve.wait_ge(loaded[s], 16 * loads if first else (t - s) * (8 * loads) + 16 * loads)
                if residual is None and not first:
                    dve.wait_ge(stored[s], (t - s) * 8)
                here = acc[:, bass.ds(t * MSGW, D)]
                step(dve.tensor_tensor(by_head(y[:, s, :]), by_head(here),
                                       repeat_inner(flat_inv[:, bass.ds(t * H, H)], C), ALU.mult))
                if own:
                    step(dve.tensor_tensor(by_head(h_in[:, s, :]), by_head(h_in[:, s, :]),
                                           repeat_inner(flat_own[:, bass.ds(t * H, H)], C), ALU.mult))
                    step(dve.tensor_tensor(y[:, s, :], y[:, s, :], h_in[:, s, :], ALU.add))
                    step(dve.tensor_tensor(y[:, s, :], y[:, s, :], bias_sb[:], ALU.add))
                if residual is not None:
                    step(dve.tensor_tensor(here, y[:, s, :], x_in[:, s, :], ALU.add))
                else:
                    step(dve.tensor_scalar(y[:, s, :], y[:, s, :], 0.0, None, op0=ALU.max))
                dve.sem_inc(used, 1)
                assert n[0] == total

            by_pairs(dve, tile)

        @block.gpsimd
        def _(pool):
            if residual is None:
                def store(t, s, first):
                    pool.wait_ge(used, t + 1)
                    pool.dma_start(table_out[bass.ds(t * P, P), :], y[:, s, :]).then_inc(stored[s], 16)

                by_pairs(pool, store)
                for s in range(2):
                    pool.wait_ge(stored[s], NTP * 8)


def layernorm_phase(nc, k, name, acc, table_out, out):
    with ExitStack() as ctx:
        m = Mem(nc, ctx, name)
        stats = m.sb("stats", [P, NTP * 6])
        mean = m.sb("mean", [P, NTP])
        var = m.sb("var", [P, NTP])
        tmp = m.sb("tmp", [P, NTP])
        eps = m.sb("eps", [P, 1])
        dv, var_made, root_made = m.sem("dve"), m.sem("var_made"), m.sem("root_made")
        normed, stored = m.sem("normed"), m.sem("stored")
        block = ctx.enter_context(nc.Block())
        st3 = stats[:].rearrange("p (t s) -> p t s", s=6)
        acc3 = acc.rearrange("p (t w) -> p t w", w=MSGW)
        SEG = 10

        @block.scalar
        def _(act):
            act.wait_ge(var_made, 1)
            act.activation(var[:], var[:], ACT.Sqrt, bias=eps[:]).then_inc(root_made, 1)

        @block.vector
        def _(dve):
            st = Steps(dve, dv)
            st(dve.memset(eps[:], EPS))
            with dve.Fori(0, NTP) as t:
                dve.bn_stats(stats[:, bass.ds(t * 6, 6)], acc[:, bass.ds(t * MSGW, D)])
            st(dve.memset(tmp[:], 0.0))
            st(dve.tensor_tensor(mean[:], st3[:, :, 1], st3[:, :, 4], ALU.add))
            st(dve.tensor_scalar(mean[:], mean[:], 0.5, None, op0=ALU.mult))
            st(dve.tensor_tensor(tmp[:], st3[:, :, 1], st3[:, :, 4], ALU.subtract))
            st(dve.tensor_tensor(tmp[:], tmp[:], tmp[:], ALU.mult))
            st(dve.tensor_scalar(tmp[:], tmp[:], 0.25, None, op0=ALU.mult))
            st(dve.tensor_tensor(var[:], st3[:, :, 2], st3[:, :, 5], ALU.add))
            st(dve.scalar_tensor_tensor(var[:], var[:], 1.0 / D, tmp[:], op0=ALU.mult, op1=ALU.add))
            dve.sem_inc(var_made, 1)
            dve.wait_ge(root_made, 1)
            st(dve.reciprocal(var[:], var[:]))
            with dve.Fori(0, NTP) as t:
                here = acc[:, bass.ds(t * MSGW, D)]
                dve.tensor_scalar(here, here, mean[:, bass.ds(t, 1)], var[:, bass.ds(t, 1)],
                                  op0=ALU.subtract, op1=ALU.mult).then_inc(normed, 1)

        @block.sync
        def _(sp):
            n = 0
            for t in range(0, NTP, SEG):
                sp.wait_ge(normed, t + SEG)
                if out is None:
                    sp.dma_start(table_out[t * P:(t + SEG) * P, :].rearrange("(t p) d -> p t d", p=P),
                                 acc3[:, t:t + SEG, 0:D]).then_inc(stored, 16)
                    n += 16
                    continue
                full = min(N // P, t + SEG) - t
                sp.dma_start(out[t * P:(t + full) * P, :].rearrange("(t p) d -> p t d", p=P),
                             acc3[:, t:t + full, 0:D]).then_inc(stored, 16)
                n += 16
                if full < SEG:
                    sp.dma_start(out[N // P * P:N, :], acc3[0:N % P, N // P, 0:D]).then_inc(stored, 16)
                    n += 16
            sp.wait_ge(stored, n)


def graph_conv_phase(nc, k, name, acc, table_in, w_rel, w_root, bias, table_out, residual):
    with ExitStack() as ctx:
        m = Mem(nc, ctx, name)
        w_sb = m.sb("w", [P, 4, D])
        bias_sb = m.sb("bias", [P, D])
        xin = m.sb("xin", [P, 2, D])
        agg = m.sb("agg", [P, 2, D])
        res = m.sb("res", [P, 2, D])
        inT = m.sb("inT", [P, 2, 2 * D])
        y = m.sb("y", [P, 2, D])
        low = m.sb("low", [P, 2, D])
        t_ps = [m.ps(f"t_ps{s}", [P, 512]) for s in range(2)]
        y_ps = [m.ps(f"y_ps{s}", [P, 512]) for s in range(2)]
        w_in = m.sem("w_in")
        loaded = [m.sem(f"loaded{s}") for s in range(2)]
        stored = [m.sem(f"stored{s}") for s in range(2)]
        agg_made, turned, inT_made, summed = m.sem("agg_made"), m.sem("turned"), m.sem("inT_made"), m.sem("summed")
        low_made, exp_made, y_made, steps = m.sem("low_made"), m.sem("exp_made"), m.sem("y_made"), m.sem("tile_steps")
        block = ctx.enter_context(nc.Block())
        loads = 1 + (residual is not None)

        @block.sync
        def _(sp):
            for n, w in enumerate((w_rel, w_root)):
                for c in range(2):
                    sp.dma_start(w_sb[:, 2 * n + c, :], w[c * P:(c + 1) * P, :]).then_inc(w_in, 16)
            sp.dma_start(bias_sb[:], bias.partition_broadcast(P)).then_inc(w_in, 16)

            def load(t, s, first):
                if not first:
                    sp.wait_ge(turned, t - 1)
                sp.dma_start(xin[:, s, :], table_in[bass.ds(t * P, P), :]).then_inc(loaded[s], 16)
                if residual is not None:
                    if not first:
                        sp.wait_ge(y_made, t - 1)
                    sp.dma_start(res[:, s, :], residual[bass.ds(t * P, P), :]).then_inc(loaded[s], 16)

            by_pairs(sp, load)

        @block.scalar
        def _(act):
            def take(t, s, first):
                if not first:
                    act.wait_ge(turned, t - 1)
                act.copy(agg[:, s, :], acc[:, bass.ds(t * MSGW, D)]).then_inc(agg_made, 1)

            def tile(t, s, first):
                take(t, s, first)
                act.wait_ge(turned, t + 1)
                if not first:
                    act.wait_ge(summed, t - 1)
                act.copy(inT[:, s, :], t_ps[s][:]).then_inc(inT_made, 1)
                act.wait_ge(low_made, t + 1)
                act.activation(low[:, s, :], low[:, s, :], ACT.Exp).then_inc(exp_made, 1)

            by_pairs(act, tile)

        @block.tensor
        def _(pe):
            pe.wait_ge(w_in, 80)

            def tile(t, s, first):
                pe.wait_ge(agg_made, t + 1)
                pe.wait_ge(loaded[s], 16 * loads if first else (t - s) * (8 * loads) + 16 * loads)
                for n, source in enumerate((agg, xin)):
                    for c in range(2):
                        ins = pe.transpose(t_ps[s][:, (2 * n + c) * P:(2 * n + c + 1) * P],
                                           source[:, s, c * P:(c + 1) * P], k.ident[:])
                ins.then_inc(turned, 1)
                pe.wait_ge(inT_made, t + 1)
                if not first:
                    pe.wait_ge(low_made, t - 1)
                for n in range(4):
                    ins = pe.matmul(y_ps[s][:, 0:D], inT[:, s, n * P:(n + 1) * P], w_sb[:, n, :],
                                    start=(n == 0), stop=(n == 3))
                ins.then_inc(summed, 1)

            by_pairs(pe, tile)

        @block.vector
        def _(dve):
            dve.wait_ge(w_in, 80)

            def tile(t, s, first):
                total = 2 + (residual is not None)
                dve.wait_ge(summed, t + 1)
                if residual is None and not first:
                    dve.wait_ge(stored[s], (t - s) * 8)
                dve.tensor_tensor(y[:, s, :], y_ps[s][:, 0:D], bias_sb[:], ALU.add).then_inc(steps, 1)
                dve.wait_ge(steps, t * total + 1)
                dve.tensor_scalar(low[:, s, :], y[:, s, :], 0.0, None, op0=ALU.min).then_inc(low_made, 1)
                dve.wait_ge(exp_made, t + 1)
                dve.tensor_scalar(low[:, s, :], low[:, s, :], -1.0, None, op0=ALU.add).then_inc(steps, 1)
                dve.wait_ge(steps, t * total + 2)
                fin = dve.scalar_tensor_tensor(y[:, s, :], y[:, s, :], 0.0, low[:, s, :], op0=ALU.max, op1=ALU.add)
                if residual is None:
                    fin.then_inc(y_made, 1)
                else:
                    fin.then_inc(steps, 1)
                    dve.wait_ge(steps, t * total + 3)
                    dve.tensor_tensor(acc[:, bass.ds(t * MSGW, D)], y[:, s, :], res[:, s, :], ALU.add).then_inc(y_made, 1)

            by_pairs(dve, tile)

        @block.gpsimd
        def _(pool):
            if residual is None:
                def store(t, s, first):
                    pool.wait_ge(y_made, t + 1)
                    pool.dma_start(table_out[bass.ds(t * P, P), :], y[:, s, :]).then_inc(stored[s], 16)

                by_pairs(pool, store)
                for s in range(2):
                    pool.wait_ge(stored[s], NTP * 8)


def batch_norm_layer_phase(nc, k, name, acc, table_in, w1, gamma1, beta1, w2, eps_weight, gamma_h, beta_h, norm_dram):
    NB = 512
    blocks = [(b, min(NB, NP - b)) for b in range(0, NP, NB)]
    stat_blocks = [(b, min(NB, N - b)) for b in range(0, N, NB)]
    with ExitStack() as ctx:
        m = Mem(nc, ctx, name)
        w_in_sb = m.sb("w_in_sb", [P, 2, 2, D])
        wT = m.sb("wT", [P, 2, 2, D])
        zT = m.sb("zT", [P, 2, NP])
        n_norm = m.sb("n_norm", [P, NP])
        xin = m.sb("xin", [P, 2, D])
        yin = m.sb("yin", [P, 2, D])
        yT = m.sb("yT", [P, 2, D])
        eps_w = m.sb("eps_w", [P, 1])
        cols = m.sb("cols", [P, 4, 2])
        stats = m.sb("stats", [P, 2, len(stat_blocks), 6])
        mv = m.sb("mv", [P, 2, 2])
        root = m.sb("root", [P, 2])
        scale = m.sb("scale", [P, 2])
        bias = m.sb("bias", [P, 2])
        eps = m.sb("eps", [P, 1])
        deg = m.sb("deg", [P, P])
        degT = m.sb("degT", [P, P])
        ps = [m.ps(f"ps{n}", [P, 512]) for n in range(6)]
        small_in, dv = m.sem("small_in"), m.sem("dve")
        deg_made, deg_root, deg_turned, degT_made, deg_stored, norm_in = (
            m.sem(n) for n in ("deg_made", "deg_root", "deg_turned", "degT_made", "deg_stored", "norm_in"))
        w_turned, wT_made = m.sem("w_turned"), m.sem("wT_made")
        loaded = [m.sem(f"loaded{s}") for s in range(2)]
        y_made, turned, yT_made, summed, z_made = (m.sem(n) for n in ("y_made", "turned", "yT_made", "summed", "z_made"))
        var_made, root_made, scale_made, relu_made = (m.sem(n) for n in ("var_made", "root_made", "scale_made", "relu_made"))
        summed2, z2_made = m.sem("summed2"), m.sem("z2_made")
        loaded2 = [m.sem(f"loaded2_{s}") for s in range(2)]
        doubled, turned2, done2 = m.sem("doubled"), m.sem("turned2"), m.sem("done2")
        block = ctx.enter_context(nc.Block())
        acc3 = acc.rearrange("p (t w) -> p t w", w=MSGW)

        @block.sync
        def _(sp):
            for n, w in enumerate((w1, w2)):
                for c in range(2):
                    sp.dma_start(w_in_sb[:, n, c, :], w[c * P:(c + 1) * P, :]).then_inc(small_in, 16)
            for n, v in enumerate((gamma1, beta1, gamma_h, beta_h)):
                sp.dma_start(cols[:, n, :], v.rearrange("(c p) -> p c", p=P),
                             allow_slow_non_contiguous=True).then_inc(small_in, 16)
            sp.dma_start(eps_w[:], eps_weight.partition_broadcast(P)).then_inc(small_in, 16)

            def load(t, s, first):
                if not first:
                    sp.wait_ge(y_made, t - 1)
                sp.dma_start(xin[:, s, :], table_in[bass.ds(t * P, P), :]).then_inc(loaded[s], 16)

            by_pairs(sp, load)
            sp.wait_ge(degT_made, 1)
            sp.dma_start(norm_dram.rearrange("(t p) -> t p", p=P), degT[0:NTP, :]).then_inc(deg_stored, 16)
            sp.wait_ge(deg_stored, 16)
            sp.dma_start(n_norm[:], norm_dram.partition_broadcast(P)).then_inc(norm_in, 16)

            sp.wait_ge(y_made, NTP)

            def load2(t, s, first):
                if not first:
                    sp.wait_ge(done2, t - 1)
                sp.dma_start(xin[:, s, :], table_in[bass.ds(t * P, P), :]).then_inc(loaded2[s], 16)

            by_pairs(sp, load2)

        @block.tensor
        def _(pe):
            pe.wait_ge(small_in, 144)
            for n in range(2):
                for c in range(2):
                    for o in range(2):
                        ins = pe.transpose(ps[n][:, (2 * c + o) * P:(2 * c + o + 1) * P],
                                           w_in_sb[:, n, o, c * P:(c + 1) * P], k.ident[:])
            ins.then_inc(w_turned, 1)
            pe.wait_ge(deg_root, 1)
            pe.transpose(ps[2][:, 0:P], deg[:], k.ident[:]).then_inc(deg_turned, 1)
            pe.wait_ge(wT_made, 1)
            pe.wait_ge(degT_made, 1)

            def tile(t, s, first):
                pe.wait_ge(y_made, t + 1)
                for c in range(2):
                    ins = pe.transpose(ps[s][:, c * P:(c + 1) * P], yin[:, s, c * P:(c + 1) * P], k.ident[:])
                ins.then_inc(turned, 1)
                pe.wait_ge(yT_made, t + 1)
                if not first:
                    pe.wait_ge(z_made, t - 1)
                for o in range(2):
                    for c in range(2):
                        ins = pe.matmul(ps[2 + s][:, o * P:(o + 1) * P], wT[:, 0, c, o * P:(o + 1) * P],
                                        yT[:, s, c * P:(c + 1) * P], start=(c == 0), stop=(c == 1))
                ins.then_inc(summed, 1)

            by_pairs(pe, tile)
            pe.wait_ge(z_made, NTP)
            pe.wait_ge(relu_made, 1)
            for n, (b, w) in enumerate(blocks):
                if n >= 2:
                    pe.wait_ge(z2_made, n - 1)
                for o in range(2):
                    for c in range(2):
                        ins = pe.matmul(ps[2 * (n % 2) + o][:, 0:w], wT[:, 1, c, o * P:(o + 1) * P],
                                        zT[:, c, b:b + w], start=(c == 0), stop=(c == 1))
                ins.then_inc(summed2, 1)
            pe.wait_ge(z2_made, len(blocks))
            pe.wait_ge(relu_made, 2)

            def back(t, s, first):
                pe.wait_ge(yT_made, t + NTP + 1)
                if not first:
                    pe.wait_ge(done2, t - 1)
                for c in range(2):
                    ins = pe.transpose(ps[s][:, c * P:(c + 1) * P], yT[:, s, c * P:(c + 1) * P], k.ident[:])
                ins.then_inc(turned2, 1)

            by_pairs(pe, back)

        @block.scalar
        def _(act):
            act.wait_ge(deg_made, 1)
            act.activation(deg[:, 0:NTP], deg[:, 0:NTP], ACT.Sqrt).then_inc(deg_made, 1)

            def tile(t, s, first):
                act.wait_ge(turned, t + 1)
                if not first:
                    act.wait_ge(summed, t - 1)
                act.copy(yT[:, s, :], ps[s][:, 0:D]).then_inc(yT_made, 1)

            by_pairs(act, tile)
            for n in range(2):
                act.wait_ge(var_made, n + 1)
                act.activation(root[:], mv[:, :, 1], ACT.Sqrt, bias=eps[:]).then_inc(root_made, 1)
                act.wait_ge(scale_made, n + 1)
                for o in range(2):
                    ins = act.activation(zT[:, o, :], zT[:, o, :], ACT.Relu, bias=bias[:, o:o + 1], scale=scale[:, o:o + 1])
                ins.then_inc(relu_made, 1)
            act.wait_ge(relu_made, 2)

            def out_tile(t, s, first):
                if first:
                    act.wait_ge(summed, NTP)
                else:
                    act.wait_ge(turned2, t - 1)
                act.copy(yT[:, s, :].rearrange("p (c n) -> p c n", c=2), zT[:, :, bass.ds(t * P, P)]).then_inc(yT_made, 1)

            by_pairs(act, out_tile)

        @block.vector
        def _(dve):
            st = Steps(dve, dv)
            st(dve.memset(eps[:], EPS))
            st(dve.memset(deg[:], 1.0))
            dve.tensor_scalar(deg[:, 0:NTP], acc3[:, :, MSG_ONE], 1.0, None, op0=ALU.max).then_inc(deg_made, 1)
            dve.wait_ge(deg_made, 2)
            st(dve.reciprocal(deg[:, 0:NTP], deg[:, 0:NTP]))
            dve.sem_inc(deg_root, 1)
            dve.wait_ge(deg_turned, 1)
            dve.tensor_copy(degT[:], ps[2][:, 0:P]).then_inc(degT_made, 1)
            dve.wait_ge(w_turned, 1)
            for n in range(2):
                st(dve.tensor_copy(wT[:, n].rearrange("p c d -> p (c d)"), ps[n][:]))
            dve.sem_inc(wT_made, 1)
            dve.wait_ge(small_in, 144)

            def tile(t, s, first):
                dve.wait_ge(loaded[s], 16 if first else (t - s) * 8 + 16)
                if not first:
                    dve.wait_ge(turned, t - 1)
                dve.scalar_tensor_tensor(yin[:, s, :], xin[:, s, :], eps_w[:], acc[:, bass.ds(t * MSGW, D)],
                                         op0=ALU.mult, op1=ALU.add).then_inc(y_made, 1)

            def take(t, s, first):
                dve.wait_ge(summed, t + 1)
                dve.tensor_copy(zT[:, :, bass.ds(t * P, P)], ps[2 + s][:, 0:D].rearrange("p (c n) -> p c n", c=2)).then_inc(z_made, 1)

            tile(0, 0, True)
            tile(1, 1, True)
            take(0, 0, True)
            take(1, 1, True)
            with dve.Fori(1, NTP // 2) as i:
                for s in range(2):
                    tile(i * 2 + s, s, False)
                for s in range(2):
                    take(i * 2 + s, s, False)
            dve.wait_ge(z_made, NTP)

            def stat(n):
                for o in range(2):
                    for b, (at, w) in enumerate(stat_blocks):
                        ins = dve.bn_stats(stats[:, o, b, :], zT[:, o, at:at + w])
                    st(ins)
                    st(dve.bn_aggr(mv[:, o, :], stats[:, o].rearrange("p b s -> p (b s)")))
                dve.sem_inc(var_made, 1)
                dve.wait_ge(root_made, n + 1)
                st(dve.reciprocal(root[:], root[:]))
                st(dve.tensor_tensor(scale[:], root[:], cols[:, 2 * n, :], ALU.mult))
                st(dve.tensor_tensor(bias[:], mv[:, :, 0], scale[:], ALU.mult))
                st(dve.tensor_tensor(bias[:], cols[:, 2 * n + 1, :], bias[:], ALU.subtract))
                dve.sem_inc(scale_made, 1)

            stat(0)
            dve.wait_ge(norm_in, 16)
            dve.wait_ge(relu_made, 1)
            for n, (b, w) in enumerate(blocks):
                dve.wait_ge(summed2, n + 1)
                for o in range(2):
                    ins = dve.tensor_tensor(zT[:, o, b:b + w], ps[2 * (n % 2) + o][:, 0:w], n_norm[:, b:b + w], ALU.mult)
                ins.then_inc(z2_made, 1)
            dve.wait_ge(z2_made, len(blocks))
            stat(1)

            def out_tile(t, s, first):
                dve.wait_ge(turned2, t + 1)
                dve.wait_ge(loaded2[s], 16 if first else (t - s) * 8 + 16)
                dve.scalar_tensor_tensor(acc[:, bass.ds(t * MSGW, D)], xin[:, s, :], 2.0, ps[s][:, 0:D],
                                         op0=ALU.mult, op1=ALU.add).then_inc(done2, 1)

            by_pairs(dve, out_tile)


class Shared:
    pass


def build_program(nc, a, out, upto=99, dbg=None):
    k = Shared()

    def dram(name, shape, dt=F32):
        return nc.dram_tensor(name, shape, dt).ap()

    table_x = dram("table_x", (NP, D))
    rec_low = dram("rec_low", (E, RW))
    rec_hi = dram("rec_hi", (EP, RW))
    tile_dram = dram("tile_dram", (NCH,), I32)
    with ExitStack() as ctx:
        m = Mem(nc, ctx, "k")
        k.iota = m.sb("iota", [P, P])
        k.ident = m.sb("ident", [P, P])
        k.before = m.sb("before", [P, P])
        k.ones = m.sb("ones", [P, P])
        k.tile_off = m.sb("tile_off", [1, NCH], I32)
        with ExitStack() as sort_ctx:
            ms = Mem(nc, sort_ctx, "sort")
            k.rec = ms.sb("rec", [P, SC, RW])
            k.chunk_no = ms.sb("chunk_no", [P, NCH // P + 1])
            k.tile_of = ms.sb("tile_of", [P, NCH // P + 1])
            k.tile_off_i = ms.sb("tile_off_i", [P, NCH // P + 1], I32)
            setup_phase(nc, k, a["src"], a["dst"], a["edge_weight"], a["edge_attr3_1x1"], a["x"], table_x, rec_hi)
            sort_phase(nc, k, "low", LOW, False, None, rec_low, None)
            sort_phase(nc, k, "high", HIGH, True, rec_low, rec_hi, tile_dram)
        k.src = m.sb("src", [P, NCH], I32)
        k.dst = m.sb("dst", [P, NCH], I32)
        k.local = m.sb("local", [P, NCH])
        k.weight = m.sb("weight", [P, NCH])
        k.dist = m.sb("dist", [P, NCH])
        k.breaks_in = m.sb("breaks_in", [1, P + 1])
        k.through_fwd = m.sb("through_fwd", [1, P])
        k.through_back = m.sb("through_back", [1, P])
        k.first_in_run = m.sb("first_in_run", [P, 1])
        k.numer = m.sb("numer", [P, H, NCH])
        k.first_max = m.sb("first_max", [P, H, NCH])
        flags_dram = dram("flags_dram", (P, RL + 1))
        edges_phase(nc, k, rec_hi, flags_dram)
        tables = [dram(f"table_{n}", (NP, D)) for n in range(3)]
        table_h = dram("table_h", (NP, D))
        table_a = dram("table_a", (NP, 2 * H))
        norm_dram = dram("norm_dram", (NP,))
        table_0, table_1, table_2 = tables

        def with_acc(name, body):
            with ExitStack() as ac:
                body(Mem(nc, ac, name).sb("acc", [P, NTP * MSGW])[:])

        def attention_layer(name, table_in, w, a_src, a_dst, bias, own, residual, table_out, normed_to, last=None):
            project_phase(nc, k, f"{name}p", table_in, w, a_src, a_dst, table_h, table_a)
            with ExitStack() as zc:
                mz = Mem(nc, zc, f"{name}z")
                z = mz.sb("z", [P, H, NCH])
                z_self = mz.sb("z_self", [P, H, NCH]) if own else None
                lookup_phase(nc, k, f"{name}l", table_a, z, z_self)
                softmax_phase(nc, k, f"{name}s", flags_dram, z, z_self, None if own else k.first_max)

            def rest(acc):
                aggregate_phase(nc, k, f"{name}a", table_h, acc, k.numer if own else k.first_max, True, True,
                                MSGW if own else MSG_M)
                attention_end_phase(nc, k, f"{name}e", acc, table_h, table_a if own else None, bias, residual, table_out)
                if residual is not None:
                    layernorm_phase(nc, k, f"{name}n", acc, normed_to, last)

            with_acc(name, rest)

        g0, g1, g2, g3 = ({n[7:]: v for n, v in a.items() if n.startswith(f"L{l}_gnn_")} for l in range(4))
        attention_layer("l0a", table_x, g0["W1"], g0["att_src1"], g0["att_dst1"], g0["b1"], True, None, table_0, None)
        if dbg and upto == 1: dbg(nc, k, locals()); return
        attention_layer("l0b", table_0, g0["W2"], g0["att_src2"], g0["att_dst2"], g0["b2"], True, table_x, None, table_1)
        if dbg and upto == 2: dbg(nc, k, locals()); return

        def conv(name, table_in, w_rel, w_root, bias, table_out, residual):
            def rest(acc):
                aggregate_phase(nc, k, f"{name}a", table_in, acc, None, False, False, D)
                graph_conv_phase(nc, k, f"{name}c", acc, table_in, w_rel, w_root, bias, table_out, residual)
                if residual is not None:
                    layernorm_phase(nc, k, f"{name}n", acc, table_0, None)

            with_acc(name, rest)

        conv("l1a", table_1, g1["W1_rel"], g1["W1_root"], g1["b1"], table_0, None)
        conv("l1b", table_0, g1["W2_rel"], g1["W2_root"], g1["b2"], table_2, None)
        conv("l1c", table_2, g1["W3_rel"], g1["W3_root"], g1["b3"], None, table_1)
        if dbg and upto == 3: dbg(nc, k, locals()); return

        def batch(acc):
            aggregate_phase(nc, k, "l2a", table_0, acc, k.weight, False, False, MSG_P)
            batch_norm_layer_phase(nc, k, "l2b", acc, table_0, g2["w1"], g2["gamma1"], g2["beta1"], g2["w2"],
                                   g2["eps_weight"], g2["gamma_h"], g2["beta_h"], norm_dram)
            layernorm_phase(nc, k, "l2n", acc, table_1, None)

        with_acc("l2", batch)
        if dbg and upto == 4: dbg(nc, k, locals()); return
        attention_layer("l3", table_1, g3["W"], g3["w_att_src"], g3["w_att_dst"], None, False, table_1, None, None, out)


def kernel(**inputs):
    import numpy as np
    import concourse.bacc as bacc
    from concourse.bass_utils import run_bass_kernel_spmd

    nc = bacc.Bacc("TRN2", target_bir_lowering=False, num_devices=1)
    arrays, args = {}, {}
    for name, value in inputs.items():
        arrays[name] = np.ascontiguousarray(value)
        args[name] = nc.dram_tensor(name, arrays[name].shape, mybir.dt.from_np(arrays[name].dtype),
                                    kind="ExternalInput").ap()
    out = nc.dram_tensor("out", (N, D), F32, kind="ExternalOutput").ap()
    build_program(nc, args, out)
    return run_bass_kernel_spmd(nc, [arrays], core_ids=[0]).results[0]["out"]
```

```python
from contextlib import ExitStack

import concourse.bass as bass
from concourse import mybir

P = 128
N = 6250
E = 100000
D = 256
H = 4
C = D // H
NT = -(-N // P)
NTP = NT + NT % 2
NP = NTP * P
SP_, SC = 125, 800
U = 8
SLOTS = 4
NCH = -(-(E // P + 1 + NT) // (U * SLOTS)) * U * SLOTS
NCH = max(NCH, 832)
EP = NCH * P
RUN = NCH // 32
RL = RUN * P
LOW, HIGH = 128, NT
RW = 4
MSG_ONE = D
MSG_P = D + 1
MSG_M = D + 1 + H
MSGW = D + 1 + 2 * H
NEG = -1.0e30
NO_NODE = -1.0
SLOPE = 0.2
EPS = 1e-5

ALU = mybir.AluOpType
ACT = mybir.ActivationFunctionType
AX = mybir.AxisListType
F32 = mybir.dt.float32
BF16 = mybir.dt.bfloat16
U16 = mybir.dt.uint16
I32 = mybir.dt.int32
assert E == SP_ * SC and NCH % (U * SLOTS) == 0 and NCH * P >= E + NT * (P - 1)


class Steps:

    def __init__(self, eng, sem):
        self.eng, self.sem, self.n = eng, sem, 0

    def __call__(self, ins):
        ins.then_inc(self.sem, 1)
        self.n += 1
        self.eng.wait_ge(self.sem, self.n)


def repeat_inner(ap, n):
    return ap.unsqueeze(2).to_broadcast([ap.shape[0], ap.shape[1], n])


def by_chunk(heads):
    return heads[:].rearrange("p h c -> p c h")


def pipeline(eng, *parts):
    lags = [lag for _, lag in parts]
    peel = max(lags) + 2 + max(lags) % 2

    def step(n, r):
        for body, lag in parts:
            if not isinstance(n, int):
                body(n - lag if lag else n, (r - lag) % 2, False)
            elif 0 <= n - lag < NTP:
                body(n - lag, (n - lag) % 2, n - lag < 2)

    for n in range(peel):
        step(n, n % 2)
    with eng.Fori(peel // 2, NTP // 2) as i:
        for r in range(2):
            step(i * 2 + r, r)
    for n in range(NTP, NTP + max(lags)):
        step(n, n % 2)


def repeat_outer(ap, n):
    return ap.unsqueeze(1).to_broadcast([ap.shape[0], n, ap.shape[1]])


class Mem:

    def __init__(self, nc, ctx, phase):
        self.nc, self.ctx, self.phase, self.sems = nc, ctx, phase, []

    def sb(self, name, shape, dt=F32):
        return self.ctx.enter_context(self.nc.sbuf_tensor(f"{self.phase}_{name}", shape, dt))

    def ps(self, name, shape, dt=F32):
        return self.ctx.enter_context(self.nc.psum_tensor(f"{self.phase}_{name}", shape, dt))

    def sem(self, name):
        if not self.sems:
            self.ctx.callback(self.clear)
        self.sems.append(self.nc.alloc_semaphore(f"{self.phase}_{name}"))
        return self.sems[-1]

    def clear(self):
        self.nc.clear_and_free_semaphores(self.sems)
        self.nc.all_engine_barrier()


def setup_phase(nc, k, src, dst, ew, dist, x, table_x):
    with ExitStack() as ctx:
        m = Mem(nc, ctx, "setup")
        ints = m.sb("edge_ints", [P, 2, SC], I32)
        fls = m.sb("edge_floats", [P, 2, SC], F32)
        zero = m.sb("zero_rows", [P, D])
        after = m.sb("after", [P, SC], I32)
        falls = m.sb("falls", [P, SC])
        fall = m.sb("fall", [P, 1])
        fall_ps = m.ps("fall_ps", [P, 512])
        const_all, fall_made, fall_summed = m.sem("const_all"), m.sem("fall_made"), m.sem("fall_summed")
        edges_in = m.sem("edges_in")
        const = m.sem("const_made")
        zero_made = m.sem("zero_made")
        after_set = m.sem("after_set")
        out_done = m.sem("setup_stored")
        dv = m.sem("setup_dve")
        block = ctx.enter_context(nc.Block())

        @block.sync
        def _(sp):
            for n, a in enumerate((src, dst)):
                sp.dma_start(ints[0:SP_, n, :], a.rearrange("(p s) -> p s", p=SP_)).then_inc(edges_in, 16)
            sp.dma_start(fls[0:SP_, 0, :], ew.rearrange("(p s) -> p s", p=SP_)).then_inc(edges_in, 16)
            sp.dma_start(fls[0:SP_, 1, :], dist.rearrange("(p s) a b -> p (s a b)", p=SP_)).then_inc(edges_in, 16)
            sp.wait_ge(after_set, 1)
            body = (SP_ - 1) * SC
            sp.dma_start(after[0:SP_ - 1, :], dst[1:1 + body].rearrange("(p s) -> p s", s=SC)).then_inc(edges_in, 16)
            sp.dma_start(after[SP_ - 1:SP_, 0:SC - 1], dst[1 + body:E].rearrange("(p s) -> p s", p=1)).then_inc(edges_in, 16)
            sp.dma_start(table_x[0:N, :], x).then_inc(out_done, 16)
            sp.wait_ge(zero_made, 1)
            sp.dma_start(table_x[N:N + 128, :], zero[:]).then_inc(out_done, 16)
            sp.dma_start(table_x[N + 128:NP, :], zero[0:NP - N - 128, :]).then_inc(out_done, 16)
            sp.wait_ge(out_done, 48)

        @block.gpsimd
        def _(pool):
            st = Steps(pool, const)
            pool.iota(k.chunk_no[:], [[P * P, NCH // P + 1]], base=0, channel_multiplier=P,
                      allow_small_or_imprecise_dtypes=True)
            pool.iota(k.iota[:], [[1, P]], base=0, channel_multiplier=0,
                      allow_small_or_imprecise_dtypes=True)
            st(pool.memset(k.ident[:], 0.0))
            st(pool.affine_select(out=k.ident[:], in_=k.ident[:], compare_op=ALU.not_equal, fill=1.0,
                                  base=0, pattern=[[-1, P]], channel_multiplier=1))
            pool.iota(k.partition[:], [[0, 1]], base=0, channel_multiplier=1,
                      allow_small_or_imprecise_dtypes=True)
            st(pool.memset(k.before[:], 1.0))
            st(pool.affine_select(out=k.before[:], in_=k.before[:], compare_op=ALU.is_ge, fill=0.0,
                                  base=-1, pattern=[[1, P]], channel_multiplier=-1))
            pool.memset(k.ones[:], 1.0).then_inc(const_all, 1)

        @block.vector
        def _(dve):
            st = Steps(dve, dv)
            dve.memset(after[:], NP).then_inc(after_set, 1)
            dve.memset(zero[:], 0.0).then_inc(zero_made, 1)
            dve.wait_ge(edges_in, 96)
            st(dve.tensor_tensor(falls[0:SP_], ints[0:SP_, 1, :], after[0:SP_], ALU.is_gt))
            dve.tensor_reduce(fall[0:SP_], falls[0:SP_], AX.X, ALU.max).then_inc(fall_made, 1)
            dve.wait_ge(fall_summed, 1)
            dve.tensor_copy(k.unsorted[:], fall_ps[0:1, 0:1])
            dve.tensor_copy(k.rec[0:SP_, :, 0], ints[0:SP_, 0, :])
            dve.tensor_copy(k.rec[0:SP_, :, 1], ints[0:SP_, 1, :])
            dve.tensor_copy(k.rec[0:SP_, :, 2], fls[0:SP_, 0, :])
            dve.tensor_copy(k.rec[0:SP_, :, 3], fls[0:SP_, 1, :])

        @block.tensor
        def _(pe):
            pe.wait_ge(const_all, 1)
            pe.wait_ge(fall_made, 1)
            pe.matmul(fall_ps[0:1, 0:1], fall[0:SP_], k.ones[0:SP_, 0:1], start=True, stop=True).then_inc(fall_summed, 1)


def sort_phase(nc, k, name, buckets, high, rec_to, tile_dram):
    CB = 8
    with ExitStack() as ctx:
        m = Mem(nc, ctx, name)
        key = m.sb("key", [P, SC])
        key_i = m.sb("key_i", [P, SC], I32)
        rank = m.sb("rank", [P, SC])
        pos = m.sb("pos", [P, SC], I32)
        mask = m.sb("mask", [P, SC], BF16)
        count = m.sb("count", [P, SC])
        one_row = m.sb("one_row", [P, SC])
        totals = m.sb("totals", [P, P])
        start = m.sb("start", [P, P])
        size = m.sb("size", [P, P])
        size_i = m.sb("size_i", [P, P], I32)
        base = m.sb("base", [P, P])
        pos_ring = m.sb("pos_ring", [P, 2, CB], I32)
        rec_ring = m.sb("rec_ring", [P, 2, CB, RW])
        chunk_at = m.sb("chunk_at", [P, NCH // P + 1, NT]) if high else None
        pads = m.sb("pad_records", [P, NCH, RW]) if high else None
        pads_made, pads_stored = m.sem("pads_made"), m.sem("pads_stored")
        before_ps = m.ps("before_ps", [P, 512])
        total_ps = m.ps("total_ps", [P, 512])
        dv = m.sem(f"dve")
        in_loop = m.sem(f"bucket_steps")
        in_loop2 = m.sem(f"base_steps")
        totals_made = m.sem(f"totals")
        base_ps_made = m.sem(f"base_ps")
        pos_made = m.sem(f"pos")
        ring_full = m.sem(f"ring_full")
        scattered = [m.sem(f"scattered{s}") for s in range(2)]
        turn = m.sem("scatter_turn")
        block = ctx.enter_context(nc.Block())
        S = slice(0, SP_)

        @block.sync
        def _(sp):
            if high:
                sp.wait_ge(pads_made, 1)
                sp.dma_start(rec_to.rearrange("(p q) w -> p (q w)", p=P),
                             pads[:].rearrange("p a b -> p (a b)")).then_inc(pads_stored, 16)

        @block.vector
        def _(dve):
            st = Steps(dve, dv)
            if high:
                st(dve.memset(pads[:], 0.0))
                dve.memset(pads[:, :, 1], NO_NODE).then_inc(pads_made, 1)
            st(dve.tensor_copy(key_i[S], k.rec[S, :, 1]))
            if high:
                st(dve.tensor_scalar(pos[S], key_i[S], 7, None, op0=ALU.arith_shift_right))
            else:
                st(dve.tensor_scalar(pos[S], key_i[S], LOW - 1, None, op0=ALU.bitwise_and))
            st(dve.tensor_copy(key[S], pos[S]))
            st(dve.memset(rank[:], 0.0))
            st(dve.memset(one_row[:], 1.0))
            st(dve.memset(totals[:], 0.0))
            with dve.Fori(0, buckets) as b:
                dve.tensor_scalar(mask[S], key[S], k.iota[S, bass.ds(b, 1)], None,
                                  op0=ALU.is_equal).then_inc(in_loop, 1)
                dve.wait_ge(in_loop, b * 4 + 1)
                dve.tensor_tensor_scan(count[S], one_row[S], mask[S], 0.0,
                                       op0=ALU.mult, op1=ALU.add).then_inc(in_loop, 1)
                dve.wait_ge(in_loop, b * 4 + 2)
                dve.tensor_copy(totals[S, bass.ds(b, 1)], count[S, SC - 1:SC]).then_inc(in_loop, 1)
                dve.copy_predicated(rank[S], mask[S].bitcast(U16), count[S]).then_inc(in_loop, 1)
                dve.wait_ge(in_loop, b * 4 + 4)
            dve.sem_inc(totals_made, 1)
            dve.wait_ge(base_ps_made, 1)
            st(dve.tensor_copy(size[:, 0:buckets], total_ps[:, 0:buckets]))
            if high:
                st(dve.tensor_scalar(size[:, 0:buckets], size[:, 0:buckets], float(P - 1), None, op0=ALU.add))
                st(dve.tensor_copy(size_i[:, 0:buckets], size[:, 0:buckets]))
                st(dve.tensor_scalar(size_i[:, 0:buckets], size_i[:, 0:buckets], -P, None, op0=ALU.bitwise_and))
                st(dve.tensor_copy(size[:, 0:buckets], size_i[:, 0:buckets]))
            st(dve.tensor_tensor_scan(start[:, 0:buckets], one_row[:, 0:buckets], size[:, 0:buckets], 0.0,
                                      op0=ALU.mult, op1=ALU.add))
            if high:
                nq = NCH // P + 1
                cols = k.chunk_no[:, 0:nq]
                st(dve.tensor_tensor(chunk_at[:, 0:nq, :], repeat_inner(cols, NT),
                                     repeat_outer(start[:, 0:NT], nq), ALU.is_ge))
                st(dve.tensor_reduce(k.tile_of[:, 0:nq], chunk_at[:, 0:nq, :], AX.X, ALU.add))
                for n, step in enumerate((MSGW, 2 * H)):
                    st(dve.tensor_scalar(chunk_at[:, 0:nq, 0], k.tile_of[:, 0:nq], float(NT - 1), float(step),
                                         op0=ALU.min, op1=ALU.mult))
                    st(dve.tensor_copy(k.tile_off_i[:, n, 0:nq], chunk_at[:, 0:nq, 0]))
            st(dve.tensor_tensor(start[:, 0:buckets], start[:, 0:buckets], size[:, 0:buckets], ALU.subtract))
            st(dve.tensor_tensor(base[:, 0:buckets], before_ps[:, 0:buckets], start[:, 0:buckets], ALU.add))
            with dve.Fori(0, buckets) as b:
                dve.tensor_scalar(count[S], key[S], k.iota[S, bass.ds(b, 1)], base[S, bass.ds(b, 1)],
                                  op0=ALU.is_equal, op1=ALU.mult).then_inc(in_loop2, 1)
                dve.wait_ge(in_loop2, b * 2 + 1)
                dve.tensor_tensor(rank[S], rank[S], count[S], ALU.add).then_inc(in_loop2, 1)
                dve.wait_ge(in_loop2, b * 2 + 2)
            st(dve.tensor_scalar(rank[S], rank[S], -1.0, None, op0=ALU.add))
            dve.tensor_copy(pos[S], rank[S]).then_inc(pos_made, 1)

        @block.tensor
        def _(pe):
            pe.wait_ge(totals_made, 1)
            pe.matmul(before_ps[:, 0:buckets], k.before[S, :], totals[S, 0:buckets], start=True, stop=True)
            pe.matmul(total_ps[:, 0:buckets], k.ones[S, :], totals[S, 0:buckets], start=True,
                      stop=True).then_inc(base_ps_made, 1)

        @block.scalar
        def _(act):
            def fill(s, at):
                act.copy(pos_ring[S, s, :], pos[S, bass.ds(at, CB)])
                act.copy(rec_ring[S, s].rearrange("p a b -> p (a b)"),
                         k.rec[S].rearrange("p a b -> p (a b)")[:, bass.ds(at * RW, CB * RW)]).then_inc(ring_full, 1)

            act.wait_ge(pos_made, 1)
            for s in range(2):
                fill(s, s * CB)
            with act.Fori(1, SC // CB // 2) as i:
                for s in range(2):
                    act.wait_ge(scattered[s], i * (16 * CB))
                    fill(s, (i * 2 + s) * CB)

        @block.gpsimd
        def _(pool):
            if high:
                pool.wait_ge(pads_stored, 16)
            with pool.Fori(0, SC // CB // 2) as i:
                for s in range(2):
                    pool.wait_ge(ring_full, i * 2 + s + 1)
                    pool.sem_inc(turn, 1)
                    for c in range(CB):
                        pool.indirect_dma_start(
                            out=rec_to, out_offset=bass.IndirectOffsetOnAxis(ap=pos_ring[S, s, c:c + 1], axis=0),
                            in_=rec_ring[S, s, c, :], in_offset=None).then_inc(scattered[s], 16)
            for s in range(2):
                pool.wait_ge(scattered[s], SC // 2 * 16)
    if not high:
        with ExitStack() as ctx:
            loaded = Mem(nc, ctx, "resorted").sem("loaded")
            block = ctx.enter_context(nc.Block())

            @block.sync
            def _(sp):
                sp.dma_start(k.rec[0:SP_].rearrange("p a b -> p (a b)"),
                             rec_to.rearrange("(p s) w -> p (s w)", p=SP_)).then_inc(loaded, 16)
                sp.wait_ge(loaded, 16)
    else:
        with ExitStack() as ctx:
            m = Mem(nc, ctx, "chunks")
            stored = m.sem("tile_offsets_stored")
            block = ctx.enter_context(nc.Block())
            nf = NCH // P

            @block.sync
            def _(sp):
                for n, row in enumerate((k.tile_off, k.tile_off_a)):
                    sp.dma_start(tile_dram[n, 0:nf * P].rearrange("(q p) -> p q", p=P), k.tile_off_i[:, n, 0:nf],
                                 allow_slow_non_contiguous=True).then_inc(stored, 16)
                    sp.dma_start(tile_dram[n, nf * P:NCH].rearrange("(p q) -> p q", q=1),
                                 k.tile_off_i[0:NCH - nf * P, n, nf:nf + 1]).then_inc(stored, 16)
                sp.wait_ge(stored, 64)
                for n, row in enumerate((k.tile_off, k.tile_off_a)):
                    sp.dma_start(row[0:1, :], tile_dram[n:n + 1, :]).then_inc(stored, 16)
                sp.wait_ge(stored, 96)



def edges_phase(nc, k, rec_hi, flags_dram):
    with ExitStack() as ctx:
        m = Mem(nc, ctx, "edges")
        rec = m.sb("rec", [P, NCH, RW])
        dst_i = m.sb("dst_i", [P, NCH], I32)
        low_i = m.sb("low_i", [P, NCH], I32)
        none = m.sb("none", [P, NCH])
        dst4 = m.sb("dst4", [P, H, NCH])
        dst_scan = m.sb("dst_scan", [P, RL])
        breaks = m.sb("breaks", [P, RL + 1])
        ends = m.sb("ends", [P, 4])
        row = m.sb("row", [1, 3, P])
        tp = [m.ps(f"tp{n}", [P, P]) for n in range(2)]
        rows_ps = m.ps("rows_ps", [P, 512])
        loaded, dv, stored = m.sem("loaded"), m.sem("dve"), m.sem("stored")
        dst4_made, turned, taken = m.sem("dst4_made"), m.sem("turned"), m.sem("taken")
        ends_made, rows_made = m.sem("ends_made"), m.sem("rows_made")
        first_made, first_turned = m.sem("first_made"), m.sem("first_turned")
        breaks_made = m.sem("breaks_made")
        block = ctx.enter_context(nc.Block())

        @block.sync
        def _(sp):
            half = NCH // 2
            by_edge = rec_hi.rearrange("(c e) w -> e c w", e=P)
            sp.dma_start(rec[:, 0:half, :], by_edge[:, 0:half, :]).then_inc(loaded, 16)
            sp.dma_start(rec[:, half:, :], by_edge[:, half:, :]).then_inc(loaded, 16)
            sp.wait_ge(breaks_made, 1)
            sp.dma_start(flags_dram, breaks[:]).then_inc(stored, 16)
            sp.wait_ge(stored, 16)

        @block.vector
        def _(dve):
            st = Steps(dve, dv)
            dve.tensor_copy(k.tiles[:], k.iota[:, 0:NT])
            dve.wait_ge(loaded, 32)
            dve.tensor_copy(dst4[:], repeat_outer(rec[:, :, 1], H)).then_inc(dst4_made, 1)
            st(dve.tensor_copy(k.src[:], rec[:, :, 0]))
            st(dve.tensor_scalar(low_i[:], k.src[:], 7, None, op0=ALU.arith_shift_right))
            st(dve.tensor_copy(k.src_tile[:], low_i[:]))
            st(dve.tensor_copy(k.weight[:], rec[:, :, 2]))
            st(dve.tensor_copy(k.dist[:], rec[:, :, 3]))
            st(dve.tensor_scalar(none[:], rec[:, :, 1], 0.0, float(8 * P), op0=ALU.is_lt, op1=ALU.mult))
            st(dve.tensor_scalar(k.local[:], rec[:, :, 1], 0.0, None, op0=ALU.max))
            st(dve.tensor_copy(dst_i[:], k.local[:]))
            st(dve.tensor_scalar(low_i[:], dst_i[:], P - 1, None, op0=ALU.bitwise_and))
            st(dve.tensor_copy(k.local[:], low_i[:]))
            st(dve.tensor_tensor(k.local[:], k.local[:], none[:], ALU.add))
            for c in range(RUN):
                dve.wait_ge(turned, c + 1)
                dve.tensor_copy(dst_scan[:, c * P:(c + 1) * P], tp[c % 2][:]).then_inc(taken, 1)
            dve.wait_ge(taken, RUN)
            st(dve.memset(breaks[:], 0.0))
            st(dve.tensor_tensor(breaks[:, 1:RL], dst_scan[:, 1:RL], dst_scan[:, 0:RL - 1], ALU.not_equal))
            st(dve.tensor_reduce(ends[:, 2:3], breaks[:], AX.X, ALU.max))
            st(dve.tensor_scalar(breaks[:], breaks[:], NEG, None, op0=ALU.mult))
            dve.sem_inc(breaks_made, 1)
            st(dve.tensor_copy(ends[:, 0:1], dst_scan[:, 0:1]))
            st(dve.tensor_copy(ends[:, 1:2], dst_scan[:, RL - 1:RL]))
            dve.sem_inc(ends_made, 1)
            dve.wait_ge(rows_made, 1)
            st(dve.tensor_copy(row[0:1].rearrange("a b c -> a (b c)"), rows_ps[0:1, 0:3 * P]))
            st(dve.memset(k.breaks_in[:], 1.0))
            for h in range(H):
                st(dve.tensor_tensor(k.breaks_in[0:1, 32 * h + 1:32 * h + 32], row[0:1, 0, 32 * h + 1:32 * h + 32],
                                     row[0:1, 1, 32 * h:32 * h + 31], ALU.not_equal))
            st(dve.tensor_tensor(k.through_fwd[:], k.breaks_in[0:1, 0:P], row[0:1, 2, :], ALU.max))
            st(dve.tensor_tensor(k.through_back[:], k.breaks_in[0:1, 1:P + 1], row[0:1, 2, :], ALU.max))
            st(dve.tensor_copy(row[0:1, 0, :], k.breaks_in[0:1, 0:P]))
            dve.sem_inc(first_made, 1)
            st(dve.tensor_scalar(k.through_fwd[:], k.through_fwd[:], NEG, None, op0=ALU.mult))
            st(dve.tensor_scalar(k.through_back[:], k.through_back[:], NEG, None, op0=ALU.mult))
            st(dve.tensor_scalar(k.breaks_in[:], k.breaks_in[:], NEG, None, op0=ALU.mult))
            dve.wait_ge(first_turned, 1)
            st(dve.tensor_copy(k.first_in_run[:], rows_ps[:, 384:385]))

        @block.tensor
        def _(pe):
            pe.wait_ge(dst4_made, 1)
            by_run = dst4[:].rearrange("p h (r c) -> p c (h r)", c=RUN)
            for c in range(RUN):
                if c >= 2:
                    pe.wait_ge(taken, c - 1)
                pe.transpose(tp[c % 2][:], by_run[:, c], k.ident[:]).then_inc(turned, 1)
            pe.wait_ge(ends_made, 1)
            for n in range(3):
                ins = pe.transpose(rows_ps[0:1, n * P:(n + 1) * P], ends[:, n:n + 1], k.ident[:])
            ins.then_inc(rows_made, 1)
            pe.wait_ge(first_made, 1)
            pe.transpose(rows_ps[:, 384:385], row[0:1, 0, :], k.ident[0:1, 0:1]).then_inc(first_turned, 1)


def codes_phase(nc, k, rec_hi, codes_dram):
    nf, rest = NCH // P, NCH % P
    with ExitStack() as ctx:
        m = Mem(nc, ctx, "codes")
        rec = m.sb("rec", [P, nf + 1, P, RW])
        ints = m.sb("ints", [P, 2, nf + 1, P], I32)
        low = m.sb("low", [P, 2, nf + 1, P], I32)
        none = m.sb("none", [P, nf + 1, P])
        codes = m.sb("codes", [P, 2, nf + 1, P], BF16)
        loaded, dv, made, stored = m.sem("loaded"), m.sem("dve"), m.sem("made"), m.sem("stored")
        block = ctx.enter_context(nc.Block())

        @block.sync
        def _(sp):
            by_chunk_rows = rec_hi.rearrange("(c e) w -> c (e w)", e=P)
            sp.dma_start(rec[:, 0:nf].rearrange("p q e w -> p q (e w)"),
                         by_chunk_rows[0:nf * P].rearrange("(q p) x -> p q x", p=P)).then_inc(loaded, 16)
            sp.dma_start(rec[0:rest, nf].rearrange("p e w -> p (e w)"), by_chunk_rows[nf * P:NCH]).then_inc(loaded, 16)
            sp.wait_ge(made, 1)
            for n in range(2):
                row = codes_dram[n].rearrange("(c e) -> c e", e=P)
                sp.dma_start(row[0:nf * P].rearrange("(q p) e -> p q e", p=P), codes[:, n, 0:nf]).then_inc(stored, 16)
                sp.dma_start(row[nf * P:NCH], codes[0:rest, n, nf]).then_inc(stored, 16)
            sp.wait_ge(stored, 64)

        @block.vector
        def _(dve):
            st = Steps(dve, dv)
            dve.wait_ge(loaded, 32)
            for rows, qs in ((slice(0, P), slice(0, nf)), (slice(0, rest), slice(nf, nf + 1))):
                at = (rows, qs)
                st(dve.tensor_scalar(none[at], rec[rows, qs, :, 1], 0.0, float(8 * P), op0=ALU.is_lt, op1=ALU.mult))
                for n in range(2):
                    st(dve.tensor_scalar(rec[rows, qs, :, n], rec[rows, qs, :, n], 0.0, None, op0=ALU.max))
                    st(dve.tensor_copy(ints[rows, n, qs], rec[rows, qs, :, n]))
                    st(dve.tensor_scalar(low[rows, n, qs], ints[rows, n, qs], P - 1, None, op0=ALU.bitwise_and))
                st(dve.tensor_copy(codes[rows, 0, qs], low[rows, 0, qs]))
                st(dve.tensor_tensor(codes[rows, 1, qs], low[rows, 1, qs], none[at], ALU.add))
            dve.sem_inc(made, 1)


def aggregate_phase(nc, k, name, table, acc, scale, head_scale, softmax, width):
    with ExitStack() as ctx:
        m = Mem(nc, ctx, name)
        ring = m.sb("messages", [P, SLOTS, U, MSGW])
        index = m.sb("index", [P, SLOTS, U], I32)
        member = m.sb("member", [P, 2, U, P])
        sums = [m.ps(f"sums{j}", [P, 512]) for j in range(U)]
        gathered = [m.sem(f"gathered{s}") for s in range(SLOTS)]
        turn = m.sem("gather_turn")
        index_ready = m.sem("index_ready")
        set_up = m.sem("set_up")
        prepared = m.sem("prepared")
        member_made = m.sem("member_made")
        chunk_summed = m.sem("chunk_summed")
        chunk_added = m.sem("chunk_added")
        block = ctx.enter_context(nc.Block())
        units = NCH // U

        @block.gpsimd
        def _(pool):
            with pool.Fori(0, units // SLOTS) as i:
                for s in range(SLOTS):
                    pool.wait_ge(index_ready, i * SLOTS + s + 1)
                    pool.sem_inc(turn, 1)
                    for j in range(U):
                        pool.indirect_dma_start(
                            out=ring[:, s, j, 0:D], out_offset=None, in_=table,
                            in_offset=bass.IndirectOffsetOnAxis(ap=index[:, s, j:j + 1], axis=0),
                        ).then_inc(gathered[s], 16)

        @block.scalar
        def _(act):
            def fill(s, u):
                if softmax:
                    act.copy(ring[:, s, :, MSG_P:MSG_P + H],
                             by_chunk(k.numer)[:, bass.ds(u * U, U), :])
                if width > MSG_M:
                    act.copy(ring[:, s, :, MSG_M:MSG_M + H],
                             by_chunk(k.first_max)[:, bass.ds(u * U, U), :])
                act.copy(index[:, s, :], k.src[:, bass.ds(u * U, U)]).then_inc(index_ready, 1)

            act.wait_ge(set_up, 1)
            for s in range(SLOTS):
                fill(s, s)
            with act.Fori(1, units // SLOTS) as i:
                for s in range(SLOTS):
                    act.wait_ge(chunk_summed, i * (SLOTS * U) + (s + 1 - SLOTS) * U)
                    fill(s, i * SLOTS + s)

        @block.vector
        def _(dve):
            def prepare(i, s):
                u = i * SLOTS + s
                dve.wait_ge(index_ready, u + 1)
                dve.tensor_tensor(member[:, s % 2], repeat_outer(k.iota[:], U),
                                  repeat_inner(k.local[:, bass.ds(u * U, U)], P), ALU.is_equal).then_inc(member_made, 1)
                dve.wait_ge(gathered[s], i * (16 * U) + 16 * U)
                msgs = ring[:, s, :, 0:D]
                if scale is None:
                    dve.sem_inc(prepared, 1)
                elif head_scale:
                    for j in range(U):
                        mj = ring[:, s, j, 0:D].rearrange("p (h f) -> p h f", h=H)
                        ins = dve.tensor_tensor(mj, mj, repeat_inner(by_chunk(scale)[:, u * U + j, :], C), ALU.mult)
                    ins.then_inc(prepared, 1)
                else:
                    dve.tensor_tensor(msgs, msgs, repeat_inner(scale[:, bass.ds(u * U, U)], D),
                                      ALU.mult).then_inc(prepared, 1)

            def add(i, s):
                u = i * SLOTS + s
                offs = nc.values_load_multi_w_load_instructions(
                    k.tile_off[0:1, bass.ds(u * U, U)], engines=(mybir.EngineType.DVE,),
                    min_val=0, max_val=(NT - 1) * MSGW, skip_runtime_bounds_check_because="made so")[1]
                for j in range(U):
                    dve.wait_ge(chunk_summed, u * U + (j + 1))
                    dve.wait_ge(chunk_added, u * U + (j + 1))
                    at = acc[:, bass.ds(offs[j], width)]
                    dve.tensor_tensor(at, at, sums[j][:, 0:width], ALU.add).then_inc(chunk_added, 1)

            dve.memset(acc, 0.0).then_inc(chunk_added, 1)
            dve.memset(ring[:, :, :, MSG_ONE], 1.0).then_inc(set_up, 1)
            prepare(0, 0)
            with dve.Fori(0, units // SLOTS - 1) as i:
                for s in range(SLOTS):
                    prepare(i + (s + 1) // SLOTS, (s + 1) % SLOTS)
                    add(i, s)
            last = units // SLOTS - 1
            for s in range(SLOTS):
                if s + 1 < SLOTS:
                    prepare(last, s + 1)
                add(last, s)

        @block.tensor
        def _(pe):
            def sum_unit(i, s, first):
                u = i * SLOTS + s
                pe.wait_ge(member_made, u + 1)
                pe.wait_ge(prepared, u + 1)
                for j in range(U):
                    if not first:
                        pe.wait_ge(chunk_added, u * U + (j + 2 - U))
                    pe.matmul(sums[j][:, 0:width], member[:, s % 2, j, :], ring[:, s, j, 0:width],
                              start=True, stop=True).then_inc(chunk_summed, 1)

            for s in range(SLOTS):
                sum_unit(0, s, s == 0)
            with pe.Fori(1, units // SLOTS) as i:
                for s in range(SLOTS):
                    sum_unit(i, s, False)


def project_phase(nc, k, name, table_in, w, att_src, att_dst, table_h):
    WE = D + 2 * H
    with ExitStack() as ctx:
        m = Mem(nc, ctx, name)
        w_sb = m.sb("w", [P, 2, WE])
        att = m.sb("att", [P, 2, D])
        prod = m.sb("prod", [P, 2, D])
        xin = m.sb("xin", [P, 2, D])
        xt = m.sb("xt", [P, 2, D])
        h_out = m.sb("h_out", [P, 2, D])
        xt_ps = [m.ps(f"xt_ps{s}", [P, 512]) for s in range(2)]
        h_ps = [m.ps(f"h_ps{s}", [P, 512]) for s in range(2)]
        w_in, dv = m.sem("w_in"), m.sem("dve")
        w_ready = m.sem("w_ready")
        loaded = [m.sem(f"loaded{s}") for s in range(2)]
        stored = [m.sem(f"stored{s}") for s in range(2)]
        turned, xt_made, summed, h_made = m.sem("turned"), m.sem("xt_made"), m.sem("summed"), m.sem("h_made")
        block = ctx.enter_context(nc.Block())

        @block.sync
        def _(sp):
            for c in range(2):
                sp.dma_start(w_sb[:, c, 0:D], w[c * P:(c + 1) * P, :]).then_inc(w_in, 16)
            for n, a in enumerate((att_src, att_dst)):
                flat = a.rearrange("h c -> (h c)") if len(a.shape) == 2 else a.rearrange("a h c -> (a h c)")
                sp.dma_start(att[:, n, :], flat.partition_broadcast(P)).then_inc(w_in, 16)

            def load(t, s, first):
                if not first:
                    sp.wait_ge(turned, t - 1)
                sp.dma_start(xin[:, s, :], table_in[bass.ds(t * P, P), :]).then_inc(loaded[s], 16)

            pipeline(sp, (load, 0))

        @block.tensor
        def _(pe):
            pe.wait_ge(w_ready, 1)

            def turn(t, s, first):
                pe.wait_ge(loaded[s], (t - s) * 8 + 16)
                if not first:
                    pe.wait_ge(xt_made, t - 1)
                for c in range(2):
                    ins = pe.transpose(xt_ps[s][:, c * P:(c + 1) * P], xin[:, s, c * P:(c + 1) * P], k.ident[:])
                ins.then_inc(turned, 1)

            def multiply(t, s, first):
                pe.wait_ge(xt_made, t + 1)
                if not first:
                    pe.wait_ge(h_made, t - 1)
                for c in range(2):
                    ins = pe.matmul(h_ps[s][:, 0:WE], xt[:, s, c * P:(c + 1) * P], w_sb[:, c, :],
                                    start=(c == 0), stop=(c == 1))
                ins.then_inc(summed, 1)

            pipeline(pe, (turn, 0), (multiply, 1))

        @block.scalar
        def _(act):
            def take(t, s, first):
                act.wait_ge(turned, t + 1)
                if not first:
                    act.wait_ge(summed, t - 1)
                act.copy(xt[:, s, :], xt_ps[s][:, 0:D]).then_inc(xt_made, 1)

            pipeline(act, (take, 0))

        @block.vector
        def _(dve):
            st = Steps(dve, dv)
            dve.wait_ge(w_in, 64)
            for n in range(2):
                for c in range(2):
                    st(dve.tensor_tensor(prod[:, c, :], w_sb[:, c, 0:D], att[:, n, :], ALU.mult))
                    st(dve.tensor_reduce(w_sb[:, c, D + n * H:D + (n + 1) * H],
                                         prod[:, c, :].rearrange("p (h f) -> p h f", h=H), AX.X, ALU.add))
            dve.sem_inc(w_ready, 1)

            def take(t, s, first):
                dve.wait_ge(summed, t + 1)
                if not first:
                    dve.wait_ge(stored[s], (t - s) * 8)
                dve.tensor_copy(k.att[:, bass.ds(t * 2 * H, 2 * H)], h_ps[s][:, D:WE])
                dve.tensor_copy(h_out[:, s, :], h_ps[s][:, 0:D]).then_inc(h_made, 1)

            pipeline(dve, (take, 0))

        @block.gpsimd
        def _(pool):
            def store(t, s, first):
                pool.wait_ge(h_made, t + 1)
                pool.dma_start(table_h[bass.ds(t * P, P), :], h_out[:, s, :]).then_inc(stored[s], 16)

            pipeline(pool, (store, 0))
            for s in range(2):
                pool.wait_ge(stored[s], NTP * 8)


def lookup_phase(nc, k, name, codes_dram, z, z_self):
    G = U // 2
    NS = H * NT
    with ExitStack() as ctx:
        m = Mem(nc, ctx, name)
        left = m.sb("left", [P, NTP, 2 * H])
        dst_parts = m.sb("dst_parts", [P, 3, NTP * 2 * H], BF16)
        src_parts = m.sb("src_parts", [P, 3, H, NT], BF16)
        codes = m.sb("codes", [P, 2, 2, U * P], BF16)
        member = m.sb("member", [P, 2, 2, U * P], BF16)
        mask = m.sb("mask", [P, 2, U, NT], BF16)
        prod = m.sb("prod", [P, 2, G, H, NT])
        picked = m.sb("picked", [P, 2, U, H])
        src_ps = [m.ps(f"src_ps{g}", [P, G, 256]) for g in range(2)]
        dst_ps = [m.ps(f"dst_ps{s}", [P, 512]) for s in range(2)]
        dv, parts_made = m.sem("dve"), m.sem("parts_made")
        codes_in = [m.sem(f"codes_in{s}") for s in range(2)]
        member_made, summed, multiplied, reduced, taken = (
            m.sem(n) for n in ("member_made", "summed", "multiplied", "reduced", "taken"))
        mask_made, copied = m.sem("mask_made"), m.sem("copied")
        block = ctx.enter_context(nc.Block())
        units = NCH // U

        @block.sync
        def _(sp):
            def load(u, s, first):
                if not first:
                    sp.wait_ge(member_made, u - 1)
                sp.dma_start(codes[:, s], codes_dram[:, bass.ds(u * (U * P), U * P)].partition_broadcast(P)).then_inc(codes_in[s], 16)

            for s in range(2):
                load(s, s, True)
            with sp.Fori(1, units // 2) as i:
                for s in range(2):
                    load(i * 2 + s, s, False)

        @block.vector
        def _(dve):
            st = Steps(dve, dv)
            st(dve.tensor_copy(left[:].rearrange("p t a -> p (t a)"), k.att[:]))
            for n in range(3):
                part = dst_parts[:, n].rearrange("p (t a) -> p t a", a=2 * H)
                st(dve.tensor_copy(part, left[:]))
                if n < 2:
                    st(dve.tensor_tensor(left[:], left[:], part, ALU.subtract))
                dve.tensor_copy(src_parts[:, n].rearrange("p h t -> p t h"), part[:, 0:NT, 0:H]).then_inc(parts_made, 1)

            def prepare(i, s):
                u = i * 2 + s
                dve.wait_ge(codes_in[s], i * 16 + 16)
                for n in range(2):
                    ins = dve.tensor_scalar(member[:, s, n], codes[:, s, n], k.partition[:], None, op0=ALU.is_equal)
                ins.then_inc(member_made, 1)
                dve.tensor_tensor(mask[:, s], repeat_outer(k.tiles[:], U),
                                  repeat_inner(k.src_tile[:, bass.ds(u * U, U)], NT), ALU.is_equal).then_inc(mask_made, 1)

            def pick(i, s):
                u = i * 2 + s
                dve.wait_ge(mask_made, u + 1)
                for g in range(2):
                    dve.wait_ge(summed, u * 2 + g + 1)
                    dve.tensor_tensor(prod[:, g], src_ps[g][:, :, 0:NS].rearrange("p c (h t) -> p c h t", h=H),
                                      mask[:, s, g * G:(g + 1) * G].unsqueeze(2).to_broadcast([P, G, H, NT]),
                                      ALU.mult).then_inc(multiplied, 1)
                for g in range(2):
                    dve.wait_ge(multiplied, u * 2 + g + 1)
                    dve.tensor_reduce(picked[:, s, g * G:(g + 1) * G], prod[:, g], AX.X, ALU.add).then_inc(reduced, 1)
                dst = dst_ps[s][:, 0:U * 2 * H].rearrange("p (c a) -> p c a", a=2 * H)
                if z_self is not None:
                    zs = by_chunk(z_self)[:, bass.ds(u * U, U), :]
                    dve.tensor_copy(zs, dst[:, :, 0:H]).then_inc(copied, 1)
                    dve.wait_ge(copied, u + 1)
                    dve.tensor_tensor(zs, zs, dst[:, :, H:], ALU.add)
                dve.wait_ge(reduced, u * 2 + 2)
                dve.tensor_tensor(by_chunk(z)[:, bass.ds(u * U, U), :], picked[:, s], dst[:, :, H:], ALU.add).then_inc(taken, 1)

            prepare(0, 0)
            with dve.Fori(0, units // 2 - 1) as i:
                prepare(i, 1)
                pick(i, 0)
                prepare(i + 1, 0)
                pick(i, 1)
            last = units // 2 - 1
            prepare(last, 1)
            pick(last, 0)
            pick(last, 1)

        @block.tensor
        def _(pe):
            pe.wait_ge(parts_made, 3)

            def look(i, s, first):
                u = i * 2 + s
                offs = nc.values_load_multi_w_load_instructions(
                    k.tile_off_a[0:1, bass.ds(u * U, U)], engines=(mybir.EngineType.PE,),
                    min_val=0, max_val=(NT - 1) * 2 * H, skip_runtime_bounds_check_because="made so")[1]
                pe.wait_ge(member_made, u + 1)
                if not first:
                    pe.wait_ge(taken, u - 1)
                for g in range(2):
                    if not (first and s == 0):
                        pe.wait_ge(multiplied, u * 2 + g - 1)
                    for c in range(G):
                        j = g * G + c
                        for n in range(3):
                            pe.matmul(src_ps[g][:, c, 0:NS], member[:, s, 0, j * P:(j + 1) * P],
                                      src_parts[:, n].rearrange("p h t -> p (h t)"), start=(n == 0), stop=(n == 2))
                        for n in range(3):
                            ins = pe.matmul(dst_ps[s][:, j * 2 * H:(j + 1) * 2 * H], member[:, s, 1, j * P:(j + 1) * P],
                                            dst_parts[:, n, bass.ds(offs[j], 2 * H)], start=(n == 0), stop=(n == 2))
                    ins.then_inc(summed, 1)

            for s in range(2):
                look(0, s, True)
            with pe.Fori(1, units // 2) as i:
                for s in range(2):
                    look(i, s, False)


def softmax_phase(nc, k, name, flags_dram, z, z_self, scaled):
    with ExitStack() as ctx:
        m = Mem(nc, ctx, name)
        breaks = m.sb("breaks", [P, RL + 1])
        z_scan = m.sb("z_scan", [P, RL])
        self_scan = m.sb("self_scan", [P, RL]) if z_self is not None else None
        fwd = m.sb("fwd", [P, RL])
        back = m.sb("back", [P, RL])
        row = m.sb("row", [1, 2, P + 2])
        carry = m.sb("carry", [P, 2])
        tp = [m.ps(f"tp{n}", [P, P]) for n in range(4)]
        row_ps = m.ps("row_ps", [P, 512])
        flags_in, dv = m.sem("flags_in"), m.sem("dve")
        leaky_made, turned, taken_v, taken_a = m.sem("leaky_made"), m.sem("turned"), m.sem("taken_dve"), m.sem("taken_act")
        last_made, row_made, row_carried, carry_made = m.sem("last_made"), m.sem("row_made"), m.sem("row_carried"), m.sem("carry_made")
        max_made, numer_made = m.sem("max_made"), m.sem("numer_made")
        block = ctx.enter_context(nc.Block())
        both = z_self is not None
        by_run = lambda t: t[:].rearrange("p h (r c) -> p c (h r)", c=RUN)

        @block.sync
        def _(sp):
            sp.dma_start(breaks[:], flags_dram).then_inc(flags_in, 16)

        @block.tensor
        def _(pe):
            pe.wait_ge(leaky_made, 1)
            for c in range(RUN):
                if c >= 2:
                    pe.wait_ge(taken_a, c - 1)
                pe.transpose(tp[c % 2][:], by_run(z)[:, c], k.ident[:]).then_inc(turned, 1)
                if both:
                    if c >= 2:
                        pe.wait_ge(taken_v, c - 1)
                    pe.transpose(tp[2 + c % 2][:], by_run(z_self)[:, c], k.ident[:]).then_inc(turned, 1)
            for n, (source, at) in enumerate(((fwd, RL - 1), (back, 0))):
                pe.wait_ge(last_made, n + 1)
                pe.transpose(row_ps[0:1, 0:P], source[:, at:at + 1], k.ident[:]).then_inc(row_made, 1)
                pe.wait_ge(row_carried, n + 1)
                pe.transpose(row_ps[:, 256 + n:257 + n], row[0:1, 1, 0:P], k.ident[0:1, 0:1]).then_inc(carry_made, 1)
            pe.wait_ge(max_made, 1)
            pe.wait_ge(taken_a, RUN)
            if both:
                pe.wait_ge(taken_v, RUN)
            for c in range(RUN):
                if c >= 2:
                    pe.wait_ge(taken_a, RUN + c - 1)
                pe.transpose(tp[c % 2][:], back[:, c * P:(c + 1) * P], k.ident[:]).then_inc(turned, 1)
                if both:
                    if c >= 2:
                        pe.wait_ge(taken_v, RUN + c - 1)
                    pe.transpose(tp[2 + c % 2][:], fwd[:, c * P:(c + 1) * P], k.ident[:]).then_inc(turned, 1)

        per = 2 if both else 1

        @block.scalar
        def _(act):
            for c in range(RUN):
                act.wait_ge(turned, per * c + 1)
                act.copy(z_scan[:, c * P:(c + 1) * P], tp[c % 2][:]).then_inc(taken_a, 1)
            for c in range(RUN):
                act.wait_ge(turned, per * (RUN + c) + 1)
                act.copy(by_run(k.numer)[:, c], tp[c % 2][:]).then_inc(taken_a, 1)
            act.wait_ge(numer_made, 1)
            act.activation(k.numer[:], k.numer[:], ACT.Exp).then_inc(numer_made, 1)

        @block.vector
        def _(dve):
            st = Steps(dve, dv)
            for t in (z, z_self) if both else (z,):
                st(dve.scalar_tensor_tensor(t[:], t[:], SLOPE, t[:], op0=ALU.mult, op1=ALU.max))
            dve.sem_inc(leaky_made, 1)
            if both:
                for c in range(RUN):
                    dve.wait_ge(turned, 2 * c + 2)
                    dve.tensor_copy(self_scan[:, c * P:(c + 1) * P], tp[2 + c % 2][:]).then_inc(taken_v, 1)
                dve.wait_ge(taken_v, RUN)
            dve.wait_ge(flags_in, 16)
            dve.wait_ge(taken_a, RUN)
            st(dve.memset(row[:], 0.0))

            def scan_fwd(initial):
                return dve.tensor_tensor_scan(fwd[:], breaks[:, 0:RL], z_scan[:], initial, op0=ALU.add, op1=ALU.max)

            def scan_back(initial):
                return dve.tensor_tensor_scan(back[:, ::-1], breaks[:, 1:RL + 1][:, ::-1], fwd[:, ::-1], initial,
                                              op0=ALU.add, op1=ALU.max)

            st(scan_fwd(NEG))
            dve.sem_inc(last_made, 1)
            dve.wait_ge(row_made, 1)
            st(dve.tensor_tensor_scan(row[0:1, 0, 1:P + 1], k.through_fwd[:], row_ps[0:1, 0:P], NEG,
                                      op0=ALU.add, op1=ALU.max))
            st(dve.tensor_tensor(row[0:1, 1, 0:P], row[0:1, 0, 0:P], k.breaks_in[0:1, 0:P], ALU.add))
            dve.sem_inc(row_carried, 1)
            dve.wait_ge(carry_made, 1)
            st(dve.tensor_copy(carry[:, 0:1], row_ps[:, 256:257]))
            st(scan_fwd(carry[:, 0:1]))
            st(scan_back(NEG))
            dve.sem_inc(last_made, 1)
            dve.wait_ge(row_made, 2)
            st(dve.memset(row[0:1, 0, P:P + 2], 0.0))
            st(dve.tensor_tensor_scan(row[0:1, 0, 0:P][:, ::-1], k.through_back[0:1, ::-1], row_ps[0:1, 0:P][:, ::-1],
                                      NEG, op0=ALU.add, op1=ALU.max))
            st(dve.tensor_tensor(row[0:1, 1, 0:P], row[0:1, 0, 1:P + 1], k.breaks_in[0:1, 1:P + 1], ALU.add))
            dve.sem_inc(row_carried, 1)
            dve.wait_ge(carry_made, 2)
            st(dve.tensor_copy(carry[:, 1:2], row_ps[:, 257:258]))
            st(scan_back(carry[:, 1:2]))
            if both:
                st(dve.tensor_tensor(back[:], back[:], self_scan[:], ALU.max))
                st(dve.tensor_scalar(fwd[:], breaks[:, 0:RL], 0.0, None, op0=ALU.not_equal))
                st(dve.tensor_copy(fwd[:, 0:1], k.first_in_run[:]))
                st(dve.tensor_tensor(fwd[:], fwd[:], back[:], ALU.mult))
            dve.sem_inc(max_made, 1)
            if both:
                for c in range(RUN):
                    dve.wait_ge(turned, 2 * (RUN + c) + 2)
                    dve.tensor_copy(by_run(k.first_max)[:, c], tp[2 + c % 2][:]).then_inc(taken_v, 1)
            dve.wait_ge(taken_a, 2 * RUN)
            dve.tensor_tensor(k.numer[:], z[:], k.numer[:], ALU.subtract).then_inc(numer_made, 1)
            if scaled is not None:
                dve.wait_ge(numer_made, 2)
                dve.tensor_tensor(scaled[:], k.numer[:], repeat_outer(k.dist[:], H), ALU.mult)


SEG = 10
assert NTP % SEG == 0


def attention_end_phase(nc, k, name, acc, table_h, own, bias, residual, table_out):
    with ExitStack() as ctx:
        m = Mem(nc, ctx, name)
        zn = m.sb("zn", [P, NTP, H])
        mx = m.sb("mx", [P, NTP, H])
        inv = m.sb("inv", [P, NTP, H])
        no_edge = m.sb("no_edge", [P, NTP])
        bias_sb = m.sb("bias", [P, D])
        h_in = m.sb("h_in", [P, 2, SEG, D])
        x_in = m.sb("x_in", [P, 2, SEG, D])
        dv, small_in, numer_ready, numer_made = m.sem("dve"), m.sem("small_in"), m.sem("numer_ready"), m.sem("numer_made")
        h_loaded = [m.sem(f"h_loaded{s}") for s in range(2)]
        x_loaded = [m.sem(f"x_loaded{s}") for s in range(2)]
        weights_made, h_scaled, x_biased, seg_made, relu_made, stored = (
            m.sem(n) for n in ("weights_made", "h_scaled", "x_biased", "seg_made", "relu_made", "stored"))
        block = ctx.enter_context(nc.Block())
        acc3 = acc.rearrange("p (t w) -> p t w", w=MSGW)
        segs = [(n, n % 2, slice(n * SEG, (n + 1) * SEG)) for n in range(NTP // SEG)]

        def rows(table, ts):
            return table[ts.start * P:ts.stop * P, :].rearrange("(t p) d -> p t d", p=P)

        def by_tile(ap):
            return ap.unsqueeze(1).to_broadcast([P, SEG, D])

        @block.sync
        def _(sp):
            if own:
                sp.dma_start(bias_sb[:], bias.partition_broadcast(P)).then_inc(small_in, 16)
            for n, s, ts in segs:
                if n >= 2:
                    sp.wait_ge(seg_made, n - 1)
                if own:
                    sp.dma_start(h_in[:, s], rows(table_h, ts)).then_inc(h_loaded[s], 16)
                if residual is not None:
                    sp.dma_start(x_in[:, s], rows(residual, ts)).then_inc(x_loaded[s], 16)

        @block.scalar
        def _(act):
            if own:
                act.wait_ge(numer_ready, 1)
                act.activation(zn[:], zn[:], ACT.Exp).then_inc(numer_made, 1)
            if residual is None:
                for n, s, ts in segs:
                    act.wait_ge(seg_made, n + 1)
                    act.activation(acc3[:, ts, 0:D], acc3[:, ts, 0:D], ACT.Relu).then_inc(relu_made, 1)
                    act.wait_ge(relu_made, n + 1)
                    act.dma_start(rows(table_out, ts), acc3[:, ts, 0:D]).then_inc(stored, 16)
                act.wait_ge(stored, 16 * len(segs))

        @block.gpsimd
        def _(pool):
            if own:
                pool.wait_ge(small_in, 16)
                pool.wait_ge(weights_made, 1)
                for n, s, ts in segs:
                    pool.wait_ge(h_loaded[s], 16 * (n // 2 + 1))
                    for t in range(SEG):
                        rows_h = h_in[:, s, t].rearrange("p (h f) -> p h f", h=H)
                        ins = pool.tensor_tensor(rows_h, rows_h, repeat_inner(zn[:, ts.start + t, :], C), ALU.mult)
                    ins.then_inc(h_scaled, 1)
                    if residual is not None:
                        pool.wait_ge(x_loaded[s], 16 * (n // 2 + 1))
                        pool.tensor_tensor(x_in[:, s], x_in[:, s], by_tile(bias_sb[:]), ALU.add).then_inc(x_biased, 1)

        @block.vector
        def _(dve):
            st = Steps(dve, dv)
            sums_p = acc3[:, :, MSG_P:MSG_P + H]
            if own:
                att = k.att[:].rearrange("p (t a) -> p t a", a=2 * H)
                st(dve.tensor_tensor(zn[:], att[:, :, 0:H], att[:, :, H:], ALU.add))
                st(dve.scalar_tensor_tensor(zn[:], zn[:], SLOPE, zn[:], op0=ALU.mult, op1=ALU.max))
                st(dve.tensor_scalar(no_edge[:], acc3[:, :, MSG_ONE], 0.5, None, op0=ALU.is_lt))
                st(dve.tensor_tensor(mx[:], zn[:], repeat_inner(no_edge[:], H), ALU.mult))
                st(dve.tensor_tensor(mx[:], mx[:], acc3[:, :, MSG_M:MSG_M + H], ALU.add))
                st(dve.tensor_tensor(zn[:], zn[:], mx[:], ALU.subtract))
                dve.sem_inc(numer_ready, 1)
                dve.wait_ge(numer_made, 1)
                st(dve.tensor_tensor(inv[:], zn[:], sums_p, ALU.add))
                st(dve.tensor_scalar(inv[:], inv[:], 1e-16, None, op0=ALU.add))
            else:
                st(dve.tensor_scalar(inv[:], sums_p, 1e-30, None, op0=ALU.max))
            st(dve.reciprocal(inv[:], inv[:]))
            if own:
                st(dve.tensor_tensor(zn[:], zn[:], inv[:], ALU.mult))
                dve.sem_inc(weights_made, 1)
                dve.wait_ge(small_in, 16)
            for n, s, ts in segs:
                here = acc3[:, ts, 0:D]
                for t in range(SEG):
                    row = acc3[:, ts.start + t, 0:D].rearrange("p (h f) -> p h f", h=H)
                    ins = dve.tensor_tensor(row, row, repeat_inner(inv[:, ts.start + t, :], C), ALU.mult)
                st(ins)
                if own:
                    dve.wait_ge(h_scaled, n + 1)
                    st(dve.tensor_tensor(here, here, h_in[:, s], ALU.add))
                if residual is None:
                    dve.tensor_tensor(here, here, by_tile(bias_sb[:]), ALU.add).then_inc(seg_made, 1)
                else:
                    dve.wait_ge(*((x_biased, n + 1) if own else (x_loaded[s], 16 * (n // 2 + 1))))
                    dve.tensor_tensor(here, here, x_in[:, s], ALU.add).then_inc(seg_made, 1)


def layernorm_phase(nc, k, name, acc, table_out, out):
    with ExitStack() as ctx:
        m = Mem(nc, ctx, name)
        stats = m.sb("stats", [P, NTP, 6])
        mean = m.sb("mean", [P, NTP])
        var = m.sb("var", [P, NTP])
        tmp = m.sb("tmp", [P, NTP])
        eps = m.sb("eps", [P, 1])
        dv, var_made, root_made = m.sem("dve"), m.sem("var_made"), m.sem("root_made")
        centred, normed, stored = m.sem("centred"), m.sem("normed"), m.sem("stored")
        block = ctx.enter_context(nc.Block())
        acc3 = acc.rearrange("p (t w) -> p t w", w=MSGW)
        segs = [(n, slice(n * SEG, (n + 1) * SEG)) for n in range(NTP // SEG)]

        @block.scalar
        def _(act):
            act.wait_ge(var_made, 1)
            act.activation(var[:], var[:], ACT.Sqrt, bias=eps[:]).then_inc(root_made, 1)

        @block.vector
        def _(dve):
            st = Steps(dve, dv)
            st(dve.memset(eps[:], EPS))
            for t in range(NTP):
                ins = dve.bn_stats(stats[:, t, :], acc3[:, t, 0:D])
            st(ins)
            st(dve.tensor_tensor(mean[:], stats[:, :, 1], stats[:, :, 4], ALU.add))
            st(dve.tensor_scalar(mean[:], mean[:], 0.5, None, op0=ALU.mult))
            st(dve.tensor_tensor(tmp[:], stats[:, :, 1], stats[:, :, 4], ALU.subtract))
            st(dve.tensor_tensor(tmp[:], tmp[:], tmp[:], ALU.mult))
            st(dve.tensor_scalar(tmp[:], tmp[:], 0.25, None, op0=ALU.mult))
            st(dve.tensor_tensor(var[:], stats[:, :, 2], stats[:, :, 5], ALU.add))
            st(dve.scalar_tensor_tensor(var[:], var[:], 1.0 / D, tmp[:], op0=ALU.mult, op1=ALU.add))
            dve.sem_inc(var_made, 1)
            dve.wait_ge(root_made, 1)
            st(dve.reciprocal(var[:], var[:]))
            for n, ts in segs:
                for t in range(ts.start, ts.stop):
                    ins = dve.tensor_scalar(acc3[:, t, 0:D], acc3[:, t, 0:D], mean[:, t:t + 1], var[:, t:t + 1],
                                            op0=ALU.subtract, op1=ALU.mult)
                ins.then_inc(normed, 1)

        @block.sync
        def _(sp):
            n_stored = 0
            for n, ts in segs:
                sp.wait_ge(normed, n + 1)
                if out is None:
                    parts = [(table_out, ts.stop)]
                else:
                    parts = [(out, min(N // P, ts.stop))]
                for table, stop in parts:
                    sp.dma_start(table[ts.start * P:stop * P, :].rearrange("(t p) d -> p t d", p=P),
                                 acc3[:, ts.start:stop, 0:D]).then_inc(stored, 16)
                    n_stored += 16
                if out is not None and stop < ts.stop:
                    sp.dma_start(out[stop * P:N, :], acc3[0:N % P, stop, 0:D]).then_inc(stored, 16)
                    n_stored += 16
            sp.wait_ge(stored, n_stored)


def graph_conv_phase(nc, k, name, acc, table_in, w_rel, w_root, bias, table_out, residual):
    with ExitStack() as ctx:
        m = Mem(nc, ctx, name)
        w_sb = m.sb("w", [P, 4, D])
        bias_sb = m.sb("bias", [P, D])
        xin = m.sb("xin", [P, 2, D])
        agg = m.sb("agg", [P, 2, D])
        res = m.sb("res", [P, 2, D])
        inT = m.sb("inT", [P, 2, 2 * D])
        y = m.sb("y", [P, 2, D])
        low = m.sb("low", [P, 2, D])
        t_ps = [m.ps(f"t_ps{s}", [P, 512]) for s in range(2)]
        y_ps = [m.ps(f"y_ps{s}", [P, 512]) for s in range(2)]
        w_in = m.sem("w_in")
        loaded = [m.sem(f"loaded{s}") for s in range(2)]
        stored = [m.sem(f"stored{s}") for s in range(2)]
        agg_made, turned, inT_made, summed = m.sem("agg_made"), m.sem("turned"), m.sem("inT_made"), m.sem("summed")
        res_loaded = [m.sem(f"res_loaded{s}") for s in range(2)]
        low_made, exp_made, y_made, y_summed, lowered, elu_made = (
            m.sem(n) for n in ("low_made", "exp_made", "y_made", "y_summed", "lowered", "elu_made"))
        block = ctx.enter_context(nc.Block())

        @block.sync
        def _(sp):
            for n, w in enumerate((w_rel, w_root)):
                for c in range(2):
                    sp.dma_start(w_sb[:, 2 * n + c, :], w[c * P:(c + 1) * P, :]).then_inc(w_in, 16)
            sp.dma_start(bias_sb[:], bias.partition_broadcast(P)).then_inc(w_in, 16)

            def load(t, s, first):
                if not first:
                    sp.wait_ge(turned, t - 1)
                sp.dma_start(xin[:, s, :], table_in[bass.ds(t * P, P), :]).then_inc(loaded[s], 16)

            pipeline(sp, (load, 0))

        @block.scalar
        def _(act):
            def place(t, s, first):
                if not first:
                    act.wait_ge(turned, t - 1)
                act.copy(agg[:, s, :], acc[:, bass.ds(t * MSGW, D)]).then_inc(agg_made, 1)

            def take(t, s, first):
                act.wait_ge(turned, t + 1)
                if not first:
                    act.wait_ge(summed, t - 1)
                act.copy(inT[:, s, :], t_ps[s][:]).then_inc(inT_made, 1)

            def exp(t, s, first):
                act.wait_ge(low_made, t + 1)
                act.activation(low[:, s, :], low[:, s, :], ACT.Exp).then_inc(exp_made, 1)

            pipeline(act, (place, 0), (take, 0), (exp, 1))

        @block.tensor
        def _(pe):
            pe.wait_ge(w_in, 80)

            def turn(t, s, first):
                pe.wait_ge(agg_made, t + 1)
                pe.wait_ge(loaded[s], (t - s) * 8 + 16)
                if not first:
                    pe.wait_ge(inT_made, t - 1)
                for n, source in enumerate((agg, xin)):
                    for c in range(2):
                        ins = pe.transpose(t_ps[s][:, (2 * n + c) * P:(2 * n + c + 1) * P],
                                           source[:, s, c * P:(c + 1) * P], k.ident[:])
                ins.then_inc(turned, 1)

            def multiply(t, s, first):
                pe.wait_ge(inT_made, t + 1)
                if not first:
                    pe.wait_ge(y_summed, t - 1)
                for n in range(4):
                    ins = pe.matmul(y_ps[s][:, 0:D], inT[:, s, n * P:(n + 1) * P], w_sb[:, n, :],
                                    start=(n == 0), stop=(n == 3))
                ins.then_inc(summed, 1)

            pipeline(pe, (turn, 0), (multiply, 1))

        @block.vector
        def _(dve):
            dve.wait_ge(w_in, 80)

            def start(t, s, first):
                dve.wait_ge(summed, t + 1)
                if residual is None and not first:
                    dve.wait_ge(stored[s], (t - s) * 8)
                if residual is not None and not first:
                    dve.wait_ge(y_made, t - 1)
                dve.tensor_tensor(y[:, s, :], y_ps[s][:, 0:D], bias_sb[:], ALU.add).then_inc(y_summed, 1)
                dve.wait_ge(y_summed, t + 1)
                dve.tensor_scalar(low[:, s, :], y[:, s, :], 0.0, None, op0=ALU.min).then_inc(low_made, 1)

            def finish(t, s, first):
                dve.wait_ge(exp_made, t + 1)
                dve.tensor_scalar(low[:, s, :], low[:, s, :], -1.0, None, op0=ALU.add).then_inc(lowered, 1)
                dve.wait_ge(lowered, t + 1)
                elu = dve.scalar_tensor_tensor(y[:, s, :], y[:, s, :], 0.0, low[:, s, :], op0=ALU.max, op1=ALU.add)
                if residual is None:
                    elu.then_inc(y_made, 1)
                else:
                    elu.then_inc(elu_made, 1)
                    dve.wait_ge(elu_made, t + 1)
                    dve.wait_ge(res_loaded[s], (t - s) * 8 + 16)
                    dve.tensor_tensor(acc[:, bass.ds(t * MSGW, D)], y[:, s, :], res[:, s, :], ALU.add).then_inc(y_made, 1)

            pipeline(dve, (start, 0), (finish, 1))

        @block.gpsimd
        def _(pool):
            if residual is None:
                def store(t, s, first):
                    pool.wait_ge(y_made, t + 1)
                    pool.dma_start(table_out[bass.ds(t * P, P), :], y[:, s, :]).then_inc(stored[s], 16)

                pipeline(pool, (store, 0))
                for s in range(2):
                    pool.wait_ge(stored[s], NTP * 8)
            else:
                def load_res(t, s, first):
                    if not first:
                        pool.wait_ge(y_made, t - 1)
                    pool.dma_start(res[:, s, :], residual[bass.ds(t * P, P), :]).then_inc(res_loaded[s], 16)

                pipeline(pool, (load_res, 0))


def batch_norm_layer_phase(nc, k, name, acc, table_in, w1, gamma1, beta1, w2, eps_weight, gamma_h, beta_h, norm_dram):
    NB = 512
    blocks = [(b, min(NB, NP - b)) for b in range(0, NP, NB)]
    stat_blocks = [(b, min(NB, N - b)) for b in range(0, N, NB)]
    with ExitStack() as ctx:
        m = Mem(nc, ctx, name)
        w_in_sb = m.sb("w_in_sb", [P, 2, 2, D])
        wT = m.sb("wT", [P, 2, 2, D])
        zT = m.sb("zT", [P, 2, NP])
        n_norm = m.sb("n_norm", [P, NP])
        xin = m.sb("xin", [P, 2, D])
        yin = m.sb("yin", [P, 2, D])
        yT = m.sb("yT", [P, 2, D])
        eps_w = m.sb("eps_w", [P, 1])
        cols = m.sb("cols", [P, 4, 2])
        stats = m.sb("stats", [P, 2, len(stat_blocks), 6])
        mv = m.sb("mv", [P, 2, 2])
        root = m.sb("root", [P, 2])
        scale = m.sb("scale", [P, 2])
        bias = m.sb("bias", [P, 2])
        eps = m.sb("eps", [P, 1])
        deg = m.sb("deg", [P, P])
        degT = m.sb("degT", [P, P])
        ps = [m.ps(f"ps{n}", [P, 512]) for n in range(6)]
        small_in, dv = m.sem("small_in"), m.sem("dve")
        deg_made, deg_root, deg_turned, degT_made, deg_stored, norm_in = (
            m.sem(n) for n in ("deg_made", "deg_root", "deg_turned", "degT_made", "deg_stored", "norm_in"))
        w_turned, wT_made = m.sem("w_turned"), m.sem("wT_made")
        loaded = [m.sem(f"loaded{s}") for s in range(2)]
        y_made, turned, yT_made, summed, z_made = (m.sem(n) for n in ("y_made", "turned", "yT_made", "summed", "z_made"))
        var_made, root_made, scale_made, relu_made = (m.sem(n) for n in ("var_made", "root_made", "scale_made", "relu_made"))
        summed2, z2_made = m.sem("summed2"), m.sem("z2_made")
        loaded2 = [m.sem(f"loaded2_{s}") for s in range(2)]
        doubled, turned2, done2 = m.sem("doubled"), m.sem("turned2"), m.sem("done2")
        block = ctx.enter_context(nc.Block())
        acc3 = acc.rearrange("p (t w) -> p t w", w=MSGW)

        @block.sync
        def _(sp):
            for n, w in enumerate((w1, w2)):
                for c in range(2):
                    sp.dma_start(w_in_sb[:, n, c, :], w[c * P:(c + 1) * P, :]).then_inc(small_in, 16)
            for n, v in enumerate((gamma1, beta1, gamma_h, beta_h)):
                sp.dma_start(cols[:, n, :], v.rearrange("(c p) -> p c", p=P),
                             allow_slow_non_contiguous=True).then_inc(small_in, 16)
            sp.dma_start(eps_w[:], eps_weight.partition_broadcast(P)).then_inc(small_in, 16)

            def load(t, s, first):
                if not first:
                    sp.wait_ge(y_made, t - 1)
                sp.dma_start(xin[:, s, :], table_in[bass.ds(t * P, P), :]).then_inc(loaded[s], 16)

            pipeline(sp, (load, 0))
            sp.wait_ge(degT_made, 1)
            sp.dma_start(norm_dram.rearrange("(t p) -> t p", p=P), degT[0:NTP, :]).then_inc(deg_stored, 16)
            sp.wait_ge(deg_stored, 16)
            sp.dma_start(n_norm[:], norm_dram.partition_broadcast(P)).then_inc(norm_in, 16)

            sp.wait_ge(y_made, NTP)

            def load2(t, s, first):
                if not first:
                    sp.wait_ge(done2, t - 1)
                sp.dma_start(xin[:, s, :], table_in[bass.ds(t * P, P), :]).then_inc(loaded2[s], 16)

            pipeline(sp, (load2, 0))

        @block.tensor
        def _(pe):
            pe.wait_ge(small_in, 144)
            for n in range(2):
                for c in range(2):
                    for o in range(2):
                        ins = pe.transpose(ps[n][:, (2 * c + o) * P:(2 * c + o + 1) * P],
                                           w_in_sb[:, n, o, c * P:(c + 1) * P], k.ident[:])
            ins.then_inc(w_turned, 1)
            pe.wait_ge(deg_root, 1)
            pe.transpose(ps[2][:, 0:P], deg[:], k.ident[:]).then_inc(deg_turned, 1)
            pe.wait_ge(wT_made, 1)
            pe.wait_ge(degT_made, 1)

            def turn(t, s, first):
                pe.wait_ge(y_made, t + 1)
                if not first:
                    pe.wait_ge(yT_made, t - 1)
                for c in range(2):
                    ins = pe.transpose(ps[s][:, c * P:(c + 1) * P], yin[:, s, c * P:(c + 1) * P], k.ident[:])
                ins.then_inc(turned, 1)

            def multiply(t, s, first):
                pe.wait_ge(yT_made, t + 1)
                if not first:
                    pe.wait_ge(z_made, t - 1)
                for o in range(2):
                    for c in range(2):
                        ins = pe.matmul(ps[2 + s][:, o * P:(o + 1) * P], wT[:, 0, c, o * P:(o + 1) * P],
                                        yT[:, s, c * P:(c + 1) * P], start=(c == 0), stop=(c == 1))
                ins.then_inc(summed, 1)

            pipeline(pe, (turn, 0), (multiply, 1))
            pe.wait_ge(z_made, NTP)
            pe.wait_ge(relu_made, 1)
            for n, (b, w) in enumerate(blocks):
                if n >= 2:
                    pe.wait_ge(z2_made, n - 1)
                for o in range(2):
                    for c in range(2):
                        ins = pe.matmul(ps[2 * (n % 2) + o][:, 0:w], wT[:, 1, c, o * P:(o + 1) * P],
                                        zT[:, c, b:b + w], start=(c == 0), stop=(c == 1))
                ins.then_inc(summed2, 1)
            pe.wait_ge(z2_made, len(blocks))
            pe.wait_ge(relu_made, 2)

            def back(t, s, first):
                pe.wait_ge(yT_made, t + NTP + 1)
                if not first:
                    pe.wait_ge(done2, t - 1)
                for c in range(2):
                    ins = pe.transpose(ps[s][:, c * P:(c + 1) * P], yT[:, s, c * P:(c + 1) * P], k.ident[:])
                ins.then_inc(turned2, 1)

            pipeline(pe, (back, 0))

        @block.scalar
        def _(act):
            act.wait_ge(deg_made, 1)
            act.activation(deg[:, 0:NTP], deg[:, 0:NTP], ACT.Sqrt).then_inc(deg_made, 1)

            def tile(t, s, first):
                act.wait_ge(turned, t + 1)
                if not first:
                    act.wait_ge(summed, t - 1)
                act.copy(yT[:, s, :], ps[s][:, 0:D]).then_inc(yT_made, 1)

            pipeline(act, (tile, 0))
            for n in range(2):
                act.wait_ge(var_made, n + 1)
                act.activation(root[:], mv[:, :, 1], ACT.Sqrt, bias=eps[:]).then_inc(root_made, 1)
                act.wait_ge(scale_made, n + 1)
                for o in range(2):
                    ins = act.activation(zT[:, o, :], zT[:, o, :], ACT.Relu, bias=bias[:, o:o + 1], scale=scale[:, o:o + 1])
                ins.then_inc(relu_made, 1)
            act.wait_ge(relu_made, 2)

            def out_tile(t, s, first):
                if first:
                    act.wait_ge(summed, NTP)
                else:
                    act.wait_ge(turned2, t - 1)
                act.copy(yT[:, s, :].rearrange("p (c n) -> p c n", c=2), zT[:, :, bass.ds(t * P, P)]).then_inc(yT_made, 1)

            pipeline(act, (out_tile, 0))

        @block.vector
        def _(dve):
            st = Steps(dve, dv)
            st(dve.memset(eps[:], EPS))
            st(dve.memset(deg[:], 1.0))
            dve.tensor_scalar(deg[:, 0:NTP], acc3[:, :, MSG_ONE], 1.0, None, op0=ALU.max).then_inc(deg_made, 1)
            dve.wait_ge(deg_made, 2)
            st(dve.reciprocal(deg[:, 0:NTP], deg[:, 0:NTP]))
            dve.sem_inc(deg_root, 1)
            dve.wait_ge(deg_turned, 1)
            dve.tensor_copy(degT[:], ps[2][:, 0:P]).then_inc(degT_made, 1)
            dve.wait_ge(w_turned, 1)
            for n in range(2):
                st(dve.tensor_copy(wT[:, n].rearrange("p c d -> p (c d)"), ps[n][:]))
            dve.sem_inc(wT_made, 1)
            dve.wait_ge(small_in, 144)

            def tile(t, s, first):
                dve.wait_ge(loaded[s], 16 if first else (t - s) * 8 + 16)
                if not first:
                    dve.wait_ge(turned, t - 1)
                dve.scalar_tensor_tensor(yin[:, s, :], xin[:, s, :], eps_w[:], acc[:, bass.ds(t * MSGW, D)],
                                         op0=ALU.mult, op1=ALU.add).then_inc(y_made, 1)

            def take(t, s, first):
                dve.wait_ge(summed, t + 1)
                dve.tensor_copy(zT[:, :, bass.ds(t * P, P)], ps[2 + s][:, 0:D].rearrange("p (c n) -> p c n", c=2)).then_inc(z_made, 1)

            pipeline(dve, (tile, 0), (take, 1))
            dve.wait_ge(z_made, NTP)

            def stat(n):
                for o in range(2):
                    for b, (at, w) in enumerate(stat_blocks):
                        ins = dve.bn_stats(stats[:, o, b, :], zT[:, o, at:at + w])
                    st(ins)
                    st(dve.bn_aggr(mv[:, o, :], stats[:, o].rearrange("p b s -> p (b s)")))
                dve.sem_inc(var_made, 1)
                dve.wait_ge(root_made, n + 1)
                st(dve.reciprocal(root[:], root[:]))
                st(dve.tensor_tensor(scale[:], root[:], cols[:, 2 * n, :], ALU.mult))
                st(dve.tensor_tensor(bias[:], mv[:, :, 0], scale[:], ALU.mult))
                st(dve.tensor_tensor(bias[:], cols[:, 2 * n + 1, :], bias[:], ALU.subtract))
                dve.sem_inc(scale_made, 1)

            stat(0)
            dve.wait_ge(norm_in, 16)
            dve.wait_ge(relu_made, 1)
            for n, (b, w) in enumerate(blocks):
                dve.wait_ge(summed2, n + 1)
                for o in range(2):
                    ins = dve.tensor_tensor(zT[:, o, b:b + w], ps[2 * (n % 2) + o][:, 0:w], n_norm[:, b:b + w], ALU.mult)
                ins.then_inc(z2_made, 1)
            dve.wait_ge(z2_made, len(blocks))
            stat(1)

            def out_tile(t, s, first):
                dve.wait_ge(turned2, t + 1)
                dve.wait_ge(loaded2[s], 16 if first else (t - s) * 8 + 16)
                dve.scalar_tensor_tensor(acc[:, bass.ds(t * MSGW, D)], xin[:, s, :], 2.0, ps[s][:, 0:D],
                                         op0=ALU.mult, op1=ALU.add).then_inc(done2, 1)

            pipeline(dve, (out_tile, 0))


class Shared:
    pass


def build_program(nc, a, out, upto=99, dbg=None):
    k = Shared()

    def dram(name, shape, dt=F32):
        return nc.dram_tensor(name, shape, dt).ap()

    table_x = dram("table_x", (NP, D))
    rec_hi = dram("rec_hi", (EP, RW))
    tile_dram = dram("tile_dram", (2, NCH), I32)
    codes_dram = dram("codes_dram", (2, EP), BF16)
    with ExitStack() as ctx:
        m = Mem(nc, ctx, "k")
        k.iota = m.sb("iota", [P, P])
        k.ident = m.sb("ident", [P, P])
        k.before = m.sb("before", [P, P])
        k.ones = m.sb("ones", [P, P])
        k.tile_off = m.sb("tile_off", [1, NCH], I32)
        k.tile_off_a = m.sb("tile_off_a", [1, NCH], I32)
        k.unsorted = m.sb("unsorted", [1, 1], I32)
        k.partition = m.sb("partition", [P, 1])
        with ExitStack() as sort_ctx:
            ms = Mem(nc, sort_ctx, "sort")
            k.rec = ms.sb("rec", [P, SC, RW])
            k.chunk_no = ms.sb("chunk_no", [P, NCH // P + 1])
            k.tile_of = ms.sb("tile_of", [P, NCH // P + 1])
            k.tile_off_i = ms.sb("tile_off_i", [P, 2, NCH // P + 1], I32)
            setup_phase(nc, k, a["src"], a["dst"], a["edge_weight"], a["edge_attr3_1x1"], a["x"], table_x)
            unsorted = nc.values_load(k.unsorted[0:1, 0:1], min_val=0, max_val=SP_)
            with nc.If(unsorted > 0):
                sort_phase(nc, k, "low", LOW, False, rec_hi[0:E, :], None)
            sort_phase(nc, k, "high", HIGH, True, rec_hi, tile_dram)
        k.src = m.sb("src", [P, NCH], I32)
        k.src_tile = m.sb("src_tile", [P, NCH], BF16)
        k.tiles = m.sb("tiles", [P, NT], BF16)
        k.local = m.sb("local", [P, NCH])
        k.weight = m.sb("weight", [P, NCH])
        k.dist = m.sb("dist", [P, NCH])
        k.breaks_in = m.sb("breaks_in", [1, P + 1])
        k.through_fwd = m.sb("through_fwd", [1, P])
        k.through_back = m.sb("through_back", [1, P])
        k.first_in_run = m.sb("first_in_run", [P, 1])
        k.att = m.sb("att", [P, NTP * 2 * H])
        k.numer = m.sb("numer", [P, H, NCH])
        k.first_max = m.sb("first_max", [P, H, NCH])
        flags_dram = dram("flags_dram", (P, RL + 1))
        edges_phase(nc, k, rec_hi, flags_dram)
        codes_phase(nc, k, rec_hi, codes_dram)
        tables = [dram(f"table_{n}", (NP, D)) for n in range(3)]
        table_h = dram("table_h", (NP, D))
        norm_dram = dram("norm_dram", (NP,))
        table_0, table_1, table_2 = tables

        def with_acc(name, body):
            with ExitStack() as ac:
                body(Mem(nc, ac, name).sb("acc", [P, NTP * MSGW])[:])

        def attention_layer(name, table_in, w, a_src, a_dst, bias, own, residual, table_out, normed_to, last=None):
            project_phase(nc, k, f"{name}p", table_in, w, a_src, a_dst, table_h)
            with ExitStack() as zc:
                mz = Mem(nc, zc, f"{name}z")
                z = mz.sb("z", [P, H, NCH])
                z_self = mz.sb("z_self", [P, H, NCH]) if own else None
                lookup_phase(nc, k, f"{name}l", codes_dram, z, z_self)
                softmax_phase(nc, k, f"{name}s", flags_dram, z, z_self, None if own else k.first_max)

            def rest(acc):
                aggregate_phase(nc, k, f"{name}a", table_h, acc, k.numer if own else k.first_max, True, True,
                                MSGW if own else MSG_M)
                attention_end_phase(nc, k, f"{name}e", acc, table_h, own, bias, residual, table_out)
                if residual is not None:
                    layernorm_phase(nc, k, f"{name}n", acc, normed_to, last)

            with_acc(name, rest)

        g0, g1, g2, g3 = ({n[7:]: v for n, v in a.items() if n.startswith(f"L{l}_gnn_")} for l in range(4))
        attention_layer("l0a", table_x, g0["W1"], g0["att_src1"], g0["att_dst1"], g0["b1"], True, None, table_0, None)
        if dbg and upto == 1: dbg(nc, k, locals()); return
        attention_layer("l0b", table_0, g0["W2"], g0["att_src2"], g0["att_dst2"], g0["b2"], True, table_x, None, table_1)
        if dbg and upto == 2: dbg(nc, k, locals()); return

        def conv(name, table_in, w_rel, w_root, bias, table_out, residual):
            def rest(acc):
                aggregate_phase(nc, k, f"{name}a", table_in, acc, None, False, False, D)
                graph_conv_phase(nc, k, f"{name}c", acc, table_in, w_rel, w_root, bias, table_out, residual)
                if residual is not None:
                    layernorm_phase(nc, k, f"{name}n", acc, table_0, None)

            with_acc(name, rest)

        conv("l1a", table_1, g1["W1_rel"], g1["W1_root"], g1["b1"], table_0, None)
        conv("l1b", table_0, g1["W2_rel"], g1["W2_root"], g1["b2"], table_2, None)
        conv("l1c", table_2, g1["W3_rel"], g1["W3_root"], g1["b3"], None, table_1)
        if dbg and upto == 3: dbg(nc, k, locals()); return

        def batch(acc):
            aggregate_phase(nc, k, "l2a", table_0, acc, k.weight, False, False, MSG_P)
            batch_norm_layer_phase(nc, k, "l2b", acc, table_0, g2["w1"], g2["gamma1"], g2["beta1"], g2["w2"],
                                   g2["eps_weight"], g2["gamma_h"], g2["beta_h"], norm_dram)
            layernorm_phase(nc, k, "l2n", acc, table_1, None)

        with_acc("l2", batch)
        if dbg and upto == 4: dbg(nc, k, locals()); return
        attention_layer("l3", table_1, g3["W"], g3["w_att_src"], g3["w_att_dst"], None, False, table_1, None, None, out)


def kernel(**inputs):
    import numpy as np
    import concourse.bacc as bacc
    from concourse.bass_utils import run_bass_kernel_spmd

    nc = bacc.Bacc("TRN2", target_bir_lowering=False, num_devices=1)
    arrays, args = {}, {}
    for name, value in inputs.items():
        arrays[name] = np.ascontiguousarray(value)
        args[name] = nc.dram_tensor(name, arrays[name].shape, mybir.dt.from_np(arrays[name].dtype),
                                    kind="ExternalInput").ap()
    out = nc.dram_tensor("out", (N, D), F32, kind="ExternalOutput").ap()
    build_program(nc, args, out)
    return run_bass_kernel_spmd(nc, [arrays], core_ids=[0]).results[0]["out"]
```

```python
from contextlib import ExitStack

import concourse.bass as bass
from concourse import mybir

P = 128
N = 6250
E = 100000
D = 256
H = 4
C = D // H
NT = -(-N // P)
NTP = NT + NT % 2
NP = NTP * P
SP_, SC = 125, 800
U = 8
SLOTS = 4
BY_GATHER = 2
FAR = 2.0 ** 100
NCH = -(-(E // P + 1 + NT) // (U * SLOTS)) * U * SLOTS
EP = NCH * P
RUN = NCH // 32
RL = RUN * P
LOW, HIGH = 128, NT
RW = 4
MSG_ONE = D
MSG_P = D + 1
MSG_M = D + 1 + H
MSGW = D + 1 + 2 * H
NEG = -1.0e30
NO_NODE = -1.0
SLOPE = 0.2
EPS = 1e-5

ALU = mybir.AluOpType
ACT = mybir.ActivationFunctionType
AX = mybir.AxisListType
F32 = mybir.dt.float32
BF16 = mybir.dt.bfloat16
U16 = mybir.dt.uint16
I32 = mybir.dt.int32
assert E == SP_ * SC and NCH % (U * SLOTS) == 0 and NCH * P >= E + NT * (P - 1)


class Steps:

    def __init__(self, eng, sem):
        self.eng, self.sem, self.n = eng, sem, 0

    def __call__(self, ins):
        ins.then_inc(self.sem, 1)
        self.n += 1
        self.eng.wait_ge(self.sem, self.n)


def repeat_inner(ap, n):
    return ap.unsqueeze(2).to_broadcast([ap.shape[0], ap.shape[1], n])


def by_chunk(heads):
    return heads[:].rearrange("p h c -> p c h")


def pipeline(eng, *parts, slots=2):
    lags = [lag for _, lag in parts]
    peel = -(-(max(lags) + slots) // slots) * slots

    def step(n, r):
        for body, lag in parts:
            if not isinstance(n, int):
                body(n - lag if lag else n, (r - lag) % slots, False)
            elif 0 <= n - lag < NTP:
                body(n - lag, (n - lag) % slots, n - lag < slots)

    for n in range(peel):
        step(n, n % slots)
    with eng.Fori(peel // slots, NTP // slots) as i:
        for r in range(slots):
            step(i * slots + r, r)
    for n in range(NTP // slots * slots, NTP + max(lags)):
        step(n, n % slots)


def before(t, n):
    return isinstance(t, int) and t < n


def repeat_outer(ap, n):
    return ap.unsqueeze(1).to_broadcast([ap.shape[0], n, ap.shape[1]])


class Mem:

    def __init__(self, nc, ctx, phase):
        self.nc, self.ctx, self.phase, self.sems = nc, ctx, phase, []

    def sb(self, name, shape, dt=F32):
        return self.ctx.enter_context(self.nc.sbuf_tensor(f"{self.phase}_{name}", shape, dt))

    def ps(self, name, shape, dt=F32):
        return self.ctx.enter_context(self.nc.psum_tensor(f"{self.phase}_{name}", shape, dt))

    def sem(self, name):
        if not self.sems:
            self.ctx.callback(self.clear)
        self.sems.append(self.nc.alloc_semaphore(f"{self.phase}_{name}"))
        return self.sems[-1]

    def clear(self):
        self.nc.clear_and_free_semaphores(self.sems)
        self.nc.all_engine_barrier()


def setup_phase(nc, k, src, dst, ew, dist, x, table_x):
    with ExitStack() as ctx:
        m = Mem(nc, ctx, "setup")
        ints = m.sb("edge_ints", [P, 2, SC], I32)
        fls = m.sb("edge_floats", [P, 2, SC], F32)
        zero = m.sb("zero_rows", [P, D])
        after = m.sb("after", [P, SC], I32)
        falls = m.sb("falls", [P, SC])
        fall = m.sb("fall", [P, 1])
        fall_ps = m.ps("fall_ps", [P, 512])
        const_all, fall_made, fall_summed = m.sem("const_all"), m.sem("fall_made"), m.sem("fall_summed")
        edges_in = m.sem("edges_in")
        const = m.sem("const_made")
        zero_made = m.sem("zero_made")
        after_set = m.sem("after_set")
        out_done = m.sem("setup_stored")
        dv = m.sem("setup_dve")
        block = ctx.enter_context(nc.Block())

        @block.sync
        def _(sp):
            for n, a in enumerate((src, dst)):
                sp.dma_start(ints[0:SP_, n, :], a.rearrange("(p s) -> p s", p=SP_)).then_inc(edges_in, 16)
            sp.dma_start(fls[0:SP_, 0, :], ew.rearrange("(p s) -> p s", p=SP_)).then_inc(edges_in, 16)
            sp.dma_start(fls[0:SP_, 1, :], dist.rearrange("(p s) a b -> p (s a b)", p=SP_)).then_inc(edges_in, 16)
            sp.wait_ge(after_set, 1)
            body = (SP_ - 1) * SC
            sp.dma_start(after[0:SP_ - 1, :], dst[1:1 + body].rearrange("(p s) -> p s", s=SC)).then_inc(edges_in, 16)
            sp.dma_start(after[SP_ - 1:SP_, 0:SC - 1], dst[1 + body:E].rearrange("(p s) -> p s", p=1)).then_inc(edges_in, 16)
            sp.dma_start(table_x[0:N, :], x).then_inc(out_done, 16)
            sp.wait_ge(zero_made, 1)
            sp.dma_start(table_x[N:N + 128, :], zero[:]).then_inc(out_done, 16)
            sp.dma_start(table_x[N + 128:NP, :], zero[0:NP - N - 128, :]).then_inc(out_done, 16)
            sp.wait_ge(out_done, 48)

        @block.gpsimd
        def _(pool):
            st = Steps(pool, const)
            pool.iota(k.chunk_no[:], [[P * P, NQ]], base=0, channel_multiplier=P,
                      allow_small_or_imprecise_dtypes=True)
            pool.iota(k.iota[:], [[1, P]], base=0, channel_multiplier=0,
                      allow_small_or_imprecise_dtypes=True)
            st(pool.memset(k.ident[:], 0.0))
            st(pool.affine_select(out=k.ident[:], in_=k.ident[:], compare_op=ALU.not_equal, fill=1.0,
                                  base=0, pattern=[[-1, P]], channel_multiplier=1))
            pool.iota(k.partition[:], [[0, 1]], base=0, channel_multiplier=1,
                      allow_small_or_imprecise_dtypes=True)
            st(pool.memset(k.before[:], 1.0))
            st(pool.affine_select(out=k.before[:], in_=k.before[:], compare_op=ALU.is_ge, fill=0.0,
                                  base=-1, pattern=[[1, P]], channel_multiplier=-1))
            pool.memset(k.ones[:], 1.0).then_inc(const_all, 1)

        @block.vector
        def _(dve):
            st = Steps(dve, dv)
            dve.memset(after[:], NP).then_inc(after_set, 1)
            dve.memset(zero[:], 0.0).then_inc(zero_made, 1)
            dve.wait_ge(edges_in, 96)
            st(dve.tensor_tensor(falls[0:SP_], ints[0:SP_, 1, :], after[0:SP_], ALU.is_gt))
            dve.tensor_reduce(fall[0:SP_], falls[0:SP_], AX.X, ALU.max).then_inc(fall_made, 1)
            dve.wait_ge(fall_summed, 1)
            dve.tensor_copy(k.unsorted[:], fall_ps[0:1, 0:1])
            dve.tensor_copy(k.rec[0:SP_, :, 0], ints[0:SP_, 0, :])
            dve.tensor_copy(k.rec[0:SP_, :, 1], ints[0:SP_, 1, :])
            dve.tensor_copy(k.rec[0:SP_, :, 2], fls[0:SP_, 0, :])
            dve.tensor_copy(k.rec[0:SP_, :, 3], fls[0:SP_, 1, :])

        @block.tensor
        def _(pe):
            pe.wait_ge(const_all, 1)
            pe.wait_ge(fall_made, 1)
            pe.matmul(fall_ps[0:1, 0:1], fall[0:SP_], k.ones[0:SP_, 0:1], start=True, stop=True).then_inc(fall_summed, 1)


NQ = NCH // P + 1


def tiles_of_chunks(dve, st, k, ends, chunk_at):
    st(dve.tensor_tensor(chunk_at[:], repeat_inner(k.chunk_no[:], NT), repeat_outer(ends[:, 0:NT], NQ), ALU.is_ge))
    st(dve.tensor_reduce(k.tile_of[:], chunk_at[:], AX.X, ALU.add))
    st(dve.tensor_scalar(k.tile_of[:], k.tile_of[:], float(NT - 1), None, op0=ALU.min))
    for n, step in enumerate((MSGW, 3 * 2 * H)):
        st(dve.tensor_scalar(chunk_at[:, :, 0], k.tile_of[:], float(step), None, op0=ALU.mult))
        st(dve.tensor_copy(k.tile_off_i[:, n, :], chunk_at[:, :, 0]))


def place_sorted_phase(nc, k, rec_in, rec_to):
    with ExitStack() as ctx:
        m = Mem(nc, ctx, "place")
        key = m.sb("key", [P, SC])
        key_i = m.sb("key_i", [P, SC], I32)
        tile_i = m.sb("tile_i", [P, SC], I32)
        mask = m.sb("mask", [P, 2, SC], BF16)
        one_row = m.sb("one_row", [P, NT])
        totals = m.sb("totals", [P, NT])
        size = m.sb("size", [P, NT])
        size_i = m.sb("size_i", [P, NT], I32)
        real_end = m.sb("real_end", [P, NT])
        ends = m.sb("ends", [P, NT])
        shift = m.sb("shift", [P, NT])
        chunk_at = m.sb("chunk_at", [P, NQ, NT])
        picked = m.sb("picked", [P, NQ, NT])
        off = m.sb("off", [P, NQ])
        left = m.sb("left", [P, NQ])
        off_i = m.sb("off_i", [P, NQ], I32)
        zero = m.sb("zero", [P, RW])
        rec = m.sb("rec", [P, NQ, P, RW])
        valid = m.sb("valid", [P, NQ, P])
        total_ps = m.ps("total_ps", [P, 512])
        dv, counted, masked = m.sem("dve"), m.sem("counted"), m.sem("masked")
        zero_made, rec_stored, totals_made, totals_summed = (
            m.sem(n) for n in ("zero_made", "rec_stored", "totals_made", "totals_summed"))
        off_made = m.sem("off_made")
        rec_loaded, struck, stored = m.sem("rec_loaded"), m.sem("struck"), m.sem("stored")
        block = ctx.enter_context(nc.Block())
        S = slice(0, SP_)
        nf, rest = NCH // P, NCH % P

        @block.sync
        def _(sp):
            sp.dma_start(rec_in[0:E].rearrange("(p s) w -> p (s w)", p=SP_),
                         k.rec[S].rearrange("p a b -> p (a b)")).then_inc(rec_stored, 16)
            sp.wait_ge(zero_made, 1)
            sp.dma_start(rec_in[E:E + P], zero[:]).then_inc(rec_stored, 16)
            sp.wait_ge(struck, 2)
            by_rows = rec_to.rearrange("(c e) w -> c (e w)", e=P)
            sp.dma_start(by_rows[0:nf * P].rearrange("(q p) x -> p q x", p=P),
                         rec[:, 0:nf].rearrange("p q e w -> p q (e w)")).then_inc(stored, 16)
            sp.dma_start(by_rows[nf * P:NCH], rec[0:rest, nf].rearrange("p e w -> p (e w)")).then_inc(stored, 16)
            sp.wait_ge(stored, 32)

        @block.gpsimd
        def _(pool):
            pool.wait_ge(rec_stored, 32)
            pool.wait_ge(off_made, 1)
            for q in range(NQ):
                pool.indirect_dma_start(
                    out=rec[:, q].rearrange("p e w -> p (e w)"), out_offset=None, in_=rec_in,
                    in_offset=bass.IndirectOffsetOnAxis(ap=off_i[:, q:q + 1], axis=0)).then_inc(rec_loaded, 16)

        @block.tensor
        def _(pe):
            pe.wait_ge(totals_made, 1)
            pe.matmul(total_ps[:, 0:NT], k.ones[S, :], totals[S, :], start=True, stop=True).then_inc(totals_summed, 1)

        @block.vector
        def _(dve):
            st = Steps(dve, dv)
            dve.memset(zero[:], 0.0).then_inc(zero_made, 1)
            st(dve.memset(one_row[:], 1.0))
            st(dve.tensor_copy(key_i[S], k.rec[S, :, 1]))
            st(dve.tensor_scalar(tile_i[S], key_i[S], 7, None, op0=ALU.arith_shift_right))
            st(dve.tensor_copy(key[S], tile_i[S]))

            def find(t, s):
                dve.tensor_scalar(mask[S, s], key[S], k.iota[S, bass.ds(t, 1)], None, op0=ALU.is_equal).then_inc(masked, 1)

            def count(t, s):
                dve.wait_ge(masked, t + 1)
                dve.tensor_reduce(totals[S, bass.ds(t, 1)], mask[S, s], AX.X, ALU.add).then_inc(counted, 1)

            find(0, 0)
            find(1, 1)
            with dve.Fori(0, (NT - 1) // 2 - 1) as i:
                for s in range(2):
                    count(i * 2 + s, s)
                    dve.wait_ge(counted, i * 2 + s + 1)
                    find(i * 2 + s + 2, s)
            count(NT - 3, 0)
            dve.wait_ge(counted, NT - 2)
            find(NT - 1, 0)
            count(NT - 2, 1)
            count(NT - 1, 0)
            dve.wait_ge(counted, NT)
            dve.sem_inc(totals_made, 1)
            dve.wait_ge(totals_summed, 1)
            st(dve.tensor_copy(totals[:], total_ps[:, 0:NT]))
            st(dve.tensor_scalar(size[:], totals[:], float(P - 1), None, op0=ALU.add))
            st(dve.tensor_copy(size_i[:], size[:]))
            st(dve.tensor_scalar(size_i[:], size_i[:], -P, None, op0=ALU.bitwise_and))
            st(dve.tensor_copy(size[:], size_i[:]))
            st(dve.tensor_tensor_scan(ends[:], one_row[:], size[:], 0.0, op0=ALU.mult, op1=ALU.add))
            st(dve.tensor_tensor_scan(real_end[:], one_row[:], totals[:], 0.0, op0=ALU.mult, op1=ALU.add))
            tiles_of_chunks(dve, st, k, ends, chunk_at)
            st(dve.tensor_tensor(shift[:], real_end[:], totals[:], ALU.subtract))
            st(dve.tensor_tensor(shift[:], shift[:], ends[:], ALU.subtract))
            st(dve.tensor_tensor(shift[:], shift[:], size[:], ALU.add))
            st(dve.tensor_tensor(chunk_at[:], repeat_inner(k.tile_of[:], NT), repeat_outer(k.iota[:, 0:NT], NQ), ALU.is_equal))
            for of_tile, of_chunk in ((shift, off), (real_end, left)):
                st(dve.tensor_tensor(picked[:], chunk_at[:], repeat_outer(of_tile[:], NQ), ALU.mult))
                st(dve.tensor_reduce(of_chunk[:], picked[:], AX.X, ALU.add))
            st(dve.tensor_tensor(off[:], off[:], k.chunk_no[:], ALU.add))
            st(dve.tensor_scalar(off[:], off[:], float(E), None, op0=ALU.min))
            st(dve.tensor_tensor(left[:], left[:], off[:], ALU.subtract))
            dve.tensor_copy(off_i[:], off[:]).then_inc(off_made, 1)
            dve.wait_ge(rec_loaded, 16 * NQ)
            for rows, qs in ((slice(0, P), slice(0, nf)), (slice(0, rest), slice(nf, NQ))):
                n = qs.stop - qs.start
                here = rec[rows, qs]
                st(dve.tensor_tensor(valid[rows, qs], repeat_outer(k.iota[rows, :], n), repeat_inner(left[rows, qs], P), ALU.is_lt))
                st(dve.tensor_scalar(here[:, :, :, 1], here[:, :, :, 1], -NO_NODE, None, op0=ALU.add))
                for w in range(RW):
                    st(dve.tensor_tensor(here[:, :, :, w], here[:, :, :, w], valid[rows, qs], ALU.mult))
                dve.tensor_scalar(here[:, :, :, 1], here[:, :, :, 1], NO_NODE, None, op0=ALU.add).then_inc(struck, 1)


def store_chunk_tiles_phase(nc, k, tile_dram):
    with ExitStack() as ctx:
        m = Mem(nc, ctx, "chunks")
        stored = m.sem("tile_offsets_stored")
        block = ctx.enter_context(nc.Block())
        nf = NCH // P

        @block.sync
        def _(sp):
            for n in range(2):
                sp.dma_start(tile_dram[n, 0:nf * P].rearrange("(q p) -> p q", p=P), k.tile_off_i[:, n, 0:nf],
                             allow_slow_non_contiguous=True).then_inc(stored, 16)
                sp.dma_start(tile_dram[n, nf * P:NCH].rearrange("(p q) -> p q", q=1),
                             k.tile_off_i[0:NCH - nf * P, n, nf:nf + 1]).then_inc(stored, 16)
            sp.wait_ge(stored, 64)
            for n, row in enumerate((k.tile_off, k.tile_off_a)):
                sp.dma_start(row[0:1, :], tile_dram[n:n + 1, :]).then_inc(stored, 16)
            sp.wait_ge(stored, 96)


def sort_phase(nc, k, name, buckets, high, rec_to):
    CB = 8
    with ExitStack() as ctx:
        m = Mem(nc, ctx, name)
        key = m.sb("key", [P, SC])
        key_i = m.sb("key_i", [P, SC], I32)
        rank = m.sb("rank", [P, SC])
        pos = m.sb("pos", [P, SC], I32)
        mask = m.sb("mask", [P, SC], BF16)
        count = m.sb("count", [P, SC])
        one_row = m.sb("one_row", [P, SC])
        totals = m.sb("totals", [P, P])
        start = m.sb("start", [P, P])
        size = m.sb("size", [P, P])
        size_i = m.sb("size_i", [P, P], I32)
        base = m.sb("base", [P, P])
        pos_ring = m.sb("pos_ring", [P, 2, CB], I32)
        rec_ring = m.sb("rec_ring", [P, 2, CB, RW])
        chunk_at = m.sb("chunk_at", [P, NQ, NT]) if high else None
        pads = m.sb("pad_records", [P, NCH, RW]) if high else None
        pads_made, pads_stored = m.sem("pads_made"), m.sem("pads_stored")
        before_ps = m.ps("before_ps", [P, 512])
        total_ps = m.ps("total_ps", [P, 512])
        dv = m.sem(f"dve")
        in_loop = m.sem(f"bucket_steps")
        in_loop2 = m.sem(f"base_steps")
        totals_made = m.sem(f"totals")
        base_ps_made = m.sem(f"base_ps")
        pos_made = m.sem(f"pos")
        ring_full = m.sem(f"ring_full")
        scattered = [m.sem(f"scattered{s}") for s in range(2)]
        turn = m.sem("scatter_turn")
        block = ctx.enter_context(nc.Block())
        S = slice(0, SP_)

        @block.sync
        def _(sp):
            if high:
                sp.wait_ge(pads_made, 1)
                sp.dma_start(rec_to.rearrange("(p q) w -> p (q w)", p=P),
                             pads[:].rearrange("p a b -> p (a b)")).then_inc(pads_stored, 16)

        @block.vector
        def _(dve):
            st = Steps(dve, dv)
            if high:
                st(dve.memset(pads[:], 0.0))
                dve.memset(pads[:, :, 1], NO_NODE).then_inc(pads_made, 1)
            st(dve.tensor_copy(key_i[S], k.rec[S, :, 1]))
            if high:
                st(dve.tensor_scalar(pos[S], key_i[S], 7, None, op0=ALU.arith_shift_right))
            else:
                st(dve.tensor_scalar(pos[S], key_i[S], LOW - 1, None, op0=ALU.bitwise_and))
            st(dve.tensor_copy(key[S], pos[S]))
            st(dve.memset(rank[:], 0.0))
            st(dve.memset(one_row[:], 1.0))
            st(dve.memset(totals[:], 0.0))
            with dve.Fori(0, buckets) as b:
                dve.tensor_scalar(mask[S], key[S], k.iota[S, bass.ds(b, 1)], None,
                                  op0=ALU.is_equal).then_inc(in_loop, 1)
                dve.wait_ge(in_loop, b * 4 + 1)
                dve.tensor_tensor_scan(count[S], one_row[S], mask[S], 0.0,
                                       op0=ALU.mult, op1=ALU.add).then_inc(in_loop, 1)
                dve.wait_ge(in_loop, b * 4 + 2)
                dve.tensor_copy(totals[S, bass.ds(b, 1)], count[S, SC - 1:SC]).then_inc(in_loop, 1)
                dve.copy_predicated(rank[S], mask[S].bitcast(U16), count[S]).then_inc(in_loop, 1)
                dve.wait_ge(in_loop, b * 4 + 4)
            dve.sem_inc(totals_made, 1)
            dve.wait_ge(base_ps_made, 1)
            st(dve.tensor_copy(size[:, 0:buckets], total_ps[:, 0:buckets]))
            if high:
                st(dve.tensor_scalar(size[:, 0:buckets], size[:, 0:buckets], float(P - 1), None, op0=ALU.add))
                st(dve.tensor_copy(size_i[:, 0:buckets], size[:, 0:buckets]))
                st(dve.tensor_scalar(size_i[:, 0:buckets], size_i[:, 0:buckets], -P, None, op0=ALU.bitwise_and))
                st(dve.tensor_copy(size[:, 0:buckets], size_i[:, 0:buckets]))
            st(dve.tensor_tensor_scan(start[:, 0:buckets], one_row[:, 0:buckets], size[:, 0:buckets], 0.0,
                                      op0=ALU.mult, op1=ALU.add))
            if high:
                tiles_of_chunks(dve, st, k, start, chunk_at)
            st(dve.tensor_tensor(start[:, 0:buckets], start[:, 0:buckets], size[:, 0:buckets], ALU.subtract))
            st(dve.tensor_tensor(base[:, 0:buckets], before_ps[:, 0:buckets], start[:, 0:buckets], ALU.add))
            with dve.Fori(0, buckets) as b:
                dve.tensor_scalar(count[S], key[S], k.iota[S, bass.ds(b, 1)], base[S, bass.ds(b, 1)],
                                  op0=ALU.is_equal, op1=ALU.mult).then_inc(in_loop2, 1)
                dve.wait_ge(in_loop2, b * 2 + 1)
                dve.tensor_tensor(rank[S], rank[S], count[S], ALU.add).then_inc(in_loop2, 1)
                dve.wait_ge(in_loop2, b * 2 + 2)
            st(dve.tensor_scalar(rank[S], rank[S], -1.0, None, op0=ALU.add))
            dve.tensor_copy(pos[S], rank[S]).then_inc(pos_made, 1)

        @block.tensor
        def _(pe):
            pe.wait_ge(totals_made, 1)
            pe.matmul(before_ps[:, 0:buckets], k.before[S, :], totals[S, 0:buckets], start=True, stop=True)
            pe.matmul(total_ps[:, 0:buckets], k.ones[S, :], totals[S, 0:buckets], start=True,
                      stop=True).then_inc(base_ps_made, 1)

        @block.scalar
        def _(act):
            def fill(s, at):
                act.copy(pos_ring[S, s, :], pos[S, bass.ds(at, CB)])
                act.copy(rec_ring[S, s].rearrange("p a b -> p (a b)"),
                         k.rec[S].rearrange("p a b -> p (a b)")[:, bass.ds(at * RW, CB * RW)]).then_inc(ring_full, 1)

            act.wait_ge(pos_made, 1)
            for s in range(2):
                fill(s, s * CB)
            with act.Fori(1, SC // CB // 2) as i:
                for s in range(2):
                    act.wait_ge(scattered[s], i * (16 * CB))
                    fill(s, (i * 2 + s) * CB)

        @block.gpsimd
        def _(pool):
            if high:
                pool.wait_ge(pads_stored, 16)
            with pool.Fori(0, SC // CB // 2) as i:
                for s in range(2):
                    pool.wait_ge(ring_full, i * 2 + s + 1)
                    pool.sem_inc(turn, 1)
                    for c in range(CB):
                        pool.indirect_dma_start(
                            out=rec_to, out_offset=bass.IndirectOffsetOnAxis(ap=pos_ring[S, s, c:c + 1], axis=0),
                            in_=rec_ring[S, s, c, :], in_offset=None).then_inc(scattered[s], 16)
            for s in range(2):
                pool.wait_ge(scattered[s], SC // 2 * 16)
    if not high:
        with ExitStack() as ctx:
            loaded = Mem(nc, ctx, "resorted").sem("loaded")
            block = ctx.enter_context(nc.Block())

            @block.sync
            def _(sp):
                sp.dma_start(k.rec[0:SP_].rearrange("p a b -> p (a b)"),
                             rec_to.rearrange("(p s) w -> p (s w)", p=SP_)).then_inc(loaded, 16)
                sp.wait_ge(loaded, 16)


def edges_phase(nc, k, rec_hi, rec_rows, flags_dram):
    with ExitStack() as ctx:
        m = Mem(nc, ctx, "edges")
        rec = m.sb("rec", [P, RW, NCH])
        dst_i = m.sb("dst_i", [P, NCH], I32)
        low_i = m.sb("low_i", [P, NCH], I32)
        none = m.sb("none", [P, NCH])
        dst4 = m.sb("dst4", [P, H, NCH])
        dst_scan = m.sb("dst_scan", [P, RL])
        breaks = m.sb("breaks", [P, RL + 1])
        ends = m.sb("ends", [P, 4])
        row = m.sb("row", [1, 3, P])
        tp = [m.ps(f"tp{n}", [P, P]) for n in range(2)]
        rows_ps = m.ps("rows_ps", [P, 512])
        rec_ps = [m.ps(f"rec_ps{n}", [P, RW, P]) for n in range(2)]
        loaded, dv, stored = m.sem("loaded"), m.sem("dve"), m.sem("stored")
        rec_turned, rec_made = m.sem("rec_turned"), m.sem("rec_made")
        dst4_made, turned, taken = m.sem("dst4_made"), m.sem("turned"), m.sem("taken")
        ends_made, rows_made = m.sem("ends_made"), m.sem("rows_made")
        first_made, first_turned = m.sem("first_made"), m.sem("first_turned")
        breaks_made = m.sem("breaks_made")
        block = ctx.enter_context(nc.Block())
        nf, rest = NCH // P, NCH % P
        columns = [(q, P) for q in range(nf)] + [(nf, rest)] * (rest > 0)

        @block.sync
        def _(sp):
            by_rows = rec_hi.rearrange("(c e) w -> c (e w)", e=P)
            sp.dma_start(rec_rows[:, 0:nf].rearrange("p q e w -> p q (e w)"),
                         by_rows[0:nf * P].rearrange("(q p) x -> p q x", p=P)).then_inc(loaded, 16)
            sp.dma_start(rec_rows[0:rest, nf].rearrange("p e w -> p (e w)"), by_rows[nf * P:NCH]).then_inc(loaded, 16)
            sp.wait_ge(breaks_made, 1)
            sp.dma_start(flags_dram, breaks[:]).then_inc(stored, 16)
            sp.wait_ge(stored, 16)

        @block.vector
        def _(dve):
            st = Steps(dve, dv)
            for q, n in columns:
                dve.wait_ge(rec_turned, q + 1)
                dve.tensor_copy(rec[:, :, q * P:q * P + n], rec_ps[q % 2][:, :, 0:n]).then_inc(rec_made, 1)
            dve.wait_ge(rec_made, len(columns))
            dve.tensor_copy(dst4[:], repeat_outer(rec[:, 1, :], H)).then_inc(dst4_made, 1)
            st(dve.tensor_copy(k.src[:], rec[:, 0, :]))
            st(dve.tensor_scalar(low_i[:], k.src[:], 7, None, op0=ALU.arith_shift_right))
            st(dve.tensor_copy(none[:], low_i[:]))
            st(dve.tensor_scalar(low_i[:], k.src[:], P - 1, None, op0=ALU.bitwise_and))
            st(dve.tensor_copy(k.weight[:], low_i[:]))
            st(dve.scalar_tensor_tensor(none[:], k.weight[:], float(NTP), none[:], op0=ALU.mult, op1=ALU.add))
            st(dve.tensor_copy(k.att_row[:], none[:]))
            st(dve.tensor_copy(k.weight[:], rec[:, 2, :]))
            st(dve.tensor_copy(k.dist[:], rec[:, 3, :]))
            st(dve.tensor_scalar(none[:], rec[:, 1, :], 0.0, float(8 * P), op0=ALU.is_lt, op1=ALU.mult))
            st(dve.tensor_scalar(k.local[:], rec[:, 1, :], 0.0, None, op0=ALU.max))
            st(dve.tensor_copy(dst_i[:], k.local[:]))
            st(dve.tensor_scalar(low_i[:], dst_i[:], P - 1, None, op0=ALU.bitwise_and))
            st(dve.tensor_copy(k.local[:], low_i[:]))
            st(dve.tensor_tensor(k.local[:], k.local[:], none[:], ALU.add))
            for c in range(RUN):
                dve.wait_ge(turned, c + 1)
                dve.tensor_copy(dst_scan[:, c * P:(c + 1) * P], tp[c % 2][:]).then_inc(taken, 1)
            dve.wait_ge(taken, RUN)
            st(dve.memset(breaks[:], 0.0))
            st(dve.tensor_tensor(breaks[:, 1:RL], dst_scan[:, 1:RL], dst_scan[:, 0:RL - 1], ALU.not_equal))
            st(dve.tensor_reduce(ends[:, 2:3], breaks[:], AX.X, ALU.max))
            st(dve.tensor_scalar(breaks[:], breaks[:], NEG, None, op0=ALU.mult))
            dve.sem_inc(breaks_made, 1)
            st(dve.tensor_copy(ends[:, 0:1], dst_scan[:, 0:1]))
            st(dve.tensor_copy(ends[:, 1:2], dst_scan[:, RL - 1:RL]))
            dve.sem_inc(ends_made, 1)
            dve.wait_ge(rows_made, 1)
            st(dve.tensor_copy(row[0:1].rearrange("a b c -> a (b c)"), rows_ps[0:1, 0:3 * P]))
            st(dve.memset(k.breaks_in[:], 1.0))
            for h in range(H):
                st(dve.tensor_tensor(k.breaks_in[0:1, 32 * h + 1:32 * h + 32], row[0:1, 0, 32 * h + 1:32 * h + 32],
                                     row[0:1, 1, 32 * h:32 * h + 31], ALU.not_equal))
            st(dve.tensor_tensor(k.through_fwd[:], k.breaks_in[0:1, 0:P], row[0:1, 2, :], ALU.max))
            st(dve.tensor_tensor(k.through_back[:], k.breaks_in[0:1, 1:P + 1], row[0:1, 2, :], ALU.max))
            st(dve.tensor_copy(row[0:1, 0, :], k.breaks_in[0:1, 0:P]))
            dve.sem_inc(first_made, 1)
            st(dve.tensor_scalar(k.through_fwd[:], k.through_fwd[:], NEG, None, op0=ALU.mult))
            st(dve.tensor_scalar(k.through_back[:], k.through_back[:], NEG, None, op0=ALU.mult))
            st(dve.tensor_scalar(k.breaks_in[:], k.breaks_in[:], NEG, None, op0=ALU.mult))
            dve.wait_ge(first_turned, 1)
            st(dve.tensor_copy(k.first_in_run[:], rows_ps[:, 384:385]))

        @block.tensor
        def _(pe):
            pe.wait_ge(loaded, 32)
            for q, n in columns:
                if q >= 2:
                    pe.wait_ge(rec_made, q - 1)
                for w in range(RW):
                    ins = pe.transpose(rec_ps[q % 2][:, w, 0:n], rec_rows[0:n, q, :, w], k.ident[0:n, 0:n])
                ins.then_inc(rec_turned, 1)
            pe.wait_ge(dst4_made, 1)
            by_run = dst4[:].rearrange("p h (r c) -> p c (h r)", c=RUN)
            for c in range(RUN):
                if c >= 2:
                    pe.wait_ge(taken, c - 1)
                pe.transpose(tp[c % 2][:], by_run[:, c], k.ident[:]).then_inc(turned, 1)
            pe.wait_ge(ends_made, 1)
            for n in range(3):
                ins = pe.transpose(rows_ps[0:1, n * P:(n + 1) * P], ends[:, n:n + 1], k.ident[:])
            ins.then_inc(rows_made, 1)
            pe.wait_ge(first_made, 1)
            pe.transpose(rows_ps[:, 384:385], row[0:1, 0, :], k.ident[0:1, 0:1]).then_inc(first_turned, 1)


def codes_phase(nc, k, rec, codes_dram):
    nf, rest = NCH // P, NCH % P
    with ExitStack() as ctx:
        m = Mem(nc, ctx, "codes")
        ints = m.sb("ints", [P, 2, nf + 1, P], I32)
        low = m.sb("low", [P, 2, nf + 1, P], I32)
        none = m.sb("none", [P, nf + 1, P])
        codes = m.sb("codes", [P, 3, nf + 1, P], BF16)
        dv, made, stored = m.sem("dve"), m.sem("made"), m.sem("stored")
        block = ctx.enter_context(nc.Block())

        @block.sync
        def _(sp):
            sp.wait_ge(made, 1)
            for n in range(3):
                row = codes_dram[n].rearrange("(c e) -> c e", e=P)
                sp.dma_start(row[0:nf * P].rearrange("(q p) e -> p q e", p=P), codes[:, n, 0:nf]).then_inc(stored, 16)
                sp.dma_start(row[nf * P:NCH], codes[0:rest, n, nf]).then_inc(stored, 16)
            sp.wait_ge(stored, 96)

        @block.vector
        def _(dve):
            st = Steps(dve, dv)
            for rows, qs in ((slice(0, P), slice(0, nf)), (slice(0, rest), slice(nf, nf + 1))):
                at = (rows, qs)
                st(dve.tensor_scalar(none[at], rec[rows, qs, :, 1], 0.0, float(8 * P), op0=ALU.is_lt, op1=ALU.mult))
                for n in range(2):
                    st(dve.tensor_scalar(rec[rows, qs, :, n], rec[rows, qs, :, n], 0.0, None, op0=ALU.max))
                    st(dve.tensor_copy(ints[rows, n, qs], rec[rows, qs, :, n]))
                    st(dve.tensor_scalar(low[rows, n, qs], ints[rows, n, qs], P - 1, None, op0=ALU.bitwise_and))
                st(dve.tensor_tensor(codes[rows, 0, qs], low[rows, 1, qs], none[at], ALU.add))
                st(dve.tensor_copy(codes[rows, 1, qs], low[rows, 0, qs]))
                st(dve.tensor_scalar(ints[rows, 0, qs], ints[rows, 0, qs], 7, None, op0=ALU.arith_shift_right))
                st(dve.tensor_copy(codes[rows, 2, qs], ints[rows, 0, qs]))
            dve.sem_inc(made, 1)


class Ring:

    def __init__(self, m):
        self.messages = m.sb("messages", [P, SLOTS, U, MSGW])
        self.index = m.sb("index", [P, SLOTS, U], I32)
        self.gathered = [m.sem(f"gathered{s}") for s in range(SLOTS)]

    def gather(self, pool, table, s):
        for j in range(U):
            pool.indirect_dma_start(
                out=self.messages[:, s, j, 0:D], out_offset=None, in_=table,
                in_offset=bass.IndirectOffsetOnAxis(ap=self.index[:, s, j:j + 1], axis=0),
            ).then_inc(self.gathered[s], 16)


def aggregate_phase(nc, k, name, table, acc, scale, head_scale, softmax, width, started=None):
    with ExitStack() as ctx:
        m = Mem(nc, ctx, name)
        slots = started or Ring(m)
        ring, index, gathered = slots.messages, slots.index, slots.gathered
        member = m.sb("member", [P, 2, U, P])
        sums = [m.ps(f"sums{j}", [P, 512]) for j in range(U)]
        turn = m.sem("gather_turn")
        index_ready = m.sem("index_ready")
        set_up = m.sem("set_up")
        prepared = m.sem("prepared")
        member_made = m.sem("member_made")
        chunk_summed = m.sem("chunk_summed")
        chunk_added = m.sem("chunk_added")
        half_cleared = m.sem("half_cleared")
        block = ctx.enter_context(nc.Block())
        half = NTP * MSGW // 2
        assert head_scale == (started is not None)
        units = NCH // U

        @block.gpsimd
        def _(pool):
            if started:
                pool.memset(acc[:, half:], 0.0).then_inc(half_cleared, 1)
            with pool.Fori(1 if started else 0, units // SLOTS) as i:
                for s in range(SLOTS):
                    pool.wait_ge(index_ready, i * SLOTS + s + 1)
                    pool.sem_inc(turn, 1)
                    slots.gather(pool, table, s)

        @block.scalar
        def _(act):
            def fill(s, u, index_too):
                if softmax:
                    ins = act.copy(ring[:, s, :, MSG_P:MSG_P + H],
                                   by_chunk(k.numer)[:, bass.ds(u * U, U), :])
                if width > MSG_M:
                    ins = act.copy(ring[:, s, :, MSG_M:MSG_M + H],
                                   by_chunk(k.first_max)[:, bass.ds(u * U, U), :])
                if index_too:
                    ins = act.copy(index[:, s, :], k.src[:, bass.ds(u * U, U)])
                ins.then_inc(index_ready, 1)

            act.wait_ge(set_up, 1)
            for s in range(SLOTS):
                fill(s, s, not started)
            with act.Fori(1, units // SLOTS) as i:
                for s in range(SLOTS):
                    act.wait_ge(chunk_summed, i * (SLOTS * U) + (s + 1 - SLOTS) * U)
                    fill(s, i * SLOTS + s, True)

        @block.vector
        def _(dve):
            def begin(i, s):
                u = i * SLOTS + s
                dve.wait_ge(index_ready, u + 1)
                dve.tensor_tensor(member[:, s % 2], repeat_outer(k.iota[:], U),
                                  repeat_inner(k.local[:, bass.ds(u * U, U)], P), ALU.is_equal).then_inc(member_made, 1)

            def take(i, s):
                dve.wait_ge(gathered[s], i * (16 * U) + 16 * U)
                msgs = ring[:, s, :, 0:D]
                if scale is None:
                    dve.sem_inc(prepared, 1)
                elif not head_scale:
                    u = i * SLOTS + s
                    dve.tensor_tensor(msgs, msgs, repeat_inner(scale[:, bass.ds(u * U, U)], D),
                                      ALU.mult).then_inc(prepared, 1)

            def scale_heads(i, s, j):
                mj = ring[:, s, j, 0:D].rearrange("p (h f) -> p h f", h=H)
                dve.tensor_tensor(mj, mj, repeat_inner(by_chunk(scale)[:, (i * SLOTS + s) * U + j, :], C),
                                  ALU.mult).then_inc(prepared, 1)

            def add(i, s, following):
                u = i * SLOTS + s
                offs = nc.values_load_multi_w_load_instructions(
                    k.tile_off[0:1, bass.ds(u * U, U)], engines=(mybir.EngineType.DVE,),
                    min_val=0, max_val=(NT - 1) * MSGW, skip_runtime_bounds_check_because="made so")[1]
                for j in range(U):
                    dve.wait_ge(chunk_summed, u * U + (j + 1))
                    dve.wait_ge(chunk_added, u * U + (j + 1))
                    at = acc[:, bass.ds(offs[j], width)]
                    dve.tensor_tensor(at, at, sums[j][:, 0:width], ALU.add).then_inc(chunk_added, 1)
                    if head_scale and following is not None:
                        scale_heads(*following, j)

            dve.memset(ring[:, :, :, MSG_ONE], 1.0).then_inc(set_up, 1)
            begin(0, 0)
            if started:
                take(0, 0)
                for j in range(U):
                    scale_heads(0, 0, j)
                dve.memset(acc[:, 0:half], 0.0).then_inc(chunk_added, 1)
                dve.wait_ge(half_cleared, 1)
            else:
                dve.memset(acc, 0.0).then_inc(chunk_added, 1)
                take(0, 0)
            with dve.Fori(0, units // SLOTS - 1) as i:
                for s in range(SLOTS):
                    following = (i + (s + 1) // SLOTS, (s + 1) % SLOTS)
                    begin(*following)
                    take(*following)
                    add(i, s, following)
            last = units // SLOTS - 1
            for s in range(SLOTS):
                following = (last, s + 1) if s + 1 < SLOTS else None
                if following:
                    begin(*following)
                    take(*following)
                add(last, s, following)

        @block.tensor
        def _(pe):
            def sum_unit(i, s, first):
                u = i * SLOTS + s
                pe.wait_ge(member_made, u + 1)
                if not head_scale:
                    pe.wait_ge(prepared, u + 1)
                for j in range(U):
                    if head_scale:
                        pe.wait_ge(prepared, u * U + (j + 1))
                    if not first:
                        pe.wait_ge(chunk_added, u * U + (j + 2 - U))
                    pe.matmul(sums[j][:, 0:width], member[:, s % 2, j, :], ring[:, s, j, 0:width],
                              start=True, stop=True).then_inc(chunk_summed, 1)

            for s in range(SLOTS):
                sum_unit(0, s, s == 0)
            with pe.Fori(1, units // SLOTS) as i:
                for s in range(SLOTS):
                    sum_unit(i, s, False)


def project_phase(nc, k, name, table_in, w, att_src, att_dst, table_h):
    WE = D + 2 * H
    with ExitStack() as ctx:
        m = Mem(nc, ctx, name)
        w_sb = m.sb("w", [P, 2, WE])
        att = m.sb("att", [P, 2, D])
        prod = m.sb("prod", [P, 2, D])
        xin = m.sb("xin", [P, 4, D])
        xt = m.sb("xt", [P, 2, D])
        h_out = m.sb("h_out", [P, 4, D])
        xt_ps = [m.ps(f"xt_ps{s}", [P, 512]) for s in range(2)]
        h_ps = [m.ps(f"h_ps{s}", [P, 512]) for s in range(2)]
        w_in, dv = m.sem("w_in"), m.sem("dve")
        w_ready = m.sem("w_ready")
        loaded = [m.sem(f"loaded{s}") for s in range(4)]
        stored = [m.sem(f"stored{s}") for s in range(4)]
        turned, xt_made, summed, h_made = m.sem("turned"), m.sem("xt_made"), m.sem("summed"), m.sem("h_made")
        block = ctx.enter_context(nc.Block())

        @block.sync
        def _(sp):
            for c in range(2):
                sp.dma_start(w_sb[:, c, 0:D], w[c * P:(c + 1) * P, :]).then_inc(w_in, 16)
            for n, a in enumerate((att_src, att_dst)):
                flat = a.rearrange("h c -> (h c)") if len(a.shape) == 2 else a.rearrange("a h c -> (a h c)")
                sp.dma_start(att[:, n, :], flat.partition_broadcast(P)).then_inc(w_in, 16)

            def load(t, s, first):
                if not first:
                    sp.wait_ge(turned, t - 3)
                sp.dma_start(xin[:, s, :], table_in[bass.ds(t * P, P), :]).then_inc(loaded[s], 16)

            pipeline(sp, (load, 0), slots=4)

        @block.tensor
        def _(pe):
            pe.wait_ge(w_ready, 1)

            def turn(t, s, first):
                pe.wait_ge(loaded[s], (t - s) * 4 + 16)
                if not before(t, 2):
                    pe.wait_ge(xt_made, t - 1)
                for c in range(2):
                    ins = pe.transpose(xt_ps[s % 2][:, c * P:(c + 1) * P], xin[:, s, c * P:(c + 1) * P], k.ident[:])
                ins.then_inc(turned, 1)

            def multiply(t, s, first):
                pe.wait_ge(xt_made, t + 1)
                if not before(t, 2):
                    pe.wait_ge(h_made, t - 1)
                for c in range(2):
                    ins = pe.matmul(h_ps[s % 2][:, 0:WE], xt[:, s % 2, c * P:(c + 1) * P], w_sb[:, c, :],
                                    start=(c == 0), stop=(c == 1))
                ins.then_inc(summed, 1)

            pipeline(pe, (turn, 0), (multiply, 1), slots=4)

        @block.scalar
        def _(act):
            def take(t, s, first):
                act.wait_ge(turned, t + 1)
                if not first:
                    act.wait_ge(summed, t - 1)
                act.copy(xt[:, s, :], xt_ps[s][:, 0:D]).then_inc(xt_made, 1)

            pipeline(act, (take, 0))

        @block.vector
        def _(dve):
            st = Steps(dve, dv)
            dve.wait_ge(w_in, 64)
            for n in range(2):
                for c in range(2):
                    st(dve.tensor_tensor(prod[:, c, :], w_sb[:, c, 0:D], att[:, n, :], ALU.mult))
                    st(dve.tensor_reduce(w_sb[:, c, D + n * H:D + (n + 1) * H],
                                         prod[:, c, :].rearrange("p (h f) -> p h f", h=H), AX.X, ALU.add))
            dve.sem_inc(w_ready, 1)

            def take(t, s, first):
                dve.wait_ge(summed, t + 1)
                if not first:
                    dve.wait_ge(stored[s], (t - s) * 4)
                dve.tensor_copy(k.att[:, bass.ds(t * 2 * H, 2 * H)], h_ps[s % 2][:, D:WE])
                dve.tensor_copy(h_out[:, s, :], h_ps[s % 2][:, 0:D]).then_inc(h_made, 1)

            pipeline(dve, (take, 0), slots=4)

        @block.gpsimd
        def _(pool):
            def store(t, s, first):
                pool.wait_ge(h_made, t + 1)
                pool.dma_start(table_h[bass.ds(t * P, P), :], h_out[:, s, :]).then_inc(stored[s], 16)

            pipeline(pool, (store, 0), slots=4)
            for s in range(4):
                pool.wait_ge(stored[s], (NTP + 3 - s) // 4 * 16)


def lookup_phase(nc, k, name, codes_dram, att_dram, z, z_self):
    NS = H * NT
    LP = U - BY_GATHER
    with ExitStack() as ctx:
        m = Mem(nc, ctx, name)
        left = m.sb("left", [P, NTP, 2 * H])
        dst_parts = m.sb("dst_parts", [P, NTP, 3, 2 * H], BF16)
        src_parts = m.sb("src_parts", [P, 3, H, NT], BF16)
        other = m.sb("other", [P, H, NT], BF16)
        dst_codes = m.sb("dst_codes", [P, SLOTS, U * P], BF16)
        src_codes = m.sb("src_codes", [P, SLOTS, 2, LP * P], BF16)
        dst_member = m.sb("dst_member", [P, 2, U * P], BF16)
        src_member = m.sb("src_member", [P, 2, 2, LP * P], BF16)
        index = m.sb("index", [P, SLOTS, BY_GATHER], I32)
        rows = m.sb("rows", [P, SLOTS, BY_GATHER, 2 * H])
        picked = m.sb("picked", [P, 2, LP, H])
        dst_sum = m.sb("dst_sum", [P, 2, U, 2 * H])
        src_ps = [m.ps(f"src_ps{s}", [P, LP, 256]) for s in range(2)]
        dst_ps = [m.ps(f"dst_ps{s}", [P, 512]) for s in range(2)]
        dv, parts_made = m.sem("dve"), m.sem("parts_made")
        codes_in = [m.sem(f"codes_in{s}") for s in range(SLOTS)]
        gathered = [m.sem(f"gathered{s}") for s in range(SLOTS)]
        turn = m.sem("gather_turn")
        index_ready, att_stored = m.sem("index_ready"), m.sem("att_stored")
        member_made, summed, reduced, taken, dst_summed = (
            m.sem(n) for n in ("member_made", "summed", "reduced", "taken", "dst_summed"))
        block = ctx.enter_context(nc.Block())
        units = NCH // U

        @block.sync
        def _(sp):
            sp.dma_start(att_dram.rearrange("(p t) a -> p (t a)", p=P), k.att[:]).then_inc(att_stored, 16)

            def load(u, s, first):
                if not first:
                    sp.wait_ge(member_made, u + 1 - SLOTS)
                at = u * (U * P)
                sp.dma_start(dst_codes[:, s], codes_dram[0, bass.ds(at, U * P)].partition_broadcast(P)).then_inc(codes_in[s], 16)
                sp.dma_start(src_codes[:, s], codes_dram[1:3, bass.ds(at, LP * P)].partition_broadcast(P)).then_inc(codes_in[s], 16)

            for s in range(SLOTS):
                load(s, s, True)
            with sp.Fori(1, units // SLOTS) as i:
                for s in range(SLOTS):
                    load(i * SLOTS + s, s, False)

        @block.scalar
        def _(act):
            def fill(s, u):
                act.copy(index[:, s, :], k.att_row[:, bass.ds(u * U + LP, BY_GATHER)]).then_inc(index_ready, 1)

            for s in range(SLOTS):
                fill(s, s)
            with act.Fori(1, units // SLOTS) as i:
                for s in range(SLOTS):
                    act.wait_ge(taken, i * SLOTS + (s + 1 - SLOTS))
                    fill(s, i * SLOTS + s)

        @block.gpsimd
        def _(pool):
            pool.wait_ge(att_stored, 16)
            with pool.Fori(0, units // SLOTS) as i:
                for s in range(SLOTS):
                    pool.wait_ge(index_ready, i * SLOTS + s + 1)
                    pool.sem_inc(turn, 1)
                    for j in range(BY_GATHER):
                        pool.indirect_dma_start(
                            out=rows[:, s, j, :], out_offset=None, in_=att_dram,
                            in_offset=bass.IndirectOffsetOnAxis(ap=index[:, s, j:j + 1], axis=0),
                        ).then_inc(gathered[s], 16)

        @block.vector
        def _(dve):
            st = Steps(dve, dv)
            for h in range(H):
                ins = dve.tensor_scalar(other[:, h, :], k.iota[:, 0:NT], k.partition[:], None, op0=ALU.is_equal)
            st(ins)
            st(dve.tensor_scalar(other[:], other[:], -1.0, FAR, op0=ALU.add, op1=ALU.mult))
            st(dve.tensor_copy(left[:].rearrange("p t a -> p (t a)"), k.att[:]))
            for n in range(3):
                part = dst_parts[:, :, n]
                st(dve.tensor_copy(part, left[:]))
                if n < 2:
                    st(dve.tensor_tensor(left[:], left[:], part, ALU.subtract))
                dve.tensor_copy(src_parts[:, n].rearrange("p h t -> p t h"), part[:, 0:NT, 0:H]).then_inc(parts_made, 1)

            def prepare(i, r):
                s = r % 2
                dve.wait_ge(codes_in[r], i * 32 + 32)
                dve.tensor_scalar(dst_member[:, s], dst_codes[:, r], k.partition[:], None, op0=ALU.is_equal)
                dve.tensor_scalar(src_member[:, s], src_codes[:, r], k.partition[:], None,
                                  op0=ALU.is_equal).then_inc(member_made, 1)

            def pick(i, r):
                s, u = r % 2, i * SLOTS + r
                dve.wait_ge(summed, u + 1)
                dst = dst_sum[:, s]
                dve.tensor_reduce(dst, dst_ps[s][:, 0:U * 3 * 2 * H].rearrange("p (c n a) -> p c a n", c=U, n=3),
                                  AX.X, ALU.add).then_inc(dst_summed, 1)
                dve.tensor_reduce(picked[:, s], src_ps[s][:, :, 0:NS].rearrange("p c (h t) -> p c h t", h=H),
                                  AX.X, ALU.max).then_inc(reduced, 1)
                dve.wait_ge(dst_summed, u + 1)
                if z_self is not None:
                    zs = by_chunk(z_self)[:, bass.ds(u * U, U), :]
                    dve.tensor_tensor(zs, dst[:, :, 0:H], dst[:, :, H:], ALU.add)
                dve.wait_ge(gathered[r], i * (16 * BY_GATHER) + 16 * BY_GATHER)
                dve.tensor_tensor(by_chunk(z)[:, bass.ds(u * U + LP, BY_GATHER), :], rows[:, r, :, 0:H],
                                  dst[:, LP:, H:], ALU.add)
                dve.wait_ge(reduced, u + 1)
                dve.tensor_tensor(by_chunk(z)[:, bass.ds(u * U, LP), :], picked[:, s], dst[:, 0:LP, H:],
                                  ALU.add).then_inc(taken, 1)

            prepare(0, 0)
            with dve.Fori(0, units // SLOTS - 1) as i:
                for r in range(SLOTS):
                    prepare(i + (r + 1) // SLOTS, (r + 1) % SLOTS)
                    pick(i, r)
            last = units // SLOTS - 1
            for r in range(SLOTS):
                if r + 1 < SLOTS:
                    prepare(last, r + 1)
                pick(last, r)

        @block.tensor
        def _(pe):
            pe.wait_ge(parts_made, 3)

            def look(i, s, first):
                u = i * 2 + s
                offs = nc.values_load_multi_w_load_instructions(
                    k.tile_off_a[0:1, bass.ds(u * U, U)], engines=(mybir.EngineType.PE,),
                    min_val=0, max_val=(NT - 1) * 3 * 2 * H, skip_runtime_bounds_check_because="made so")[1]
                pe.wait_ge(member_made, u + 1)
                if not first:
                    pe.wait_ge(taken, u - 1)
                for j in range(U):
                    edges = slice(j * P, (j + 1) * P)
                    if j < LP:
                        for n in range(3):
                            pe.matmul(src_ps[s][:, j, 0:NS], src_member[:, s, 0, edges],
                                      src_parts[:, n].rearrange("p h t -> p (h t)"), start=(n == 0), stop=False)
                        pe.matmul(src_ps[s][:, j, 0:NS], src_member[0:NT, s, 1, edges],
                                  other[0:NT].rearrange("p h t -> p (h t)"), start=False, stop=True)
                    ins = pe.matmul(dst_ps[s][:, j * 3 * 2 * H:(j + 1) * 3 * 2 * H], dst_member[:, s, edges],
                                    dst_parts[:].rearrange("p t n a -> p (t n a)")[:, bass.ds(offs[j], 3 * 2 * H)],
                                    start=True, stop=True)
                ins.then_inc(summed, 1)

            for s in range(2):
                look(0, s, True)
            with pe.Fori(1, units // 2) as i:
                for s in range(2):
                    look(i, s, False)


def softmax_phase(nc, k, name, flags_dram, z, z_self, scaled, ring, table):
    with ExitStack() as ctx:
        m = Mem(nc, ctx, name)
        breaks = m.sb("breaks", [P, RL + 1])
        z_scan = m.sb("z_scan", [P, RL])
        self_scan = m.sb("self_scan", [P, RL]) if z_self is not None else None
        fwd = m.sb("fwd", [P, RL])
        back = m.sb("back", [P, RL])
        row = m.sb("row", [1, 2, P + 2])
        carry = m.sb("carry", [P, 2])
        tp = [m.ps(f"tp{n}", [P, P]) for n in range(4)]
        row_ps = m.ps("row_ps", [P, 512])
        flags_in, dv = m.sem("flags_in"), m.sem("dve")
        leaky_made, turned, taken_v, taken_a = m.sem("leaky_made"), m.sem("turned"), m.sem("taken_dve"), m.sem("taken_act")
        last_made, row_made, row_carried, carry_made = m.sem("last_made"), m.sem("row_made"), m.sem("row_carried"), m.sem("carry_made")
        index_ready = m.sem("index_ready")
        max_made, numer_made = m.sem("max_made"), m.sem("numer_made")
        block = ctx.enter_context(nc.Block())
        both = z_self is not None
        by_run = lambda t: t[:].rearrange("p h (r c) -> p c (h r)", c=RUN)

        @block.sync
        def _(sp):
            sp.dma_start(breaks[:], flags_dram).then_inc(flags_in, 16)

        @block.tensor
        def _(pe):
            pe.wait_ge(leaky_made, 1)
            for c in range(RUN):
                if c >= 2:
                    pe.wait_ge(taken_a, c - 1)
                pe.transpose(tp[c % 2][:], by_run(z)[:, c], k.ident[:]).then_inc(turned, 1)
                if both:
                    if c >= 2:
                        pe.wait_ge(taken_v, c - 1)
                    pe.transpose(tp[2 + c % 2][:], by_run(z_self)[:, c], k.ident[:]).then_inc(turned, 1)
            for n, (source, at) in enumerate(((fwd, RL - 1), (back, 0))):
                pe.wait_ge(last_made, n + 1)
                pe.transpose(row_ps[0:1, 0:P], source[:, at:at + 1], k.ident[:]).then_inc(row_made, 1)
                pe.wait_ge(row_carried, n + 1)
                pe.transpose(row_ps[:, 256 + n:257 + n], row[0:1, 1, 0:P], k.ident[0:1, 0:1]).then_inc(carry_made, 1)
            pe.wait_ge(max_made, 1)
            pe.wait_ge(taken_a, RUN)
            if both:
                pe.wait_ge(taken_v, RUN)
            for c in range(RUN):
                if c >= 2:
                    pe.wait_ge(taken_a, RUN + c - 1)
                pe.transpose(tp[c % 2][:], back[:, c * P:(c + 1) * P], k.ident[:]).then_inc(turned, 1)
                if both:
                    if c >= 2:
                        pe.wait_ge(taken_v, RUN + c - 1)
                    pe.transpose(tp[2 + c % 2][:], fwd[:, c * P:(c + 1) * P], k.ident[:]).then_inc(turned, 1)

        per = 2 if both else 1

        @block.gpsimd
        def _(pool):
            for s in range(SLOTS):
                pool.wait_ge(index_ready, s + 1)
                ring.gather(pool, table, s)

        @block.scalar
        def _(act):
            for s in range(SLOTS):
                act.copy(ring.index[:, s, :], k.src[:, s * U:(s + 1) * U]).then_inc(index_ready, 1)
            for c in range(RUN):
                act.wait_ge(turned, per * c + 1)
                act.copy(z_scan[:, c * P:(c + 1) * P], tp[c % 2][:]).then_inc(taken_a, 1)
            for c in range(RUN):
                act.wait_ge(turned, per * (RUN + c) + 1)
                act.copy(by_run(k.numer)[:, c], tp[c % 2][:]).then_inc(taken_a, 1)
            act.wait_ge(numer_made, 1)
            act.activation(k.numer[:], k.numer[:], ACT.Exp).then_inc(numer_made, 1)

        @block.vector
        def _(dve):
            st = Steps(dve, dv)
            for t in (z, z_self) if both else (z,):
                st(dve.scalar_tensor_tensor(t[:], t[:], SLOPE, t[:], op0=ALU.mult, op1=ALU.max))
            dve.sem_inc(leaky_made, 1)
            if both:
                for c in range(RUN):
                    dve.wait_ge(turned, 2 * c + 2)
                    dve.tensor_copy(self_scan[:, c * P:(c + 1) * P], tp[2 + c % 2][:]).then_inc(taken_v, 1)
                dve.wait_ge(taken_v, RUN)
            dve.wait_ge(flags_in, 16)
            dve.wait_ge(taken_a, RUN)
            st(dve.memset(row[:], 0.0))

            def scan_fwd(initial):
                return dve.tensor_tensor_scan(fwd[:], breaks[:, 0:RL], z_scan[:], initial, op0=ALU.add, op1=ALU.max)

            def scan_back(initial):
                return dve.tensor_tensor_scan(back[:, ::-1], breaks[:, 1:RL + 1][:, ::-1], fwd[:, ::-1], initial,
                                              op0=ALU.add, op1=ALU.max)

            st(scan_fwd(NEG))
            dve.sem_inc(last_made, 1)
            dve.wait_ge(row_made, 1)
            st(dve.tensor_tensor_scan(row[0:1, 0, 1:P + 1], k.through_fwd[:], row_ps[0:1, 0:P], NEG,
                                      op0=ALU.add, op1=ALU.max))
            st(dve.tensor_tensor(row[0:1, 1, 0:P], row[0:1, 0, 0:P], k.breaks_in[0:1, 0:P], ALU.add))
            dve.sem_inc(row_carried, 1)
            dve.wait_ge(carry_made, 1)
            st(dve.tensor_copy(carry[:, 0:1], row_ps[:, 256:257]))
            st(scan_fwd(carry[:, 0:1]))
            st(scan_back(NEG))
            dve.sem_inc(last_made, 1)
            dve.wait_ge(row_made, 2)
            st(dve.memset(row[0:1, 0, P:P + 2], 0.0))
            st(dve.tensor_tensor_scan(row[0:1, 0, 0:P][:, ::-1], k.through_back[0:1, ::-1], row_ps[0:1, 0:P][:, ::-1],
                                      NEG, op0=ALU.add, op1=ALU.max))
            st(dve.tensor_tensor(row[0:1, 1, 0:P], row[0:1, 0, 1:P + 1], k.breaks_in[0:1, 1:P + 1], ALU.add))
            dve.sem_inc(row_carried, 1)
            dve.wait_ge(carry_made, 2)
            st(dve.tensor_copy(carry[:, 1:2], row_ps[:, 257:258]))
            st(scan_back(carry[:, 1:2]))
            if both:
                st(dve.tensor_tensor(back[:], back[:], self_scan[:], ALU.max))
                st(dve.tensor_scalar(fwd[:], breaks[:, 0:RL], 0.0, None, op0=ALU.not_equal))
                st(dve.tensor_copy(fwd[:, 0:1], k.first_in_run[:]))
                st(dve.tensor_tensor(fwd[:], fwd[:], back[:], ALU.mult))
            dve.sem_inc(max_made, 1)
            if both:
                for c in range(RUN):
                    dve.wait_ge(turned, 2 * (RUN + c) + 2)
                    dve.tensor_copy(by_run(k.first_max)[:, c], tp[2 + c % 2][:]).then_inc(taken_v, 1)
            dve.wait_ge(taken_a, 2 * RUN)
            dve.tensor_tensor(k.numer[:], z[:], k.numer[:], ALU.subtract).then_inc(numer_made, 1)
            if scaled is not None:
                dve.wait_ge(numer_made, 2)
                dve.tensor_tensor(scaled[:], k.numer[:], repeat_outer(k.dist[:], H), ALU.mult)


SEG = 10
assert NTP % SEG == 0


def attention_end_phase(nc, k, name, acc, table_h, own, bias, residual, table_out):
    with ExitStack() as ctx:
        m = Mem(nc, ctx, name)
        zn = m.sb("zn", [P, NTP, H])
        mx = m.sb("mx", [P, NTP, H])
        inv = m.sb("inv", [P, NTP, H])
        no_edge = m.sb("no_edge", [P, NTP])
        bias_sb = m.sb("bias", [P, D])
        h_in = m.sb("h_in", [P, 2, SEG, D])
        x_in = m.sb("x_in", [P, 2, SEG, D])
        dv, small_in, numer_ready, numer_made = m.sem("dve"), m.sem("small_in"), m.sem("numer_ready"), m.sem("numer_made")
        h_loaded = [m.sem(f"h_loaded{s}") for s in range(2)]
        x_loaded = [m.sem(f"x_loaded{s}") for s in range(2)]
        weights_made, h_scaled, x_biased, seg_made, relu_made, stored = (
            m.sem(n) for n in ("weights_made", "h_scaled", "x_biased", "seg_made", "relu_made", "stored"))
        block = ctx.enter_context(nc.Block())
        acc3 = acc.rearrange("p (t w) -> p t w", w=MSGW)
        segs = [(n, n % 2, slice(n * SEG, (n + 1) * SEG)) for n in range(NTP // SEG)]

        def rows(table, ts):
            return table[ts.start * P:ts.stop * P, :].rearrange("(t p) d -> p t d", p=P)

        def by_tile(ap):
            return ap.unsqueeze(1).to_broadcast([P, SEG, D])

        @block.sync
        def _(sp):
            if own:
                sp.dma_start(bias_sb[:], bias.partition_broadcast(P)).then_inc(small_in, 16)
            for n, s, ts in segs:
                if n >= 2:
                    sp.wait_ge(seg_made, n - 1)
                if own:
                    sp.dma_start(h_in[:, s], rows(table_h, ts)).then_inc(h_loaded[s], 16)
                if residual is not None:
                    sp.dma_start(x_in[:, s], rows(residual, ts)).then_inc(x_loaded[s], 16)

        @block.scalar
        def _(act):
            if own:
                act.wait_ge(numer_ready, 1)
                act.activation(zn[:], zn[:], ACT.Exp).then_inc(numer_made, 1)
            if residual is None:
                for n, s, ts in segs:
                    act.wait_ge(seg_made, n + 1)
                    act.activation(acc3[:, ts, 0:D], acc3[:, ts, 0:D], ACT.Relu).then_inc(relu_made, 1)
                    act.wait_ge(relu_made, n + 1)
                    act.dma_start(rows(table_out, ts), acc3[:, ts, 0:D]).then_inc(stored, 16)
                act.wait_ge(stored, 16 * len(segs))

        @block.gpsimd
        def _(pool):
            if own:
                pool.wait_ge(small_in, 16)
                pool.wait_ge(weights_made, 1)
                for n, s, ts in segs:
                    pool.wait_ge(h_loaded[s], 16 * (n // 2 + 1))
                    for t in range(SEG):
                        rows_h = h_in[:, s, t].rearrange("p (h f) -> p h f", h=H)
                        ins = pool.tensor_tensor(rows_h, rows_h, repeat_inner(zn[:, ts.start + t, :], C), ALU.mult)
                    ins.then_inc(h_scaled, 1)
                    if residual is not None:
                        pool.wait_ge(x_loaded[s], 16 * (n // 2 + 1))
                        pool.tensor_tensor(x_in[:, s], x_in[:, s], by_tile(bias_sb[:]), ALU.add).then_inc(x_biased, 1)

        @block.vector
        def _(dve):
            st = Steps(dve, dv)
            sums_p = acc3[:, :, MSG_P:MSG_P + H]
            if own:
                att = k.att[:].rearrange("p (t a) -> p t a", a=2 * H)
                st(dve.tensor_tensor(zn[:], att[:, :, 0:H], att[:, :, H:], ALU.add))
                st(dve.scalar_tensor_tensor(zn[:], zn[:], SLOPE, zn[:], op0=ALU.mult, op1=ALU.max))
                st(dve.tensor_scalar(no_edge[:], acc3[:, :, MSG_ONE], 0.5, None, op0=ALU.is_lt))
                st(dve.tensor_tensor(mx[:], zn[:], repeat_inner(no_edge[:], H), ALU.mult))
                st(dve.tensor_tensor(mx[:], mx[:], acc3[:, :, MSG_M:MSG_M + H], ALU.add))
                st(dve.tensor_tensor(zn[:], zn[:], mx[:], ALU.subtract))
                dve.sem_inc(numer_ready, 1)
                dve.wait_ge(numer_made, 1)
                st(dve.tensor_tensor(inv[:], zn[:], sums_p, ALU.add))
                st(dve.tensor_scalar(inv[:], inv[:], 1e-16, None, op0=ALU.add))
            else:
                st(dve.tensor_scalar(inv[:], sums_p, 1e-30, None, op0=ALU.max))
            st(dve.reciprocal(inv[:], inv[:]))
            if own:
                st(dve.tensor_tensor(zn[:], zn[:], inv[:], ALU.mult))
                dve.sem_inc(weights_made, 1)
                dve.wait_ge(small_in, 16)
            for n, s, ts in segs:
                here = acc3[:, ts, 0:D]
                for t in range(SEG):
                    row = acc3[:, ts.start + t, 0:D].rearrange("p (h f) -> p h f", h=H)
                    ins = dve.tensor_tensor(row, row, repeat_inner(inv[:, ts.start + t, :], C), ALU.mult)
                st(ins)
                if own:
                    dve.wait_ge(h_scaled, n + 1)
                    st(dve.tensor_tensor(here, here, h_in[:, s], ALU.add))
                if residual is None:
                    dve.tensor_tensor(here, here, by_tile(bias_sb[:]), ALU.add).then_inc(seg_made, 1)
                else:
                    dve.wait_ge(*((x_biased, n + 1) if own else (x_loaded[s], 16 * (n // 2 + 1))))
                    dve.tensor_tensor(here, here, x_in[:, s], ALU.add).then_inc(seg_made, 1)


def layernorm_phase(nc, k, name, acc, table_out, out, made_stats=None):
    with ExitStack() as ctx:
        m = Mem(nc, ctx, name)
        stats = made_stats or m.sb("stats", [P, NTP, 6])
        mean = m.sb("mean", [P, NTP])
        var = m.sb("var", [P, NTP])
        tmp = m.sb("tmp", [P, NTP])
        eps = m.sb("eps", [P, 1])
        dv, var_made, root_made = m.sem("dve"), m.sem("var_made"), m.sem("root_made")
        centred, normed, stored = m.sem("centred"), m.sem("normed"), m.sem("stored")
        block = ctx.enter_context(nc.Block())
        acc3 = acc.rearrange("p (t w) -> p t w", w=MSGW)
        segs = [(n, slice(n * SEG, (n + 1) * SEG)) for n in range(NTP // SEG)]

        @block.scalar
        def _(act):
            act.wait_ge(var_made, 1)
            act.activation(var[:], var[:], ACT.Sqrt, bias=eps[:]).then_inc(root_made, 1)

        @block.vector
        def _(dve):
            st = Steps(dve, dv)
            st(dve.memset(eps[:], EPS))
            if not made_stats:
                for t in range(NTP):
                    ins = dve.bn_stats(stats[:, t, :], acc3[:, t, 0:D])
                st(ins)
            st(dve.tensor_tensor(mean[:], stats[:, :, 1], stats[:, :, 4], ALU.add))
            st(dve.tensor_scalar(mean[:], mean[:], 0.5, None, op0=ALU.mult))
            st(dve.tensor_tensor(tmp[:], stats[:, :, 1], stats[:, :, 4], ALU.subtract))
            st(dve.tensor_tensor(tmp[:], tmp[:], tmp[:], ALU.mult))
            st(dve.tensor_scalar(tmp[:], tmp[:], 0.25, None, op0=ALU.mult))
            st(dve.tensor_tensor(var[:], stats[:, :, 2], stats[:, :, 5], ALU.add))
            st(dve.scalar_tensor_tensor(var[:], var[:], 1.0 / D, tmp[:], op0=ALU.mult, op1=ALU.add))
            dve.sem_inc(var_made, 1)
            dve.wait_ge(root_made, 1)
            st(dve.reciprocal(var[:], var[:]))
            for n, ts in segs:
                for t in range(ts.start, ts.stop):
                    ins = dve.tensor_scalar(acc3[:, t, 0:D], acc3[:, t, 0:D], mean[:, t:t + 1], var[:, t:t + 1],
                                            op0=ALU.subtract, op1=ALU.mult)
                ins.then_inc(normed, 1)

        @block.sync
        def _(sp):
            n_stored = 0
            for n, ts in segs:
                sp.wait_ge(normed, n + 1)
                if out is None:
                    parts = [(table_out, ts.stop)]
                else:
                    parts = [(out, min(N // P, ts.stop))]
                for table, stop in parts:
                    sp.dma_start(table[ts.start * P:stop * P, :].rearrange("(t p) d -> p t d", p=P),
                                 acc3[:, ts.start:stop, 0:D]).then_inc(stored, 16)
                    n_stored += 16
                if out is not None and stop < ts.stop:
                    sp.dma_start(out[stop * P:N, :], acc3[0:N % P, stop, 0:D]).then_inc(stored, 16)
                    n_stored += 16
            sp.wait_ge(stored, n_stored)


def graph_conv_phase(nc, k, name, acc, table_in, w_rel, w_root, bias, table_out, residual, row_stats):
    with ExitStack() as ctx:
        m = Mem(nc, ctx, name)
        w_sb = m.sb("w", [P, 4, D])
        bias_sb = m.sb("bias", [P, D])
        xin = m.sb("xin", [P, 4, D])
        agg = m.sb("agg", [P, 2, D])
        res = m.sb("res", [P, 4, D])
        inT = m.sb("inT", [P, 2, 2 * D])
        y = m.sb("y", [P, 2, D])
        y_out = m.sb("y_out", [P, 4, D])
        low = m.sb("low", [P, 2, D])
        t_ps = [m.ps(f"t_ps{s}", [P, 512]) for s in range(2)]
        y_ps = [m.ps(f"y_ps{s}", [P, 512]) for s in range(2)]
        w_in = m.sem("w_in")
        loaded = [m.sem(f"loaded{s}") for s in range(4)]
        stored = [m.sem(f"stored{s}") for s in range(4)]
        agg_made, turned, inT_made, summed = m.sem("agg_made"), m.sem("turned"), m.sem("inT_made"), m.sem("summed")
        res_loaded = [m.sem(f"res_loaded{s}") for s in range(4)]
        low_made, exp_made, y_made, y_summed, lowered, elu_made = (
            m.sem(n) for n in ("low_made", "exp_made", "y_made", "y_summed", "lowered", "elu_made"))
        block = ctx.enter_context(nc.Block())

        @block.sync
        def _(sp):
            for n, w in enumerate((w_rel, w_root)):
                for c in range(2):
                    sp.dma_start(w_sb[:, 2 * n + c, :], w[c * P:(c + 1) * P, :]).then_inc(w_in, 16)
            sp.dma_start(bias_sb[:], bias.partition_broadcast(P)).then_inc(w_in, 16)

            def load(t, s, first):
                if not first:
                    sp.wait_ge(turned, t - 3)
                sp.dma_start(xin[:, s, :], table_in[bass.ds(t * P, P), :]).then_inc(loaded[s], 16)

            pipeline(sp, (load, 0), slots=4)

        @block.scalar
        def _(act):
            def place(t, s, first):
                if not first:
                    act.wait_ge(turned, t - 1)
                act.copy(agg[:, s, :], acc[:, bass.ds(t * MSGW, D)]).then_inc(agg_made, 1)

            def take(t, s, first):
                act.wait_ge(turned, t + 1)
                if not first:
                    act.wait_ge(summed, t - 1)
                act.copy(inT[:, s, :], t_ps[s][:]).then_inc(inT_made, 1)

            def exp(t, s, first):
                act.wait_ge(low_made, t + 1)
                act.activation(low[:, s, :], low[:, s, :], ACT.Exp).then_inc(exp_made, 1)

            pipeline(act, (place, 0), (take, 1), (exp, 3))

        @block.tensor
        def _(pe):
            pe.wait_ge(w_in, 80)

            def turn(t, s, first):
                pe.wait_ge(agg_made, t + 1)
                pe.wait_ge(loaded[s], (t - s) * 4 + 16)
                if not before(t, 2):
                    pe.wait_ge(inT_made, t - 1)
                for n, source in enumerate((agg[:, s % 2], xin[:, s])):
                    for c in range(2):
                        ins = pe.transpose(t_ps[s % 2][:, (2 * n + c) * P:(2 * n + c + 1) * P],
                                           source[:, c * P:(c + 1) * P], k.ident[:])
                ins.then_inc(turned, 1)

            def multiply(t, s, first):
                pe.wait_ge(inT_made, t + 1)
                if not before(t, 2):
                    pe.wait_ge(y_summed, t - 1)
                for n in range(4):
                    ins = pe.matmul(y_ps[s % 2][:, 0:D], inT[:, s % 2, n * P:(n + 1) * P], w_sb[:, n, :],
                                    start=(n == 0), stop=(n == 3))
                ins.then_inc(summed, 1)

            pipeline(pe, (turn, 0), (multiply, 2), slots=4)

        @block.vector
        def _(dve):
            dve.wait_ge(w_in, 80)

            def start(t, s, first):
                b = s % 2
                dve.wait_ge(summed, t + 1)
                if not before(t, 2):
                    dve.wait_ge(y_made, t - 1)
                dve.tensor_tensor(y[:, b, :], y_ps[b][:, 0:D], bias_sb[:], ALU.add).then_inc(y_summed, 1)
                dve.wait_ge(y_summed, t + 1)
                dve.tensor_scalar(low[:, b, :], y[:, b, :], 0.0, None, op0=ALU.min).then_inc(low_made, 1)

            def finish(t, s, first):
                b = s % 2
                dve.wait_ge(exp_made, t + 1)
                dve.tensor_scalar(low[:, b, :], low[:, b, :], -1.0, None, op0=ALU.add).then_inc(lowered, 1)
                dve.wait_ge(lowered, t + 1)
                if residual is None:
                    if not first:
                        dve.wait_ge(stored[s], (t - s) * 4)
                    dve.scalar_tensor_tensor(y_out[:, s, :], y[:, b, :], 0.0, low[:, b, :],
                                             op0=ALU.max, op1=ALU.add).then_inc(y_made, 1)
                else:
                    dve.scalar_tensor_tensor(y[:, b, :], y[:, b, :], 0.0, low[:, b, :],
                                             op0=ALU.max, op1=ALU.add).then_inc(elu_made, 1)
                    dve.wait_ge(elu_made, t + 1)
                    dve.wait_ge(res_loaded[s], (t - s) * 4 + 16)
                    dve.tensor_tensor(acc[:, bass.ds(t * MSGW, D)], y[:, b, :], res[:, s, :], ALU.add).then_inc(y_made, 1)

            def stat(t, s, first):
                dve.wait_ge(y_made, t + 1)
                dve.bn_stats(row_stats[:].rearrange("p t s -> p (t s)")[:, bass.ds(t * 6, 6)], acc[:, bass.ds(t * MSGW, D)])

            pipeline(dve, (start, 0), (finish, 1), *([] if residual is None else [(stat, 2)]), slots=4)

        @block.gpsimd
        def _(pool):
            if residual is None:
                def store(t, s, first):
                    pool.wait_ge(y_made, t + 1)
                    pool.dma_start(table_out[bass.ds(t * P, P), :], y_out[:, s, :]).then_inc(stored[s], 16)

                pipeline(pool, (store, 0), slots=4)
                for s in range(4):
                    pool.wait_ge(stored[s], (NTP + 3 - s) // 4 * 16)
            else:
                def load_res(t, s, first):
                    if not first:
                        pool.wait_ge(y_made, t - 3)
                    pool.dma_start(res[:, s, :], residual[bass.ds(t * P, P), :]).then_inc(res_loaded[s], 16)

                pipeline(pool, (load_res, 0), slots=4)


def batch_norm_layer_phase(nc, k, name, acc, table_in, w1, gamma1, beta1, w2, eps_weight, gamma_h, beta_h, norm_dram, row_stats):
    NB = 512
    blocks = [(b, min(NB, NP - b)) for b in range(0, NP, NB)]
    with ExitStack() as ctx:
        m = Mem(nc, ctx, name)
        w_in_sb = m.sb("w_in_sb", [P, 2, 2, D])
        wT = m.sb("wT", [P, 2, 2, D])
        zT = m.sb("zT", [P, 2, NP])
        n_norm = m.sb("n_norm", [P, NP])
        xin = m.sb("xin", [P, 4, D])
        yin = m.sb("yin", [P, 2, D])
        yT = m.sb("yT", [P, 2, D])
        eps_w = m.sb("eps_w", [P, 1])
        cols = m.sb("cols", [P, 4, 2])
        tile_stats = m.sb("tile_stats", [P, 2, NT * 6])
        block_stats = m.sb("block_stats", [P, 2, len(blocks) * 6])
        mv = m.sb("mv", [P, 2, 2])
        root = m.sb("root", [P, 2])
        scale = m.sb("scale", [P, 2])
        bias = m.sb("bias", [P, 2])
        eps = m.sb("eps", [P, 1])
        deg = m.sb("deg", [P, P])
        degT = m.sb("degT", [P, P])
        ps = [m.ps(f"ps{n}", [P, 512]) for n in range(6)]
        small_in, dv = m.sem("small_in"), m.sem("dve")
        deg_made, deg_root, deg_turned, degT_made, deg_stored, norm_in = (
            m.sem(n) for n in ("deg_made", "deg_root", "deg_turned", "degT_made", "deg_stored", "norm_in"))
        w_turned, wT_made = m.sem("w_turned"), m.sem("wT_made")
        loaded = [m.sem(f"loaded{s}") for s in range(4)]
        y_made, turned, yT_made, summed, z_made = (m.sem(n) for n in ("y_made", "turned", "yT_made", "summed", "z_made"))
        var_made, root_made, scale_made, relu_made = (m.sem(n) for n in ("var_made", "root_made", "scale_made", "relu_made"))
        summed2, z2_made = m.sem("summed2"), m.sem("z2_made")
        stats_made = m.sem("stats_made")
        loaded2 = [m.sem(f"loaded2_{s}") for s in range(4)]
        doubled, turned2, done2 = m.sem("doubled"), m.sem("turned2"), m.sem("done2")
        block = ctx.enter_context(nc.Block())
        acc3 = acc.rearrange("p (t w) -> p t w", w=MSGW)

        @block.sync
        def _(sp):
            for n, w in enumerate((w1, w2)):
                for c in range(2):
                    sp.dma_start(w_in_sb[:, n, c, :], w[c * P:(c + 1) * P, :]).then_inc(small_in, 16)
            for n, v in enumerate((gamma1, beta1, gamma_h, beta_h)):
                sp.dma_start(cols[:, n, :], v.rearrange("(c p) -> p c", p=P),
                             allow_slow_non_contiguous=True).then_inc(small_in, 16)
            sp.dma_start(eps_w[:], eps_weight.partition_broadcast(P)).then_inc(small_in, 16)

            def load(t, s, first):
                if not first:
                    sp.wait_ge(y_made, t - 3)
                sp.dma_start(xin[:, s, :], table_in[bass.ds(t * P, P), :]).then_inc(loaded[s], 16)

            pipeline(sp, (load, 0), slots=4)
            sp.wait_ge(degT_made, 1)
            sp.dma_start(norm_dram.rearrange("(t p) -> t p", p=P), degT[0:NTP, :]).then_inc(deg_stored, 16)
            sp.wait_ge(deg_stored, 16)
            sp.dma_start(n_norm[:], norm_dram.partition_broadcast(P)).then_inc(norm_in, 16)

            sp.wait_ge(y_made, NTP)

            def load2(t, s, first):
                if not first:
                    sp.wait_ge(done2, t - 3)
                sp.dma_start(xin[:, s, :], table_in[bass.ds(t * P, P), :]).then_inc(loaded2[s], 16)

            pipeline(sp, (load2, 0), slots=4)

        @block.tensor
        def _(pe):
            pe.wait_ge(small_in, 144)
            for n in range(2):
                for c in range(2):
                    for o in range(2):
                        ins = pe.transpose(ps[n][:, (2 * c + o) * P:(2 * c + o + 1) * P],
                                           w_in_sb[:, n, o, c * P:(c + 1) * P], k.ident[:])
            ins.then_inc(w_turned, 1)
            pe.wait_ge(deg_root, 1)
            pe.transpose(ps[2][:, 0:P], deg[:], k.ident[:]).then_inc(deg_turned, 1)
            pe.wait_ge(wT_made, 1)
            pe.wait_ge(degT_made, 1)

            def turn(t, s, first):
                pe.wait_ge(y_made, t + 1)
                if not first:
                    pe.wait_ge(yT_made, t - 1)
                for c in range(2):
                    ins = pe.transpose(ps[s][:, c * P:(c + 1) * P], yin[:, s, c * P:(c + 1) * P], k.ident[:])
                ins.then_inc(turned, 1)

            def multiply(t, s, first):
                pe.wait_ge(yT_made, t + 1)
                if not first:
                    pe.wait_ge(z_made, t - 1)
                for o in range(2):
                    for c in range(2):
                        ins = pe.matmul(ps[2 + s][:, o * P:(o + 1) * P], wT[:, 0, c, o * P:(o + 1) * P],
                                        yT[:, s, c * P:(c + 1) * P], start=(c == 0), stop=(c == 1))
                ins.then_inc(summed, 1)

            pipeline(pe, (turn, 0), (multiply, 1))
            pe.wait_ge(z_made, NTP)
            for n, (b, w) in enumerate(blocks):
                pe.wait_ge(relu_made, n + 1)
                if n >= 2:
                    pe.wait_ge(z2_made, n - 1)
                for o in range(2):
                    for c in range(2):
                        ins = pe.matmul(ps[2 * (n % 2) + o][:, 0:w], wT[:, 1, c, o * P:(o + 1) * P],
                                        zT[:, c, b:b + w], start=(c == 0), stop=(c == 1))
                ins.then_inc(summed2, 1)
            pe.wait_ge(z2_made, len(blocks))

            def back(t, s, first):
                pe.wait_ge(yT_made, t + NTP + 1)
                if not first:
                    pe.wait_ge(done2, t - 1)
                for c in range(2):
                    ins = pe.transpose(ps[s][:, c * P:(c + 1) * P], yT[:, s, c * P:(c + 1) * P], k.ident[:])
                ins.then_inc(turned2, 1)

            pipeline(pe, (back, 0))

        @block.scalar
        def _(act):
            act.wait_ge(deg_made, 1)
            act.activation(deg[:, 0:NTP], deg[:, 0:NTP], ACT.Sqrt).then_inc(deg_made, 1)

            def tile(t, s, first):
                act.wait_ge(turned, t + 1)
                if not first:
                    act.wait_ge(summed, t - 1)
                act.copy(yT[:, s, :], ps[s][:, 0:D]).then_inc(yT_made, 1)

            pipeline(act, (tile, 0))

            def root_of_var(n):
                act.wait_ge(var_made, n + 1)
                act.activation(root[:], mv[:, :, 1], ACT.Sqrt, bias=eps[:]).then_inc(root_made, 1)
                act.wait_ge(scale_made, n + 1)

            root_of_var(0)
            for b, w in blocks:
                for o in range(2):
                    ins = act.activation(zT[:, o, b:b + w], zT[:, o, b:b + w], ACT.Relu,
                                         bias=bias[:, o:o + 1], scale=scale[:, o:o + 1])
                ins.then_inc(relu_made, 1)
            root_of_var(1)

            def out_tile(t, s, first):
                if first:
                    act.wait_ge(summed, NTP)
                else:
                    act.wait_ge(turned2, t - 1)
                for o in range(2):
                    ins = act.activation(yT[:, s, o * P:(o + 1) * P], zT[:, o, bass.ds(t * P, P)], ACT.Relu,
                                         bias=bias[:, o:o + 1], scale=scale[:, o:o + 1])
                ins.then_inc(yT_made, 1)

            pipeline(act, (out_tile, 0))

        @block.vector
        def _(dve):
            st = Steps(dve, dv)
            st(dve.memset(eps[:], EPS))
            st(dve.memset(deg[:], 1.0))
            dve.tensor_scalar(deg[:, 0:NTP], acc3[:, :, MSG_ONE], 1.0, None, op0=ALU.max).then_inc(deg_made, 1)
            dve.wait_ge(deg_made, 2)
            st(dve.reciprocal(deg[:, 0:NTP], deg[:, 0:NTP]))
            dve.sem_inc(deg_root, 1)
            dve.wait_ge(deg_turned, 1)
            dve.tensor_copy(degT[:], ps[2][:, 0:P]).then_inc(degT_made, 1)
            dve.wait_ge(w_turned, 1)
            for n in range(2):
                st(dve.tensor_copy(wT[:, n].rearrange("p c d -> p (c d)"), ps[n][:]))
            dve.sem_inc(wT_made, 1)
            dve.wait_ge(small_in, 144)

            def tile(t, s, first):
                dve.wait_ge(loaded[s], (t - s) * 4 + 16)
                if not before(t, 2):
                    dve.wait_ge(turned, t - 1)
                dve.scalar_tensor_tensor(yin[:, s % 2, :], xin[:, s, :], eps_w[:], acc[:, bass.ds(t * MSGW, D)],
                                         op0=ALU.mult, op1=ALU.add).then_inc(y_made, 1)

            def take(t, s, first):
                dve.wait_ge(summed, t + 1)
                dve.tensor_copy(zT[:, :, bass.ds(t * P, P)], ps[2 + s % 2][:, 0:D].rearrange("p (c n) -> p c n", c=2)).then_inc(z_made, 1)

            def stat_tile(t, s, first):
                w = max(0, min(P, N - t * P)) if isinstance(t, int) else P
                if w:
                    dve.wait_ge(z_made, t + 1)
                    for o in range(2):
                        dve.bn_stats(tile_stats[:, o, bass.ds(t * 6, 6)], zT[:, o, bass.ds(t * P, w)]).then_inc(stats_made, 1)

            pipeline(dve, (tile, 0), (take, 2), (stat_tile, 3), slots=4)
            dve.wait_ge(stats_made, 2 * NT)

            def stat(n, stats):
                for o in range(2):
                    st(dve.bn_aggr(mv[:, o, :], stats[:, o]))
                dve.sem_inc(var_made, 1)
                dve.wait_ge(root_made, n + 1)
                st(dve.reciprocal(root[:], root[:]))
                st(dve.tensor_tensor(scale[:], root[:], cols[:, 2 * n, :], ALU.mult))
                st(dve.tensor_tensor(bias[:], mv[:, :, 0], scale[:], ALU.mult))
                st(dve.tensor_tensor(bias[:], cols[:, 2 * n + 1, :], bias[:], ALU.subtract))
                dve.sem_inc(scale_made, 1)

            stat(0, tile_stats)
            dve.wait_ge(norm_in, 16)
            for n, (b, w) in enumerate(blocks):
                dve.wait_ge(summed2, n + 1)
                for o in range(2):
                    ins = dve.tensor_tensor(zT[:, o, b:b + w], ps[2 * (n % 2) + o][:, 0:w], n_norm[:, b:b + w], ALU.mult)
                ins.then_inc(z2_made, 1)
                dve.wait_ge(z2_made, n + 1)
                for o in range(2):
                    dve.bn_stats(block_stats[:, o, n * 6:(n + 1) * 6], zT[:, o, b:min(b + w, N)]).then_inc(stats_made, 1)
            dve.wait_ge(stats_made, 2 * NT + 2 * len(blocks))
            stat(1, block_stats)

            def out_tile(t, s, first):
                dve.wait_ge(turned2, t + 1)
                dve.wait_ge(loaded2[s], (t - s) * 4 + 16)
                dve.scalar_tensor_tensor(acc[:, bass.ds(t * MSGW, D)], xin[:, s, :], 2.0, ps[s % 2][:, 0:D],
                                         op0=ALU.mult, op1=ALU.add).then_inc(done2, 1)

            def stat_rows(t, s, first):
                dve.wait_ge(done2, t + 1)
                dve.bn_stats(row_stats[:].rearrange("p t s -> p (t s)")[:, bass.ds(t * 6, 6)], acc[:, bass.ds(t * MSGW, D)])

            pipeline(dve, (out_tile, 0), (stat_rows, 1), slots=4)


class Shared:
    pass


def build_program(nc, a, out):
    k = Shared()

    def dram(name, shape, dt=F32):
        return nc.dram_tensor(name, shape, dt).ap()

    table_x = dram("table_x", (NP, D))
    rec_hi = dram("rec_hi", (EP, RW))
    rec_in = dram("rec_in", (E + P, RW))
    tile_dram = dram("tile_dram", (2, NCH), I32)
    codes_dram = dram("codes_dram", (3, EP), BF16)
    att_dram = dram("att_dram", (NP, 2 * H))
    with ExitStack() as ctx:
        m = Mem(nc, ctx, "k")
        k.iota = m.sb("iota", [P, P])
        k.ident = m.sb("ident", [P, P])
        k.before = m.sb("before", [P, P])
        k.ones = m.sb("ones", [P, P])
        k.tile_off = m.sb("tile_off", [1, NCH], I32)
        k.tile_off_a = m.sb("tile_off_a", [1, NCH], I32)
        k.unsorted = m.sb("unsorted", [1, 1], I32)
        k.partition = m.sb("partition", [P, 1])
        with ExitStack() as sort_ctx:
            ms = Mem(nc, sort_ctx, "sort")
            k.rec = ms.sb("rec", [P, SC, RW])
            k.chunk_no = ms.sb("chunk_no", [P, NQ])
            k.tile_of = ms.sb("tile_of", [P, NQ])
            k.tile_off_i = ms.sb("tile_off_i", [P, 2, NQ], I32)
            setup_phase(nc, k, a["src"], a["dst"], a["edge_weight"], a["edge_attr3_1x1"], a["x"], table_x)
            unsorted = nc.values_load(k.unsorted[0:1, 0:1], min_val=0, max_val=SP_)
            with nc.If(unsorted > 0):
                sort_phase(nc, k, "low", LOW, False, rec_hi[0:E, :])
                sort_phase(nc, k, "high", HIGH, True, rec_hi)
            with nc.Else():
                place_sorted_phase(nc, k, rec_in, rec_hi)
            store_chunk_tiles_phase(nc, k, tile_dram)
        k.src = m.sb("src", [P, NCH], I32)
        k.att_row = m.sb("att_row", [P, NCH], I32)
        k.local = m.sb("local", [P, NCH])
        k.weight = m.sb("weight", [P, NCH])
        k.dist = m.sb("dist", [P, NCH])
        k.breaks_in = m.sb("breaks_in", [1, P + 1])
        k.through_fwd = m.sb("through_fwd", [1, P])
        k.through_back = m.sb("through_back", [1, P])
        k.first_in_run = m.sb("first_in_run", [P, 1])
        k.att = m.sb("att", [P, NTP * 2 * H])
        k.numer = m.sb("numer", [P, H, NCH])
        k.first_max = m.sb("first_max", [P, H, NCH])
        flags_dram = dram("flags_dram", (P, RL + 1))
        with ExitStack() as rows_ctx:
            rec_rows = Mem(nc, rows_ctx, "rows").sb("rec_rows", [P, NQ, P, RW])
            edges_phase(nc, k, rec_hi, rec_rows, flags_dram)
            codes_phase(nc, k, rec_rows, codes_dram)
        tables = [dram(f"table_{n}", (NP, D)) for n in range(3)]
        table_h = dram("table_h", (NP, D))
        norm_dram = dram("norm_dram", (NP,))
        row_stats = m.sb("row_stats", [P, NTP, 6])
        table_0, table_1, table_2 = tables

        def with_acc(name, body):
            with ExitStack() as ac:
                body(Mem(nc, ac, name).sb("acc", [P, NTP * MSGW])[:])

        def attention_layer(name, table_in, w, a_src, a_dst, bias, own, residual, table_out, normed_to, last=None):
            project_phase(nc, k, f"{name}p", table_in, w, a_src, a_dst, table_h)
            with ExitStack() as ring_ctx:
                ring = Ring(Mem(nc, ring_ctx, f"{name}g"))
                with ExitStack() as zc:
                    mz = Mem(nc, zc, f"{name}z")
                    z = mz.sb("z", [P, H, NCH])
                    z_self = mz.sb("z_self", [P, H, NCH]) if own else None
                    lookup_phase(nc, k, f"{name}l", codes_dram, att_dram, z, z_self)
                    softmax_phase(nc, k, f"{name}s", flags_dram, z, z_self, None if own else k.first_max, ring, table_h)

                def rest(acc):
                    aggregate_phase(nc, k, f"{name}a", table_h, acc, k.numer if own else k.first_max, True, True,
                                    MSGW if own else MSG_M, ring)
                    attention_end_phase(nc, k, f"{name}e", acc, table_h, own, bias, residual, table_out)
                    if residual is not None:
                        layernorm_phase(nc, k, f"{name}n", acc, normed_to, last)

                with_acc(name, rest)

        g0, g1, g2, g3 = ({n[7:]: v for n, v in a.items() if n.startswith(f"L{l}_gnn_")} for l in range(4))
        attention_layer("l0a", table_x, g0["W1"], g0["att_src1"], g0["att_dst1"], g0["b1"], True, None, table_0, None)
        attention_layer("l0b", table_0, g0["W2"], g0["att_src2"], g0["att_dst2"], g0["b2"], True, table_x, None, table_1)

        def conv(name, table_in, w_rel, w_root, bias, table_out, residual):
            def rest(acc):
                aggregate_phase(nc, k, f"{name}a", table_in, acc, None, False, False, D)
                graph_conv_phase(nc, k, f"{name}c", acc, table_in, w_rel, w_root, bias, table_out, residual, row_stats)
                if residual is not None:
                    layernorm_phase(nc, k, f"{name}n", acc, table_0, None, row_stats)

            with_acc(name, rest)

        conv("l1a", table_1, g1["W1_rel"], g1["W1_root"], g1["b1"], table_0, None)
        conv("l1b", table_0, g1["W2_rel"], g1["W2_root"], g1["b2"], table_2, None)
        conv("l1c", table_2, g1["W3_rel"], g1["W3_root"], g1["b3"], None, table_1)

        def batch(acc):
            aggregate_phase(nc, k, "l2a", table_0, acc, k.weight, False, False, MSG_P)
            batch_norm_layer_phase(nc, k, "l2b", acc, table_0, g2["w1"], g2["gamma1"], g2["beta1"], g2["w2"],
                                   g2["eps_weight"], g2["gamma_h"], g2["beta_h"], norm_dram, row_stats)
            layernorm_phase(nc, k, "l2n", acc, table_1, None, row_stats)

        with_acc("l2", batch)
        attention_layer("l3", table_1, g3["W"], g3["w_att_src"], g3["w_att_dst"], None, False, table_1, None, None, out)


def kernel(**inputs):
    import numpy as np
    import concourse.bacc as bacc
    from concourse.bass_utils import run_bass_kernel_spmd

    nc = bacc.Bacc("TRN2", target_bir_lowering=False, num_devices=1)
    arrays, args = {}, {}
    for name, value in inputs.items():
        arrays[name] = np.ascontiguousarray(value)
        args[name] = nc.dram_tensor(name, arrays[name].shape, mybir.dt.from_np(arrays[name].dtype),
                                    kind="ExternalInput").ap()
    out = nc.dram_tensor("out", (N, D), F32, kind="ExternalOutput").ap()
    build_program(nc, args, out)
    return run_bass_kernel_spmd(nc, [arrays], core_ids=[0]).results[0]["out"]
```
